# Optimizing a Trainium2 kernel written in Bass

```python
import numpy as np
import jax
import jax.numpy as jnp

def _softmax(x, axis=-1):
    return jax.nn.softmax(x, axis=axis)

def _gelu(x):
    return jax.nn.gelu(x, approximate=True)

def _silu(x):
    return jax.nn.silu(x)

def _sigmoid(x):
    return jax.nn.sigmoid(x)

def _layernorm(x, axis=-1, eps=1e-05):
    m = jnp.mean(x, axis=axis, keepdims=True)
    v = jnp.var(x, axis=axis, keepdims=True)
    return (x - m) / jnp.sqrt(v + eps)

def _scatter_add(tgt, idx, src, axis=0):
    return tgt.at[idx].add(src)

def _segment_sum(src, seg, n):
    return jax.ops.segment_sum(src, seg, n)
kernel_name = 'mk_hybrid_d1_jaxref_r8_ff3ee8'

def setup_inputs(seed: int=0):
    np.random.seed(seed)
    _w = jnp.asarray

    def _L0_attn_a_setup():
        import jax, jax.numpy as jnp
        import numpy as np
        EMB, HEADS, HIDDEN = (128, 16, 64)
        BS, N = (2, 256)
        key = jax.random.key(seed)
        ks = jax.random.split(key, 7)
        s_in = 1.0 / np.sqrt(EMB)
        s_u = 1.0 / np.sqrt(HEADS * HIDDEN)
        return {'x': jax.random.normal(ks[0], (BS, N, EMB), dtype=jnp.float32), 'w_q': jax.random.uniform(ks[1], (EMB, HEADS * HIDDEN), jnp.float32, -s_in, s_in), 'w_k': jax.random.uniform(ks[2], (EMB, HEADS * HIDDEN), jnp.float32, -s_in, s_in), 'w_v': jax.random.uniform(ks[3], (EMB, HEADS * HIDDEN), jnp.float32, -s_in, s_in), 'w_u': jax.random.uniform(ks[4], (HEADS * HIDDEN, EMB), jnp.float32, -s_u, s_u), 'b_u': jax.random.uniform(ks[5], (EMB,), jnp.float32, -s_u, s_u)}
    _L0_attn_a_in = _L0_attn_a_setup()

    def _L0_attn_b_setup():
        import jax, jax.numpy as jnp
        import numpy as np
        HEADS = 16
        key = jax.random.key(seed)
        k1, k2, k3 = jax.random.split(key, 3)
        B, N, C = (4, 512, 128)
        x = jax.random.normal(k1, (B, N, C), dtype=jnp.float32)
        w_qkv = jax.random.normal(k2, (3 * C, C), dtype=jnp.float32) * C ** (-0.5)
        w_proj = jax.random.normal(k3, (C, C), dtype=jnp.float32) * C ** (-0.5)
        b_proj = jnp.zeros((C,), dtype=jnp.float32)
        return {'x': x, 'w_qkv': w_qkv, 'w_proj': w_proj, 'b_proj': b_proj}
    _L0_attn_b_in = _L0_attn_b_setup()

    def _L0_ffn_setup():
        import jax, jax.numpy as jnp
        import numpy as np
        E, K, H, F = (64, 6, 128, 64)
        SHARED_F = 256
        B, S = (1, 256)
        T = B * S
        CAP = 2 * ((T * K + E - 1) // E)
        key = jax.random.key(seed)
        ks = jax.random.split(key, 6)
        s = 0.05
        return {'hidden_states': jax.random.normal(ks[0], (B, S, H), jnp.float32), 'router_weight': jax.random.normal(ks[1], (E, H), jnp.float32) * s, 'expert_bias': jnp.zeros((E,), jnp.float32), 'w1': jax.random.normal(ks[2], (E, H, F), jnp.float32) * s, 'w2': jax.random.normal(ks[3], (E, F, H), jnp.float32) * s, 'sw1': jax.random.normal(ks[4], (SHARED_F, H), jnp.float32) * s, 'sw2': jax.random.normal(ks[5], (H, SHARED_F), jnp.float32) * s}
    _L0_ffn_in = _L0_ffn_setup()
    _d = {'L0_attn_a_x': _L0_attn_a_in['x'], 'L0_attn_a_w_q': _L0_attn_a_in['w_q'], 'L0_attn_a_w_k': _L0_attn_a_in['w_k'], 'L0_attn_a_w_v': _L0_attn_a_in['w_v'], 'L0_attn_a_w_u': _L0_attn_a_in['w_u'], 'L0_attn_a_b_u': _L0_attn_a_in['b_u'], 'L0_attn_b_w_qkv': _L0_attn_b_in['w_qkv'], 'L0_attn_b_w_proj': _L0_attn_b_in['w_proj'], 'L0_attn_b_b_proj': _L0_attn_b_in['b_proj'], 'L0_ffn_router_weight': _L0_ffn_in['router_weight'], 'L0_ffn_expert_bias': _L0_ffn_in['expert_bias'], 'L0_ffn_w1': _L0_ffn_in['w1'], 'L0_ffn_w2': _L0_ffn_in['w2'], 'L0_ffn_sw1': _L0_ffn_in['sw1'], 'L0_ffn_sw2': _L0_ffn_in['sw2']}
    _x0 = _d['L0_attn_a_x']
    _d['L0_attn_a_x'] = jax.random.normal(jax.random.fold_in(jax.random.key(seed), 1), (4, 1024, 128), dtype=_x0.dtype)
    del _x0
    return _d

def reference(L0_attn_a_x, L0_attn_a_w_q, L0_attn_a_w_k, L0_attn_a_w_v, L0_attn_a_w_u, L0_attn_a_b_u, L0_attn_b_w_qkv, L0_attn_b_w_proj, L0_attn_b_b_proj, L0_ffn_router_weight, L0_ffn_expert_bias, L0_ffn_w1, L0_ffn_w2, L0_ffn_sw1, L0_ffn_sw2):

    def _L0_attn_a_ref(x, w_q, w_k, w_v, w_u, b_u):
        import jax, jax.numpy as jnp
        import numpy as np
        EMB, HEADS, HIDDEN = (128, 16, 64)
        BS, N = (2, 256)
        bs, n, emb = x.shape
        h, hd = (HEADS, HIDDEN)
        q = (x @ w_q).reshape(bs, n, h, hd)
        k = (x @ w_k).reshape(bs, n, h, hd)
        v = (x @ w_v).reshape(bs, n, h, hd)
        scale = 1.0 / jnp.sqrt(jnp.asarray(hd, dtype=x.dtype))
        q = q * scale
        k = k * scale
        dot = jnp.einsum('bqhd,bkhd->bhqk', q, k)
        causal = jnp.tril(jnp.ones((n, n), dtype=bool))
        dot = jnp.where(causal, dot, jnp.asarray(-jnp.inf, dtype=dot.dtype))
        att = jax.nn.softmax(dot, axis=-1)
        out = jnp.einsum('bhqk,bkhd->bqhd', att, v).reshape(bs, n, h * hd)
        return out @ w_u + b_u

    def _L0_attn_b_ref(x, w_qkv, w_proj, b_proj):
        import jax, jax.numpy as jnp
        import numpy as np
        HEADS = 16
        B, N, C = x.shape
        H = HEADS
        D = C // H
        qkv = x @ w_qkv.T
        q, k, v = jnp.split(qkv, 3, axis=-1)

        def to_bhdn(t):
            return t.reshape(B, N, H, D).transpose(0, 2, 3, 1)
        q = jax.nn.relu(to_bhdn(q))
        k = jax.nn.relu(to_bhdn(k))
        v = to_bhdn(v)
        eps = jnp.finfo(q.dtype).eps
        ksum = k.sum(axis=-1)
        z = 1.0 / (jnp.einsum('bhd,bhdn->bhn', ksum, q) + eps)
        context = jnp.einsum('bhdn,bhen->bhde', v, k)
        out = jnp.einsum('bhde,bhen->bhdn', context, q)
        out = out * z[:, :, None, :]
        out = out.transpose(0, 3, 1, 2).reshape(B, N, C)
        return out @ w_proj.T + b_proj

    def _L0_ffn_ref(hidden_states, router_weight, expert_bias, w1, w2, sw1, sw2):
        import jax, jax.numpy as jnp
        import numpy as np
        E, K, H, F = (64, 6, 128, 64)
        SHARED_F = 256
        B, S = (1, 256)
        T = B * S
        CAP = 2 * ((T * K + E - 1) // E)
        b, s, h = hidden_states.shape
        x = hidden_states.reshape(-1, h)
        t = x.shape[0]
        logits = x @ router_weight.T
        scores = jax.nn.sigmoid(logits)
        _, top_idx = jax.lax.top_k(scores + expert_bias[None, :], K)
        top_scores = jnp.take_along_axis(scores, top_idx, axis=1)
        probs = top_scores / (jnp.sum(top_scores, axis=-1, keepdims=True) + 1e-20)
        flat_e = top_idx.reshape(-1)
        order = jnp.argsort(flat_e)
        sorted_e = flat_e[order]
        token_of = order // K
        counts = jnp.bincount(flat_e, length=E)
        offsets = jnp.cumsum(counts) - counts
        pos = jnp.arange(t * K) - offsets[sorted_e]
        valid = pos < CAP
        slot = jnp.where(valid, sorted_e * CAP + pos, E * CAP)
        xs = jnp.zeros((E * CAP + 1, h), x.dtype).at[slot].set(x[token_of])
        xs = xs[:-1].reshape(E, CAP, h)
        hmid = jax.nn.gelu(jnp.einsum('ech,ehf->ecf', xs, w1), approximate=True)
        y = jnp.einsum('ecf,efh->ech', hmid, w2).reshape(E * CAP, h)
        pair_w = jnp.where(valid, probs.reshape(-1)[order], 0.0)
        y_pair = y[jnp.minimum(slot, E * CAP - 1)] * pair_w[:, None]
        out = jnp.zeros((t, h), x.dtype).at[token_of].add(y_pair)
        shared = jax.nn.gelu(x @ sw1.T, approximate=True) @ sw2.T
        return (out + shared).reshape(b, s, h)
    x = L0_attn_a_x
    x = x + _L0_attn_a_ref(_layernorm(x, axis=-1), L0_attn_a_w_q, L0_attn_a_w_k, L0_attn_a_w_v, L0_attn_a_w_u, L0_attn_a_b_u)
    x = x + _L0_ffn_ref(_layernorm(x, axis=-1), L0_ffn_router_weight, L0_ffn_expert_bias, L0_ffn_w1, L0_ffn_w2, L0_ffn_sw1, L0_ffn_sw2)
    x = x + _L0_attn_b_ref(_layernorm(x, axis=-1), L0_attn_b_w_qkv, L0_attn_b_w_proj, L0_attn_b_b_proj)
    x = x + _L0_ffn_ref(_layernorm(x, axis=-1), L0_ffn_router_weight, L0_ffn_expert_bias, L0_ffn_w1, L0_ffn_w2, L0_ffn_sw1, L0_ffn_sw2)
    return x

_drawn_inputs = setup_inputs


def setup_inputs(seed=0):
    import zlib

    import numpy as np

    out = dict(_drawn_inputs(seed))
    spreads = {'L0_attn_b_b_proj': (0.0, 0.1), 'L0_ffn_expert_bias': (0.0, 0.1)}
    factors = {'L0_attn_a_w_q': 8.0, 'L0_attn_a_w_k': 8.0}
    for name, (base, spread) in spreads.items():
        noise = np.random.default_rng([zlib.crc32(name.encode()), seed]).standard_normal(out[name].shape)
        drawn = base * np.exp(spread * noise) if base else spread * noise
        out[name] = jnp.asarray(drawn.astype(out[name].dtype))
    for name, factor in factors.items():
        out[name] = (out[name] * factor).astype(out[name].dtype)
    return out
```

```python
import concourse.bass as bass
from concourse import mybir
from contextlib import ExitStack

F32 = mybir.dt.float32
BF16 = mybir.dt.bfloat16
I32 = mybir.dt.int32
ALU = mybir.AluOpType
ACT = mybir.ActivationFunctionType
AX = mybir.AxisListType
ds = bass.ds

P = 128
B, N, C = 4, 1024, 128
T = B * N
NT = T // P
BT = N // P
GT = 4
NG = NT // GT
GC = GT * P
EPS_LN = 1e-5

HEADS, HD = 16, 64
PAIRS = HEADS // 2
NP = B * PAIRS
SCALE_QK = 1.0 / HD

HB, DB = 16, 8
EPS_Z = 1.1920928955078125e-07

E, K, F = 64, 6, 64
CAP = 2 * ((256 * K + E - 1) // E)
HE = E // 2
SF = 256
ZR = T + P
TW = C + E
ZPARTS = 8
EMPTY = -3.0e38


class Steps:

    def __init__(self, eng, sem):
        self.eng, self.sem, self.n = eng, sem, 0

    def mark(self, ins):
        ins.then_inc(self.sem, 1)
        self.n += 1
        return self.n

    def wait(self, n=None):
        self.eng.wait_ge(self.sem, self.n if n is None else n)


def blocks_of(i):
    return [(k, min(k + GT, i + 1)) for k in range(0, i + 1, GT)]


def evacs(i):
    return sum(len(blocks_of(k)) for k in range(i))


EV_PAIR = evacs(BT)


def build(nc, x, ident_in, causal_in, causal_sel_in, wqk_in, wv_in, wu_in, bu_in,
          wqB_in, wkvB_in, wpB_in, bpB_in, headmask_in, rw_in, eb_in, w1_in, w2_in, sw1_in, sw2_in,
          keyrow_in, offs_in, out, table, zbuf, stop):
    ctx = ExitStack()
    with ctx:
        def sb(name, shape, dt=F32):
            return ctx.enter_context(nc.sbuf_tensor(name, shape, dt))

        def sem(name):
            return ctx.enter_context(nc.semaphore(name))

        X = sb("X", [P, NT, C])
        XT = sb("XT", [P, T])
        ident = sb("ident", [P, P])
        mean_var = sb("mean_var", [P, NT, 2])
        rstd = sb("rstd", [P, NT])
        shift = sb("shift", [P, NT])

        in_loaded = sem("in_loaded")

        with nc.Block() as block:
            @block.sync
            def _(sp):
                sp.dma_start(X[:, :, :], x.rearrange("(t p) c -> p t c", p=P)).then_inc(in_loaded, 16)
                sp.dma_start(ident[:, :], ident_in).then_inc(in_loaded, 16)
                sp.wait_ge(in_loaded, 32)

        layernorm(nc, X, mean_var, rstd, shift, "a")
        transpose_x(nc, X, XT, rstd, shift, ident, "a")
        attention_a(nc, X, XT, ident, causal_in, causal_sel_in, wqk_in, wv_in, wu_in, bu_in, zbuf)
        if stop == "a":
            return store(nc, X, out, sem)
        experts(nc, X, XT, mean_var, rstd, shift, ident, rw_in, eb_in, w1_in, w2_in, sw1_in, sw2_in,
                keyrow_in, offs_in, table, zbuf, 0)
        if stop == "f":
            return store(nc, X, out, sem)
        attention_b(nc, X, mean_var, rstd, shift, ident, wqB_in, wkvB_in, wpB_in, bpB_in, headmask_in)
        if stop == "b":
            return store(nc, X, out, sem)
        experts(nc, X, XT, mean_var, rstd, shift, ident, rw_in, eb_in, w1_in, w2_in, sw1_in, sw2_in,
                keyrow_in, offs_in, table, zbuf, 1)
        store(nc, X, out, sem)


def store(nc, X, out, sem):
    out_done = sem("out_done")
    with nc.Block() as block:
        @block.sync
        def _(sp):
            sp.dma_start(out.rearrange("(t p) c -> p t c", p=P), X[:, :, :]).then_inc(out_done, 16)
            sp.wait_ge(out_done, 16)


def layernorm(nc, X, mean_var, rstd, shift, tag):
    ctx = ExitStack()
    with ctx:
        stats = ctx.enter_context(nc.sbuf_tensor(f"stats_{tag}", [P, 2, BT, 6], F32))
        stat_step = ctx.enter_context(nc.semaphore(f"stat_step_{tag}"))
        fin_step = ctx.enter_context(nc.semaphore(f"fin_step_{tag}"))
        std_done = ctx.enter_context(nc.semaphore(f"std_done_{tag}"))
        block = ctx.enter_context(nc.Block())

        @block.vector
        def _(dve):
            n = 0
            for g in range(B):
                for k in range(BT):
                    nc.vector.bn_stats(stats[:, g % 2, k, :], X[:, g * BT + k, :]).then_inc(stat_step, 1)
                n += BT
                dve.wait_ge(stat_step, n)
                for k in range(BT):
                    nc.vector.bn_aggr(mean_var[:, g * BT + k, :], stats[:, g % 2, k, :]).then_inc(stat_step, 1)
                n += BT
            dve.wait_ge(stat_step, n)
            nc.vector.tensor_scalar(rstd[:, :], mean_var[:, :, 1], EPS_LN, None, ALU.add).then_inc(fin_step, 1)
            dve.wait_ge(std_done, 1)
            nc.vector.reciprocal(rstd[:, :], rstd[:, :]).then_inc(fin_step, 1)
            dve.wait_ge(fin_step, 2)
            nc.vector.scalar_tensor_tensor(out=shift[:, :], in0=mean_var[:, :, 0], scalar=-1.0, in1=rstd[:, :],
                                           op0=ALU.mult, op1=ALU.mult).then_inc(fin_step, 1)

        @block.scalar
        def _(act):
            act.wait_ge(fin_step, 1)
            nc.scalar.activation(rstd[:, :], rstd[:, :], ACT.Sqrt).then_inc(std_done, 1)


def transpose_x(nc, X, XT, rstd, shift, ident, tag):
    ctx = ExitStack()
    with ctx:
        xn = ctx.enter_context(nc.sbuf_tensor(f"xn_{tag}", [P, 2, GT, C], F32))
        tps = [ctx.enter_context(nc.psum_tensor(f"tps_{tag}{u}", [P, GC], F32)) for u in range(2)]
        normed = ctx.enter_context(nc.semaphore(f"normed_{tag}"))
        turned = ctx.enter_context(nc.semaphore(f"turned_{tag}"))
        copied = ctx.enter_context(nc.semaphore(f"copied_{tag}"))
        block = ctx.enter_context(nc.Block())

        @block.vector
        def _(dve):
            with dve.Fori(0, NG // 2) as j:
                for u in range(2):
                    if u == 0:
                        dve.wait_ge(turned, 2 * j + 1)
                    for k in range(GT):
                        t = (2 * j + u) * GT + k
                        nc.vector.tensor_scalar(xn[:, u, k, :], X[:, t, :], rstd[:, ds(t, 1)], shift[:, ds(t, 1)],
                                                ALU.mult, ALU.add).then_inc(normed, 1)

        @block.tensor
        def _(pe):
            pe.sem_inc(turned, 1)
            with pe.Fori(0, NG // 2) as j:
                for u in range(2):
                    pe.wait_ge(normed, (2 * j + u + 1) * GT)
                    pe.wait_ge(copied, 2 * j + 1)
                    for k in range(GT):
                        last = nc.tensor.transpose(tps[u][:, k * P:(k + 1) * P], xn[:, u, k, :], ident[:, :])
                    last.then_inc(turned, 1)

        @block.scalar
        def _(act):
            act.sem_inc(copied, 1)
            with act.Fori(0, NG // 2) as j:
                for u in range(2):
                    act.wait_ge(turned, 2 * j + u + 2)
                    nc.scalar.activation(XT[:, ds((2 * j + u) * GC, GC)], tps[u][:, :], ACT.Copy).then_inc(copied, 1)


def attention_a(nc, X, XT, ident, causal_in, causal_sel_in, wqk_in, wv_in, wu_in, bu_in, zbuf):
    ctx = ExitStack()
    with ctx:
        def sb(name, shape, dt=F32):
            return ctx.enter_context(nc.sbuf_tensor(name, shape, dt))

        def pb(name, shape, dt=F32):
            return ctx.enter_context(nc.psum_tensor(name, shape, dt))

        def sem(name):
            return ctx.enter_context(nc.semaphore(name))

        causal_f = sb("causal_f", [P, P + HD])
        causal_sel_f = sb("causal_sel_f", [P, 2, P])
        causal = sb("causal", [P, P + HD], BF16)
        causal_sel = sb("causal_sel", [P, 2, P], BF16)
        wv = sb("wv", [P, PAIRS, P])
        wu = sb("wu", [P, PAIRS, P])
        bu = sb("bu", [P, C])
        wqk = sb("wqk", [P, 2, 2, P])
        xb = sb("xb", [P, 2, N])
        QT = sb("QT", [P, 2, N])
        KT = sb("KT", [P, 2, N])
        V = sb("V", [P, 2, BT, P])
        probs = sb("probs", [P, 2, 2, N])
        PT = sb("PT", [P, 2, 2, N])
        OT = sb("OT", [P, N])
        zero_tile = sb("zero_tile", [P, 2 * ZR * C // P // ZPARTS])
        negmax = sb("negmax", [P, 2, 2])
        rowsum = sb("rowsum", [P, 2, 2])
        rinv = sb("rinv", [P, 2, 2])
        exp_warm = sb("exp_warm", [P, 1])

        S = [pb(f"S{h}", [P, N]) for h in range(2)]
        TP = [pb(f"TP{u}", [P, GC]) for u in range(2)]
        O = pb("O", [P, GC])
        G = pb("G", [P, GC])

        cst_loaded = sem("cst_loaded")
        cst_cast = sem("cst_cast")
        zeroed = sem("zeroed")
        pt_zeroed = sem("pt_zeroed")
        z_cleared = sem("z_cleared")
        bias_added = sem("bias_added")
        pair_loaded = [sem(f"pair_loaded{u}") for u in range(2)]
        scores_ready = sem("scores_ready")
        max_ready = sem("max_ready")
        exp_ready = sem("exp_ready")
        rinv_ready = sem("rinv_ready")
        probs_ready = sem("probs_ready")
        run_turned = sem("run_turned")
        pt_dve = sem("pt_dve")
        pt_act = sem("pt_act")
        step_summed = sem("step_summed")
        o_copied = sem("o_copied")
        proj_ready = sem("proj_ready")
        g_act = sem("g_act")
        g_dve = sem("g_dve")
        y_added = sem("y_added")

        FILLS = [("q", 0, "act"), ("q", 1, "act"), ("y", 0, "dve"), ("y", 1, "dve"),
                 ("k", 0, "act"), ("k", 1, "dve"), ("v", 0, "act"), ("v", 1, "dve")]
        FIRST = [f for f in FILLS if f[0] != "y"]
        A_PAIR = sum(f[2] == "act" for f in FILLS)
        D_PAIR = sum(f[2] == "dve" for f in FILLS)
        A_FIRST = sum(f[2] == "act" for f in FIRST)
        D_FIRST = sum(f[2] == "dve" for f in FIRST)

        def g_before(fills, n, eng):
            return sum(f[2] == eng for f in fills[:n])

        def ev_count(i):
            last = len(blocks_of(BT - 1))
            if i == -2:
                return 0
            return last + evacs(i + 1)

        ONE = 1
        block = ctx.enter_context(nc.Block())

        @block.sync
        def _(sp):
            sp.dma_start(causal_f[:, :], causal_in).then_inc(cst_loaded, 16)
            sp.dma_start(causal_sel_f[:, :, :], causal_sel_in).then_inc(cst_loaded, 16)
            sp.dma_start(bu[:, :], bu_in).then_inc(cst_loaded, 16)
            sp.dma_start(wv[:, :, :], wv_in.rearrange("n p c -> p n c")).then_inc(cst_loaded, 16)
            sp.dma_start(wu[:, :, :], wu_in.rearrange("n p c -> p n c")).then_inc(cst_loaded, 16)
            for u in range(2):
                sp.dma_start(wqk[:, u, :, :], wqk_in[u]).then_inc(pair_loaded[u], 16)
                sp.dma_start(xb[:, u, :], XT[:, 0:N]).then_inc(pair_loaded[u], 16)
            sp.wait_ge(zeroed, 4)
            for zb in zbuf:
                rows = zb.rearrange("(p r) c -> p (r c)", p=P)
                w = rows.shape[1] // ZPARTS
                for n in range(ZPARTS):
                    sp.dma_start(rows[:, n * w:(n + 1) * w], zero_tile[:, :]).then_inc(z_cleared, 16)
            with sp.Fori(0, NP // 2) as j:
                for u in range(2):
                    nxt = 2 * ((j + 1) % 4) + u
                    batch = ((j + 1) // 4) % 4
                    sp.wait_ge(proj_ready, len(FIRST) + (2 * j + u) * BT)
                    sp.dma_start(wqk[:, u, :, :], wqk_in[ds(nxt, 1)].rearrange("a p q c -> (a p) q c"))\
                        .then_inc(pair_loaded[u], 16)
                    sp.dma_start(xb[:, u, :], XT[:, ds(batch * N, N)]).then_inc(pair_loaded[u], 16)
            sp.wait_ge(z_cleared, 16 * 2 * ZPARTS)
            sp.wait_ge(cst_loaded, 80)
            sp.wait_ge(pair_loaded[0], 32 * (NP // 2 + 1))
            sp.wait_ge(pair_loaded[1], 32 * (NP // 2 + 1))

        def pair_fill(pe, kind, half, par, y_batch_pair):
            if kind in "qk":
                last = nc.tensor.matmul(G[:, :], wqk[:, par, "qk".index(kind), :],
                                        xb[:, par, half * GC:(half + 1) * GC], start=True, stop=True)
            else:
                for k in range(GT):
                    t = half * GT + k
                    if kind == "v":
                        lhs, rhs = xb[:, par, t * P:(t + 1) * P], wv[:, y_batch_pair, :]
                    else:
                        lhs, rhs = OT[:, t * P:(t + 1) * P], wu[:, y_batch_pair, :]
                    last = nc.tensor.matmul(G[:, k * P:(k + 1) * P], lhs, rhs, start=True, stop=True)
            last.then_inc(proj_ready, 1)

        @block.tensor
        def _(pe):
            pe.sem_inc(run_turned, ONE)
            pe.sem_inc(step_summed, ONE)
            pe.wait_ge(pair_loaded[0], 32)
            pe.wait_ge(cst_loaded, 80)
            for n, (kind, half, _) in enumerate(FIRST):
                pe.wait_ge(g_act, g_before(FIRST, n, "act"))
                pe.wait_ge(g_dve, g_before(FIRST, n, "dve"))
                pair_fill(pe, kind, half, 0, 0)
            pe.wait_ge(cst_cast, 2)
            pe.wait_ge(zeroed, 3)
            pe.wait_ge(pt_zeroed, 1)
            nc.tensor.matmul(O[:, :], OT[:, 0:P], OT[:, 0:GC], start=True, stop=True)

            def scores(j, u, i):
                s = 2 * BT * j + BT * u + i
                if i == 0:
                    pe.wait_ge(g_act, A_FIRST + (2 * j + u) * A_PAIR)
                    pe.wait_ge(g_dve, D_FIRST + (2 * j + u) * D_PAIR)
                pe.wait_ge(exp_ready, ONE + 2 * s)
                for a, b in blocks_of(i):
                    diag = b == i + 1
                    for h in range(2):
                        r = slice(h * HD, (h + 1) * HD)
                        nc.tensor.matmul(S[h][:, a * P:b * P], QT[r, u, i * P:(i + 1) * P],
                                         KT[r, u, a * P:b * P], start=True, stop=not diag)
                for h in range(2):
                    r = slice(h * HD, (h + 1) * HD)
                    nc.tensor.matmul(S[h][:, i * P:(i + 1) * P], causal_sel[r, 0, :], causal[r, 0:P],
                                     start=False, stop=False)
                for h in range(2):
                    r = slice(h * HD, (h + 1) * HD)
                    last = nc.tensor.matmul(S[h][:, i * P + HD:(i + 1) * P], causal_sel[r, 1, :], causal[r, P:],
                                            start=False, stop=True)
                last.then_inc(scores_ready, 1)

            def turn_runs(j, u, i):
                pi = (i - 1) % BT
                base = 2 * (2 * j + u) * EV_PAIR
                done = 2 * (evacs(pi) if i > 0 else -len(blocks_of(pi)))
                offset = 2 * len(blocks_of(BT - 1))
                s = 2 * BT * j + BT * u + i
                out_list = []
                for h in range(2):
                    for r, (a, b) in enumerate(blocks_of(pi)):
                        n = h * len(blocks_of(pi)) + r

                        def run(h=h, r=r, a=a, b=b, n=n):
                            if n == 0 or (h == 1 and r == 0):
                                pe.wait_ge(probs_ready, ONE + (2 * s - 1 + h if i > 0 or u > 0 else 2 * s))
                            wait_bank(j, u, i, h, r)
                            for k in range(a, b):
                                last = nc.tensor.transpose(TP[n % 2][:, (k - a) * P:(k - a + 1) * P],
                                                           probs[:, h, (pi + 0) % 2, k * P:(k + 1) * P], ident[:, :])
                            last.then_inc(run_turned, 1)
                        out_list.append(run)
                return out_list

            def wait_bank(j, u, i, h, r):
                pi = (i - 1) % BT
                m = len(blocks_of(pi))
                n = h * m + r
                before = (2 * j + u) * EV_PAIR + ev_count(i - 2)
                done = [(hh, rr) for hh in range(2) for rr in range(m)][:max(n - 1, 0)]
                pe.wait_ge(pt_dve, ONE + before + sum(hh == 0 for hh, _ in done))
                pe.wait_ge(pt_act, ONE + before + sum(hh == 1 for hh, _ in done))

            def sum_values(j, u, i):
                pi, pu = (i - 2) % BT, (u if i >= 2 else 1 - u)
                out_list = []
                for k in range(pi + 1):
                    def one(k=k):
                        if k == 0:
                            c = (2 * j + u) * EV_PAIR + ev_count(i - 2)
                            pe.wait_ge(pt_dve, ONE + c)
                            pe.wait_ge(pt_act, ONE + c)
                            if pi % GT == 0:
                                pe.wait_ge(o_copied, 2 * (2 * j + u) + 1 + pi // GT)
                        for h in range(2):
                            last = nc.tensor.matmul(O[h * HD:(h + 1) * HD, (pi % GT) * P:(pi % GT + 1) * P],
                                                    V[:, pu, k, h * HD:(h + 1) * HD],
                                                    PT[:, h, pi % 2, k * P:(k + 1) * P],
                                                    start=(k == 0), stop=(k == pi))
                        if k == pi:
                            last.then_inc(step_summed, 1)
                    out_list.append(one)
                return out_list

            with pe.Fori(0, NP // 2) as j:
                for u in range(2):
                    for i in range(BT):
                        scores(j, u, i)
                        kind, half, _ = FILLS[i]
                        if i == 0:
                            pe.wait_ge(pair_loaded[1 - u], 32 * (j + 1) if u == 0 else 32 * (j + 2))
                        pe.wait_ge(g_act, A_FIRST + (2 * j + u) * A_PAIR + g_before(FILLS, i, "act"))
                        pe.wait_ge(g_dve, D_FIRST + (2 * j + u) * D_PAIR + g_before(FILLS, i, "dve"))
                        if kind == "y" and half == 0:
                            pe.wait_ge(o_copied, 2 * (2 * j + u) + 1)
                        n = {("v", 0): 2 * (j % 4) + 1, ("v", 1): 2 * ((j + 1) % 4),
                             ("y", 0): 2 * ((j + 3) % 4) + 1, ("y", 1): 2 * (j % 4)}.get((kind, u), 0)
                        pair_fill(pe, kind, half, 1 - u, n)
                        runs = turn_runs(j, u, i)
                        sums = sum_values(j, u, i)
                        half_sums = (len(sums) + 1) // 2
                        for r, run in enumerate(runs):
                            run()
                            if r == 1:
                                for one in sums[:half_sums]:
                                    one()
                                if len(runs) == 2:
                                    for one in sums[half_sums:]:
                                        one()
                            if r == 2:
                                for one in sums[half_sums:]:
                                    one()
            J = NP // 2
            for run in turn_runs(J, 0, 0):
                run()
            for i in (0, 1):
                for one in sum_values(J, 0, i):
                    one()
            for half in range(2):
                pe.wait_ge(o_copied, 2 * 2 * J + 1)
                pe.wait_ge(g_act, A_FIRST + NP * A_PAIR)
                pe.wait_ge(g_dve, D_FIRST + NP * D_PAIR + half)
                pair_fill(pe, "y", half, 0, PAIRS - 1)

        def empty_act(kind, half, par, count_wait):
            dst = {"q": QT, "k": KT}.get(kind)
            if kind in "qk":
                nc.scalar.activation(dst[:, par, half * GC:(half + 1) * GC], G[:, :], ACT.Copy,
                                     scale=SCALE_QK if kind == "q" else 1.0).then_inc(g_act, 1)
            else:
                nc.scalar.activation(V[:, par, half * GT:(half + 1) * GT, :],
                                     G[:, :].rearrange("p (t c) -> p t c", t=GT), ACT.Copy).then_inc(g_act, 1)

        @block.scalar
        def _(act):
            act.sem_inc(exp_ready, ONE)
            act.sem_inc(pt_act, ONE)
            for n, (kind, half, who) in enumerate(FIRST):
                if who == "act":
                    act.wait_ge(proj_ready, n + 1)
                    if n == 0:
                        act.wait_ge(zeroed, 3)
                        act.wait_ge(pt_zeroed, 1)
                    empty_act(kind, half, 0, None)
            nc.scalar.activation(exp_warm[:, :], ident[:, 0:1], ACT.Exp)

            def copy_runs(j, u, i):
                pi = (i - 1) % BT
                m = len(blocks_of(pi))
                before = 2 * ((2 * j + u) * EV_PAIR + ev_count(i - 2))
                for r, (a, b) in enumerate(blocks_of(pi)):
                    act.wait_ge(run_turned, ONE + before + m + r + 1)
                    if r == 0:
                        act.wait_ge(step_summed, ONE + 2 * BT * j + BT * u + i)
                    nc.scalar.activation(PT[:, 1, pi % 2, a * P:b * P], TP[(m + r) % 2][:, 0:(b - a) * P],
                                         ACT.Copy).then_inc(pt_act, 1)

            def copy_out(j, u, i):
                pi = (i - 2) % BT
                act.wait_ge(step_summed, ONE + 2 * BT * j + BT * u + i + 1)
                if i == 5:
                    act.wait_ge(proj_ready, len(FIRST) + (2 * j + u) * BT + 4)
                nc.scalar.activation(OT[:, (pi // GT) * GC:(pi // GT + 1) * GC], O[:, :], ACT.Copy)\
                    .then_inc(o_copied, 1)

            with act.Fori(0, NP // 2) as j:
                for u in range(2):
                    for i in range(BT):
                        s = 2 * BT * j + BT * u + i
                        kind, half, who = FILLS[i]
                        if i == 2 or i == 6:
                            copy_out(j, u, i - 1)
                        for h in range(2):
                            act.wait_ge(max_ready, 2 * s + h + 1)
                            if h == 0 and (u > 0 or i > 1):
                                act.wait_ge(run_turned, ONE + 2 * ((2 * j + u) * EV_PAIR + ev_count(i - 2)))
                            elif h == 0:
                                act.wait_ge(run_turned, ONE + 2 * (2 * j * EV_PAIR + ev_count(i - 2)))
                            w = (i + 1) * P
                            nc.scalar.activation(probs[:, h, i % 2, 0:w], S[h][:, 0:w], ACT.Exp,
                                                 bias=negmax[:, i % 2, h:h + 1],
                                                 accum_out=rowsum[:, i % 2, h:h + 1]).then_inc(exp_ready, 1)
                            if h == 0 and who == "act":
                                act.wait_ge(proj_ready, len(FIRST) + (2 * j + u) * BT + i + 1)
                                empty_act(kind, half, 1 - u, None)
                        copy_runs(j, u, i)
            J = NP // 2
            copy_runs(J, 0, 0)
            copy_out(J, 0, 1)

        @block.vector
        def _(dve):
            dve.sem_inc(pt_dve, ONE)
            nc.vector.memset(PT[:, :, 0, :], 0.0).then_inc(pt_zeroed, 1)
            dve.wait_ge(cst_loaded, 80)
            nc.vector.tensor_copy(causal[:, :], causal_f[:, :]).then_inc(cst_cast, 1)
            nc.vector.tensor_copy(causal_sel[:, :, :], causal_sel_f[:, :, :]).then_inc(cst_cast, 1)

            def empty_dve(kind, half, par, j, u):
                if kind == "y":
                    b = ((j + 15) // 4) % 4 if u == 0 else j // 4
                    xs = X[:, ds(b * BT + half * GT, GT), :]
                    nc.vector.tensor_tensor(xs, G[:, :].rearrange("p (t c) -> p t c", t=GT), xs, ALU.add)\
                        .then_inc(g_dve, 1)
                elif kind == "k":
                    nc.vector.tensor_copy(KT[:, par, half * GC:(half + 1) * GC], G[:, :]).then_inc(g_dve, 1)
                else:
                    nc.vector.tensor_copy(V[:, par, half * GT:(half + 1) * GT, :],
                                          G[:, :].rearrange("p (t c) -> p t c", t=GT)).then_inc(g_dve, 1)

            for n, (kind, half, who) in enumerate(FIRST):
                if who == "dve":
                    dve.wait_ge(proj_ready, n + 1)
                    if n < 4:
                        dve.wait_ge(zeroed, 3)
                        dve.wait_ge(pt_zeroed, 1)
                    empty_dve(kind, half, 0, 0, 0)
            dve.wait_ge(bias_added, 1)

            def copy_runs(j, u, i):
                pi = (i - 1) % BT
                before = 2 * ((2 * j + u) * EV_PAIR + ev_count(i - 2))
                for r, (a, b) in enumerate(blocks_of(pi)):
                    dve.wait_ge(run_turned, ONE + before + r + 1)
                    if r == 0:
                        dve.wait_ge(step_summed, ONE + 2 * BT * j + BT * u + i)
                    nc.vector.tensor_copy(PT[:, 0, pi % 2, a * P:b * P], TP[r % 2][:, 0:(b - a) * P])\
                        .then_inc(pt_dve, 1)

            with dve.Fori(0, NP // 2) as j:
                for u in range(2):
                    for i in range(BT):
                        s = 2 * BT * j + BT * u + i
                        kind, half, who = FILLS[i]
                        dve.wait_ge(scores_ready, s + 1)
                        for h in range(2):
                            if (u > 0 or i > 0) and h == 0:
                                dve.wait_ge(exp_ready, ONE + 2 * s)
                            nc.vector.tensor_reduce(out=negmax[:, i % 2, h:h + 1], in_=S[h][:, 0:(i + 1) * P],
                                                    op=ALU.max, axis=AX.X, negate=True).then_inc(max_ready, 1)
                        if who == "dve":
                            dve.wait_ge(proj_ready, len(FIRST) + (2 * j + u) * BT + i + 1)
                            if kind == "y":
                                dve.wait_ge(g_dve, D_FIRST + (2 * j + u) * D_PAIR + g_before(FILLS, i, "dve"))
                            empty_dve(kind, half, 1 - u, j, u)
                        copy_runs(j, u, i)
                        dve.wait_ge(exp_ready, ONE + 2 * s + 2)
                        dve.wait_ge(probs_ready, ONE + (2 * s if (u, i) == (0, 0) else 2 * s - 2))
                        nc.vector.reciprocal(rinv[:, i % 2, :], rowsum[:, i % 2, :]).then_inc(rinv_ready, 1)
            J = NP // 2
            copy_runs(J, 0, 0)
            for half in range(2):
                dve.wait_ge(proj_ready, len(FIRST) + NP * BT + half + 1)
                dve.wait_ge(g_dve, D_FIRST + NP * D_PAIR + half)
                xs = X[:, (B - 1) * BT + half * GT:(B - 1) * BT + (half + 1) * GT, :]
                nc.vector.tensor_tensor(xs, G[:, :].rearrange("p (t c) -> p t c", t=GT), xs, ALU.add)\
                    .then_inc(g_dve, 1)

        @block.gpsimd
        def _(pool):
            pool.sem_inc(probs_ready, ONE)
            nc.gpsimd.memset(probs[:, :, 1, :], 0.0).then_inc(zeroed, 1)
            nc.gpsimd.memset(V[:, 1, :, :], 0.0).then_inc(zeroed, 1)
            nc.gpsimd.memset(OT[:, :], 0.0).then_inc(zeroed, 1)
            nc.gpsimd.memset(zero_tile[:, :], 0.0).then_inc(zeroed, 1)
            pool.wait_ge(cst_loaded, 80)
            nc.gpsimd.tensor_tensor(X[:, :, :], X[:, :, :], bu[:, :].unsqueeze(1).to_broadcast([P, NT, C]), ALU.add)\
                .then_inc(bias_added, 1)
            with pool.Fori(0, NP // 2) as j:
                for u in range(2):
                    for i in range(BT):
                        s = 2 * BT * j + BT * u + i
                        pool.wait_ge(rinv_ready, s + 1)
                        pool.nop(nofuse=True)
                        for h in range(2):
                            p = probs[:, h, i % 2, 0:(i + 1) * P]
                            nc.gpsimd.tensor_scalar(p, p, rinv[:, i % 2, h:h + 1], 1.0, ALU.mult, ALU.mult)\
                                .then_inc(probs_ready, 1)


def experts(nc, X, XT, mean_var, rstd, shift, ident, rw_in, eb_in, w1_in, w2_in, sw1_in, sw2_in,
            keyrow_in, offs_in, table, zbuf, layer):
    tag = f"f{layer}"
    layernorm(nc, X, mean_var, rstd, shift, tag)
    ctx = ExitStack()
    with ctx:
        shared_out = ctx.enter_context(nc.sbuf_tensor(f"shared_out_{tag}", [P, NT, C], F32))
        gather_idx = ctx.enter_context(nc.sbuf_tensor(f"gather_idx_{tag}", [P, HE], I32))
        scatter_idx = ctx.enter_context(nc.sbuf_tensor(f"scatter_idx_{tag}", [P, HE], I32))
        router(nc, X, XT, rstd, shift, ident, rw_in, eb_in, keyrow_in, offs_in, table,
               gather_idx, scatter_idx, tag)
        routed(nc, XT, ident, w1_in, w2_in, sw1_in, sw2_in, table, zbuf[layer], gather_idx, scatter_idx,
               shared_out, tag)
        combine(nc, X, zbuf[layer], shared_out, tag)


def router(nc, X, XT, rstd, shift, ident, rw_in, eb_in, keyrow_in, offs_in, table,
           gather_idx, scatter_idx, tag):
    ctx = ExitStack()
    with ctx:
        def sb(name, shape, dt=F32):
            return ctx.enter_context(nc.sbuf_tensor(f"{name}_{tag}", shape, dt))

        def pb(name, shape, dt=F32):
            return ctx.enter_context(nc.psum_tensor(f"{name}_{tag}", shape, dt))

        def sem(name):
            return ctx.enter_context(nc.semaphore(f"{name}_{tag}"))

        rw = sb("rw", [P, E])
        eb = sb("eb", [P, E])
        keyrow = sb("keyrow", [P, T // 2])
        offs = sb("offs", [P, HE + 1])
        ident_bf = sb("ident_bf", [P, P], BF16)
        xn = sb("xn", [P, 2, GT, C])
        xg = sb("xg", [P, GC])
        scores = sb("scores", [P, GT, E])
        biased = sb("biased", [P, GT, E])
        top8 = sb("top8", [P, GT, 8])
        marked = sb("marked", [P, GT, E])
        mask = sb("mask", [P, GT, E], BF16)
        chosen = sb("chosen", [P, GT, E])
        total = sb("total", [P, GT])
        weights = sb("weights", [P, GT, E])
        keys = sb("keys", [P, T // 2])
        first = sb("first", [P, CAP])
        both = sb("both", [E, 2 * CAP])
        merged = sb("merged", [E, CAP])
        spread = sb("spread", [HE, P])
        slot_key = sb("slot_key", [P, HE])
        slot_tok = sb("slot_tok", [P, HE])
        spare = sb("spare", [P, HE])
        spare2 = sb("spare2", [P, HE])
        table_warm = sb("table_warm", [P, 1])

        tp = pb("tp", [P, GC])
        lg = pb("lg", [P, GC])
        mt = pb("mt", [P, GC], BF16)
        st = pb("st", [P, GC])

        loaded = sem("loaded")
        cast = sem("cast")
        normed = sem("normed")
        turned = sem("turned")
        xt_copied = sem("xt_copied")
        logits = sem("logits")
        scored = sem("scored")
        step = sem("step")
        mask_ready = sem("mask_ready")
        mask_turned = sem("mask_turned")
        keys_ready = sem("keys_ready")
        written = [sem(f"written{u}") for u in range(2)]
        fstep = sem("fstep")
        spread_ready = sem("spread_ready")
        spread_turned = sem("spread_turned")
        block = ctx.enter_context(nc.Block())
        tab = table.rearrange("(t p) w -> p t w", p=P)

        @block.sync
        def _(sp):
            sp.dma_start(rw[:, :], rw_in).then_inc(loaded, 16)
            sp.dma_start(eb[:, :], eb_in).then_inc(loaded, 16)
            for h in range(2):
                sp.dma_start(keyrow[h * E:(h + 1) * E, :], keyrow_in[:, h * T // 2:(h + 1) * T // 2]).then_inc(loaded, 16)
            sp.dma_start(offs[:, :], offs_in).then_inc(loaded, 16)
            for u in range(2):
                sp.sem_inc(written[u], 1)
            with sp.Fori(0, NG // 2) as j:
                for u in range(2):
                    g = 2 * j + u
                    sp.wait_ge(normed, (g + 1) * GT)
                    sp.dma_start(tab[:, ds(g * GT, GT), 0:C], xn[:, u, :, :]).then_inc(written[u], 16)
                    sp.wait_ge(mask_ready, 2 * g + 3)
                    sp.dma_start(tab[:, ds(g * GT, GT), C:], weights[:, :, :]).then_inc(written[u], 16)
            for u in range(2):
                sp.wait_ge(written[u], 32 * (NG // 2) + 1)

        @block.tensor
        def _(pe):
            pe.sem_inc(turned, 1)
            pe.sem_inc(mask_turned, 1)
            pe.wait_ge(loaded, 80)
            pe.wait_ge(cast, 1)
            for half in range(2):
                with pe.Fori(half * NG // 4, (half + 1) * NG // 4) as j:
                    for u in range(2):
                        g = 2 * j + u
                        pe.wait_ge(normed, (g + 1) * GT)
                        for k in range(GT):
                            last = nc.tensor.transpose(tp[:, k * P:(k + 1) * P], xn[:, u, k, :], ident[:, :])
                        last.then_inc(turned, 1)
                        pe.wait_ge(xt_copied, 2 * (g + 1))
                        for k in range(GT):
                            last = nc.tensor.matmul(lg[:, k * E:(k + 1) * E], xg[:, k * P:(k + 1) * P], rw[:, :],
                                                    start=True, stop=True)
                        last.then_inc(logits, 1)
                        pe.wait_ge(mask_ready, 2 * g + 2)
                        pe.nop(nofuse=True)
                        for k in range(GT):
                            last = nc.tensor.transpose(mt[half * E:(half + 1) * E, k * P:(k + 1) * P],
                                                       mask[:, k, :], ident_bf[:, :])
                        last.then_inc(mask_turned, 1)
            pe.wait_ge(spread_ready, 1)
            nc.tensor.transpose(st[:, 0:HE], spread[:, :], ident[0:HE, 0:HE]).then_inc(spread_turned, 1)

        @block.scalar
        def _(act):
            nc.scalar.activation(table_warm[:, :], ident[:, 0:1], ACT.Sigmoid)
            with act.Fori(0, NG) as g:
                act.wait_ge(turned, g + 2)
                nc.scalar.activation(xg[:, :], tp[:, :], ACT.Copy).then_inc(xt_copied, 1)
                nc.scalar.activation(XT[:, ds(g * GC, GC)], tp[:, :], ACT.Copy).then_inc(xt_copied, 1)
                act.wait_ge(logits, g + 1)
                act.wait_ge(mask_ready, 2 * g + 1)
                nc.scalar.activation(scores[:, :, :], lg[:, 0:GT * E].rearrange("p (k e) -> p k e", k=GT),
                                     ACT.Sigmoid).then_inc(scored, 1)

        @block.vector
        def _(dve):
            dve.sem_inc(mask_ready, 1)
            nc.vector.tensor_copy(ident_bf[:, :], ident[:, :]).then_inc(cast, 1)
            dve.wait_ge(loaded, 80)
            per = 2 * GT + 6

            def normalise(g, u, j):
                for k in range(GT):
                    t = g * GT + k
                    nc.vector.tensor_scalar(xn[:, u, k, :], X[:, t, :], rstd[:, ds(t, 1)], shift[:, ds(t, 1)],
                                            ALU.mult, ALU.add).then_inc(normed, 1)

            normalise(0, 0, 0)
            for half in range(2):
                with dve.Fori(half * NG // 4, (half + 1) * NG // 4) as j:
                    for u in range(2):
                        g = 2 * j + u
                        if u == 0:
                            dve.wait_ge(turned, g + 1)
                            dve.wait_ge(written[1], 32 * j + 1)
                            normalise(g + 1, 1, j)
                        else:
                            dve.wait_ge(turned, g + 1)
                            dve.wait_ge(written[0], 32 * j + 33)
                            normalise((g + 1) % NG, 0, j)
                        dve.wait_ge(scored, g + 1)
                        nc.vector.tensor_tensor(biased[:, :, :], scores[:, :, :],
                                                eb[:, :].unsqueeze(1).to_broadcast([P, GT, E]), ALU.add).then_inc(step, 1)
                        dve.wait_ge(step, g * per + 1)
                        dve.nop(nofuse=True)
                        for k in range(GT):
                            nc.vector.max(top8[:, k, :], biased[:, k, :]).then_inc(step, 1)
                        dve.wait_ge(step, g * per + 1 + GT)
                        nc.vector.memset(top8[:, :, K:], EMPTY).then_inc(step, 1)
                        dve.wait_ge(step, g * per + 2 + GT)
                        dve.nop(nofuse=True)
                        for k in range(GT):
                            nc.vector.match_replace(marked[:, k, :], top8[:, k, :], biased[:, k, :], 2 * EMPTY / 3).then_inc(step, 1)
                        dve.wait_ge(step, g * per + 2 + 2 * GT)
                        dve.wait_ge(mask_turned, g + 1)
                        nc.vector.tensor_tensor(mask[:, :, :], marked[:, :, :], biased[:, :, :], ALU.not_equal)\
                            .then_inc(mask_ready, 1)
                        dve.wait_ge(mask_ready, 2 * g + 2)
                        nc.vector.tensor_tensor(chosen[:, :, :], mask[:, :, :], scores[:, :, :], ALU.mult).then_inc(step, 1)
                        dve.wait_ge(step, g * per + 3 + 2 * GT)
                        nc.vector.tensor_reduce(out=total[:, :], in_=chosen[:, :, :], op=ALU.add, axis=AX.X).then_inc(step, 1)
                        dve.wait_ge(step, g * per + 4 + 2 * GT)
                        nc.vector.tensor_scalar(total[:, :], total[:, :], 1e-20, None, ALU.add).then_inc(step, 1)
                        dve.wait_ge(step, g * per + 5 + 2 * GT)
                        nc.vector.reciprocal(total[:, :], total[:, :]).then_inc(step, 1)
                        dve.wait_ge(step, g * per + 6 + 2 * GT)
                        nc.vector.tensor_tensor(weights[:, :, :], chosen[:, :, :],
                                                total[:, :].unsqueeze(2).to_broadcast([P, GT, E]), ALU.mult)\
                            .then_inc(mask_ready, 1)
                        dve.wait_ge(mask_turned, g + 2)
                        r = slice(half * E, (half + 1) * E)
                        cols = ds((g - half * NG // 2) * GC, GC)
                        nc.vector.tensor_tensor(keys[r, cols], mt[r, :], keyrow[r, cols], ALU.mult).then_inc(keys_ready, 1)
            dve.wait_ge(keys_ready, NG)
            n = 0

            def link(ins):
                nonlocal n
                ins.then_inc(fstep, 1)
                n += 1
                dve.wait_ge(fstep, n)

            for r in range(CAP // 8):
                link(nc.vector.max(first[:, r * 8:(r + 1) * 8], keys[:, :]))
                link(nc.vector.match_replace(keys[:, :], first[:, r * 8:(r + 1) * 8], keys[:, :], -1.0))
            link(nc.vector.tensor_copy(both[:, 0:CAP], first[0:E, :]))
            link(nc.vector.tensor_copy(both[:, CAP:], first[E:, :]))
            for r in range(CAP // 8):
                link(nc.vector.max(merged[:, r * 8:(r + 1) * 8], both[:, :]))
                link(nc.vector.match_replace(both[:, :], merged[:, r * 8:(r + 1) * 8], both[:, :], -1.0))
            link(nc.vector.memset(spread[:, :], 0.0))
            link(nc.vector.tensor_copy(spread[:, 0:CAP], merged[0:HE, :]))
            nc.vector.tensor_copy(spread[:, HD:HD + CAP], merged[HE:, :]).then_inc(spread_ready, 1)
            dve.wait_ge(spread_turned, 1)
            link(nc.vector.tensor_copy(slot_key[:, :], st[:, 0:HE]))
            link(nc.vector.tensor_scalar(slot_tok[:, :], slot_key[:, :], -1.0, float(T), ALU.mult, ALU.add))
            link(nc.vector.tensor_scalar(gather_idx[:, :], slot_tok[:, :], float(T - 1), None, ALU.min))
            link(nc.vector.tensor_scalar(spare[:, :], slot_key[:, :], 0.0, offs[:, HE:], ALU.is_equal, ALU.mult))
            link(nc.vector.tensor_tensor(spare2[:, :], spare[:, :], offs[:, 0:HE], ALU.add))
            link(nc.vector.tensor_tensor(scatter_idx[:, :], spare2[:, :], slot_tok[:, :], ALU.add))


def routed(nc, XT, ident, w1_in, w2_in, sw1_in, sw2_in, table, zb, gather_idx, scatter_idx, shared_out, tag):
    ctx = ExitStack()
    with ctx:
        def sb(name, shape, dt=F32):
            return ctx.enter_context(nc.sbuf_tensor(f"{name}_{tag}", shape, dt))

        def pb(name, shape, dt=F32):
            return ctx.enter_context(nc.psum_tensor(f"{name}_{tag}", shape, dt))

        def sem(name):
            return ctx.enter_context(nc.semaphore(f"{name}_{tag}"))

        R = 4
        w1 = sb("w1", [P, R, P])
        w2 = sb("w2", [P, R, P])
        sw1 = sb("sw1", [P, SF])
        sw2 = sb("sw2", [P, 2, C])
        gi = [sb(f"gi{u}", [P, 1], I32) for u in range(R)]
        si = [sb(f"si{u}", [P, 1], I32) for u in range(R)]
        rows = [sb(f"rows{u}", [P, TW]) for u in range(R)]
        xs = sb("xs", [P, 2, P])
        hid = sb("hid", [P, 2, HD])
        ys = [sb(f"ys{u}", [P, C]) for u in range(2)]
        hidden = sb("hidden", [P, 2, 2 * P])
        table_warm = sb("table_warm2", [P, 1])
        tg = [pb(f"tg{u}", [P, P]) for u in range(2)]
        hq = [pb(f"hq{u}", [P, HD]) for u in range(2)]
        yq = [pb(f"yq{u}", [P, C]) for u in range(2)]
        hp = pb("hp", [P, 2, 2 * P])
        sp_out = pb("sp_out", [P, 2, C])

        w_loaded = [sem(f"w_loaded{u}") for u in range(R)]
        sw_loaded = sem("sw_loaded")
        idx_ready = sem("idx_ready")
        gathered = [sem(f"gathered{u}") for u in range(R)]
        scattered = sem("scattered")
        rows_turned = sem("rows_turned")
        xs_copied = sem("xs_copied")
        h_ready = sem("hid_ready")
        gelu_ready = sem("hgelu_ready")
        y_ready = sem("y_ready")
        y_scaled = sem("y_scaled")
        sh_ready = sem("sh_ready")
        sh_gelu = sem("sh_gelu")
        s_ready = sem("s_ready")
        s_copied = sem("s_copied")
        block = ctx.enter_context(nc.Block())
        J = HE // R
        AHEAD = R - 1

        @block.sync
        def _(sp):
            sp.dma_start(sw1[:, :], sw1_in).then_inc(sw_loaded, 16)
            sp.dma_start(sw2[:, :, :], sw2_in.rearrange("(k p) c -> p k c", p=P)).then_inc(sw_loaded, 16)
            with sp.Fori(0, J) as j:
                for u in range(R):
                    m = R * j + u
                    if u == 0:
                        sp.wait_ge(y_ready, m + 1)
                    sp.dma_start(w1[:, u, :], w1_in[ds(m, 1)].rearrange("a p c -> (a p) c")).then_inc(w_loaded[u], 16)
                    sp.dma_start(w2[:, u, :], w2_in[ds(m, 1)].rearrange("a p c -> (a p) c")).then_inc(w_loaded[u], 16)
            sp.wait_ge(sw_loaded, 32)

        @block.gpsimd
        def _(pool):
            def gather(m, u, done):
                nc.gpsimd.tensor_copy(gi[u][:, :], gather_idx[:, ds(m, 1)]).then_inc(idx_ready, 1)
                pool.wait_ge(idx_ready, done)
                pool.nop(nofuse=True)
                nc.gpsimd.indirect_dma_start(out=rows[u][:, :], out_offset=None, in_=table,
                                             in_offset=bass.IndirectOffsetOnAxis(ap=gi[u][:, 0:1], axis=0))\
                    .then_inc(gathered[u], 16)

            for m in range(AHEAD):
                gather(m, m, m + 1)
            with pool.Fori(0, J) as j:
                for u in range(R):
                    m = R * j + u
                    nc.gpsimd.tensor_copy(si[u][:, :], scatter_idx[:, ds(m, 1)]).then_inc(idx_ready, 1)
                    pool.wait_ge(y_scaled, 2 * m + 1)
                    gather((m + AHEAD) % HE, (u + AHEAD) % R, 2 * m + AHEAD + 2)
                    if u:
                        pool.wait_ge(scattered, 16 * m)
                    pool.wait_ge(y_scaled, 2 * m + 3)
                    pool.nop(nofuse=True)
                    nc.gpsimd.indirect_dma_start(out=zb, out_offset=bass.IndirectOffsetOnAxis(ap=si[u][:, 0:1], axis=0),
                                                 in_=ys[u % 2][:, :], in_offset=None, compute_op=ALU.add)\
                        .then_inc(scattered, 16)
                pool.wait_ge(scattered, 16 * R * (j + 1))
            pool.wait_ge(scattered, 16 * HE)
            for u in range(AHEAD):
                pool.wait_ge(gathered[u], 16 * (J + 1))

        @block.tensor
        def _(pe):
            def turn(u, at, n):
                pe.wait_ge(gathered[u], n)
                nc.tensor.transpose(tg[at][:, :], rows[u][:, 0:C], ident[:, :]).then_inc(rows_turned, 1)

            pe.sem_inc(y_ready, 1)
            turn(0, 0, 16)
            pe.wait_ge(sw_loaded, 32)
            with pe.Fori(0, J) as j:
                for u in range(R):
                    m = R * j + u
                    b = u % 2
                    turn((u + 1) % R, 1 - b, 16 * (j + 1) if u + 1 < R else 16 * (j + 2))
                    pe.wait_ge(xs_copied, m + 1)
                    pe.wait_ge(w_loaded[u], 32 * (j + 1))
                    for h in range(2):
                        last = nc.tensor.matmul(hq[b][h * HD:(h + 1) * HD, :], w1[:, u, h * HD:(h + 1) * HD],
                                                xs[:, b, h * HD:(h + 1) * HD], start=True, stop=True)
                    last.then_inc(h_ready, 1)
                    if b == 0:
                        for c in range(2):
                            last = nc.tensor.matmul(hp[:, c, :], sw1[:, c * P:(c + 1) * P],
                                                    XT[:, ds(m * P, 2 * P)], start=True, stop=True)
                        last.then_inc(sh_ready, 1)
                    else:
                        n = (R // 2) * j + u // 2
                        pe.wait_ge(sh_gelu, n + 1)
                        pe.wait_ge(s_copied, n + 1)
                        for k in range(2):
                            for c in range(2):
                                last = nc.tensor.matmul(sp_out[:, k, :], hidden[:, c, k * P:(k + 1) * P],
                                                        sw2[:, c, :], start=(c == 0), stop=(c == 1))
                        last.then_inc(s_ready, 1)
                    pe.wait_ge(gelu_ready, m + 1)
                    pe.nop(nofuse=True)
                    for h in range(2):
                        r = slice(h * HD, (h + 1) * HD)
                        last = nc.tensor.matmul(yq[b][r, :], hid[r, b, :], w2[r, u, :], start=True, stop=True)
                    last.then_inc(y_ready, 1)

        @block.scalar
        def _(act):
            act.sem_inc(s_copied, 1)
            nc.scalar.activation(table_warm[:, :], ident[:, 0:1], ACT.Gelu_apprx_tanh)
            with act.Fori(0, J) as j:
                for u in range(R):
                    m = R * j + u
                    b = u % 2
                    act.wait_ge(h_ready, m + 1)
                    nc.scalar.activation(hid[:, b, :], hq[b][:, :], ACT.Gelu_apprx_tanh).then_inc(gelu_ready, 1)
                    n = (R // 2) * j + u // 2
                    if b == 0:
                        act.wait_ge(sh_ready, n + 1)
                        nc.scalar.activation(hidden[:, :, :], hp[:, :, :], ACT.Gelu_apprx_tanh).then_inc(sh_gelu, 1)
                    else:
                        act.wait_ge(s_ready, n + 1)
                        nc.scalar.activation(shared_out[:, ds(2 * n, 2), :], sp_out[:, :, :], ACT.Copy)\
                            .then_inc(s_copied, 1)

        @block.vector
        def _(dve):
            dve.sem_inc(y_scaled, 1)

            def copy_xs(m, b):
                dve.wait_ge(rows_turned, m + 1)
                nc.vector.tensor_copy(xs[:, b, :], tg[b][:, :]).then_inc(xs_copied, 1)

            copy_xs(0, 0)
            with dve.Fori(0, J) as j:
                for u in range(R):
                    m = R * j + u
                    b = u % 2
                    copy_xs(m + 1, 1 - b)
                    dve.wait_ge(y_ready, m + 2)
                    dve.wait_ge(idx_ready, 2 * m + AHEAD + 1)
                    for h in range(2):
                        r = slice(h * HD, (h + 1) * HD)
                        nc.vector.tensor_scalar(ys[b][r, :], yq[b][r, :], rows[u][r, ds(C + h * HE + m, 1)], None,
                                                ALU.mult).then_inc(y_scaled, 1)


def combine(nc, X, zb, shared_out, tag):
    ctx = ExitStack()
    with ctx:
        z = [ctx.enter_context(nc.sbuf_tensor(f"z{h}_{tag}", [P, NT, C], F32)) for h in range(2)]
        z_loaded = [ctx.enter_context(nc.semaphore(f"z_loaded{c}_{tag}")) for c in range(B)]
        added = ctx.enter_context(nc.semaphore(f"added_{tag}"))
        block = ctx.enter_context(nc.Block())

        @block.sync
        def _(sp):
            for c in range(B):
                for h in range(2):
                    src = zb[h * ZR:h * ZR + T, :].rearrange("(t p) c -> p t c", p=P)
                    ts = slice(c * BT, (c + 1) * BT)
                    sp.dma_start(z[h][:, ts, :], src[:, ts, :]).then_inc(z_loaded[c], 16)

        @block.vector
        def _(dve):
            nc.vector.tensor_tensor(X[:, :, :], X[:, :, :], shared_out[:, :, :], ALU.add).then_inc(added, 1)
            n = 1
            for c in range(B):
                ts = slice(c * BT, (c + 1) * BT)
                dve.wait_ge(z_loaded[c], 32)
                for h in range(2):
                    dve.wait_ge(added, n)
                    nc.vector.tensor_tensor(X[:, ts, :], X[:, ts, :], z[h][:, ts, :], ALU.add).then_inc(added, 1)
                    n += 1


def attention_b(nc, X, mean_var, rstd, shift, ident, wq_in, wkv_in, wp_in, bp_in, headmask_in):
    layernorm(nc, X, mean_var, rstd, shift, "b")
    ctx = ExitStack()
    with ctx:
        def sb(name, shape, dt=F32):
            return ctx.enter_context(nc.sbuf_tensor(f"{name}_b", shape, dt))

        def pb(name, shape, dt=F32):
            return ctx.enter_context(nc.psum_tensor(f"{name}_b", shape, dt))

        def sem(name):
            return ctx.enter_context(nc.semaphore(f"{name}_b"))

        wq = sb("wq", [P, C])
        wkv = sb("wkv", [P, 2 * C])
        wp = sb("wp", [P, C])
        bp = sb("bp", [P, C])
        headmask = sb("headmask", [P, C])
        xn = sb("xn", [P, BT, C])
        xb = sb("xb", [P, N])
        kk = sb("kk", [P, BT, C])
        vv = sb("vv", [P, BT, C + 1])
        qT = sb("qT", [P, N])
        W = C + HB
        kv = sb("kv", [P, W])
        ksum = sb("ksum", [P, 1])
        z = sb("z", [P, BT, HB])
        o = sb("o", [P, BT, C])
        oT = sb("oT", [P, N])
        tp = [pb(f"tp{u}", [P, GC]) for u in range(2)]
        pj = [pb(f"pj{u}", [P, GC]) for u in range(2)]
        kvp = pb("kvp", [P, GC])
        op = [pb(f"op{u}", [P, 2, 2 * C]) for u in range(2)]

        loaded = sem("loaded")
        ones_set = sem("ones_set")
        normed = sem("normed")
        turned = sem("turned")
        t_copied = sem("t_copied")
        pj_ready = sem("pj_ready")
        pj_act = sem("pj_act")
        pj_dve = sem("pj_dve")
        kv_ready = sem("kv_ready")
        kstep = sem("kstep")
        op_ready = sem("op_ready")
        o_ready = sem("o_ready")
        zstep = sem("zstep")
        biased = sem("biased")
        block = ctx.enter_context(nc.Block())

        @block.sync
        def _(sp):
            for dst, src in ((wq, wq_in), (wkv, wkv_in), (wp, wp_in), (bp, bp_in), (headmask, headmask_in)):
                sp.dma_start(dst[:, :], src).then_inc(loaded, 16)

        @block.gpsimd
        def _(pool):
            nc.gpsimd.memset(vv[:, :, C:], 1.0).then_inc(ones_set, 1)
            pool.wait_ge(loaded, 80)
            with pool.Fori(0, B) as b:
                pool.wait_ge(normed, (b + 1) * BT)
                xs = X[:, ds(b * BT, BT), :]
                nc.gpsimd.tensor_tensor(xs, xs, bp[:, :].unsqueeze(1).to_broadcast([P, BT, C]), ALU.add)\
                    .then_inc(biased, 1)

        @block.tensor
        def _(pe):
            pe.wait_ge(loaded, 80)
            pe.wait_ge(ones_set, 1)
            with pe.Fori(0, B) as b:
                for h in range(2):
                    pe.wait_ge(normed, b * BT + (h + 1) * GT)
                    for k in range(GT):
                        last = nc.tensor.transpose(tp[h][:, k * P:(k + 1) * P], xn[:, h * GT + k, :], ident[:, :])
                    last.then_inc(turned, 1)
                pe.wait_ge(t_copied, 4 * b + 2)
                for n in range(4):
                    if n >= 2:
                        pe.wait_ge(pj_act, 6 * b + n - 1)
                        pe.wait_ge(pj_dve, 6 * b + n)
                    elif n == 0:
                        pe.wait_ge(pj_dve, 6 * b + 1)
                    for k in range(2):
                        t = 2 * n + k
                        last = nc.tensor.matmul(pj[n % 2][:, k * 2 * C:(k + 1) * 2 * C], xb[:, t * P:(t + 1) * P],
                                                wkv[:, :], start=True, stop=True)
                    last.then_inc(pj_ready, 1)
                for n in range(2):
                    pe.wait_ge(pj_act, 6 * b + n + 3)
                    pe.wait_ge(pj_dve, 6 * b + n + 4)
                    nc.tensor.matmul(pj[n][:, :], wq[:, :], xb[:, n * GC:(n + 1) * GC], start=True, stop=True)\
                        .then_inc(pj_ready, 1)
                for t in range(BT):
                    last = nc.tensor.matmul(kvp[:, 0:C + 1], kk[:, t, :], vv[:, t, :], start=(t == 0), stop=(t == BT - 1))
                last.then_inc(kv_ready, 1)
                pe.wait_ge(pj_act, 6 * b + 6)
                pe.wait_ge(kstep, 3 * b + 3)
                for n in range(4):
                    if n >= 2:
                        pe.wait_ge(o_ready, 4 * b + n - 1)
                    for k in range(2):
                        t = 2 * n + k
                        last = nc.tensor.matmul(op[n % 2][:, k, 0:W], qT[:, t * P:(t + 1) * P], kv[:, :],
                                                start=True, stop=True)
                    last.then_inc(op_ready, 1)
                for h in range(2):
                    pe.wait_ge(o_ready, 4 * b + 2 * h + 2)
                    for k in range(GT):
                        last = nc.tensor.transpose(tp[h][:, k * P:(k + 1) * P], o[:, h * GT + k, :], ident[:, :])
                    last.then_inc(turned, 1)
                for h in range(2):
                    pe.wait_ge(t_copied, 4 * b + 3 + h)
                    for k in range(GT):
                        t = h * GT + k
                        last = nc.tensor.matmul(pj[h][:, k * P:(k + 1) * P], oT[:, t * P:(t + 1) * P], wp[:, :],
                                                start=True, stop=True)
                    last.then_inc(pj_ready, 1)

        @block.scalar
        def _(act):
            with act.Fori(0, B) as b:
                for h in range(2):
                    act.wait_ge(turned, 4 * b + h + 1)
                    nc.scalar.activation(xb[:, h * GC:(h + 1) * GC], tp[h][:, :], ACT.Copy).then_inc(t_copied, 1)
                for n in range(4):
                    act.wait_ge(pj_dve, 6 * b + n + 2)
                    nc.scalar.activation(kk[:, 2 * n:2 * n + 2, :],
                                         pj[n % 2][:, :].rearrange("p (k s c) -> p k s c", k=2, s=2)[:, :, 0, :],
                                         ACT.Relu).then_inc(pj_act, 1)
                for n in range(2):
                    act.wait_ge(pj_ready, 8 * b + 5 + n)
                    nc.scalar.activation(qT[:, n * GC:(n + 1) * GC], pj[n][:, :], ACT.Relu).then_inc(pj_act, 1)
                for h in range(2):
                    act.wait_ge(turned, 4 * b + 3 + h)
                    nc.scalar.activation(oT[:, h * GC:(h + 1) * GC], tp[h][:, :], ACT.Copy).then_inc(t_copied, 1)

        @block.vector
        def _(dve):
            dve.sem_inc(pj_dve, 1)
            dve.wait_ge(loaded, 80)
            dve.wait_ge(ones_set, 1)
            with dve.Fori(0, B) as b:
                for t in range(BT):
                    tt = b * BT + t
                    nc.vector.tensor_scalar(xn[:, t, :], X[:, tt, :], rstd[:, ds(tt, 1)], shift[:, ds(tt, 1)],
                                            ALU.mult, ALU.add).then_inc(normed, 1)
                for n in range(4):
                    dve.wait_ge(pj_ready, 8 * b + n + 1)
                    nc.vector.tensor_copy(vv[:, 2 * n:2 * n + 2, 0:C],
                                          pj[n % 2][:, :].rearrange("p (k s c) -> p k s c", k=2, s=2)[:, :, 1, :])\
                        .then_inc(pj_dve, 1)
                dve.wait_ge(kv_ready, b + 1)
                nc.vector.tensor_tensor(kv[:, 0:C], kvp[:, 0:C], headmask[:, :], ALU.mult).then_inc(kstep, 1)
                nc.vector.tensor_copy(ksum[:, :], kvp[:, C:C + 1]).then_inc(kstep, 1)
                dve.wait_ge(kstep, 3 * b + 2)
                nc.vector.tensor_scalar(kv[:, C:], headmask[:, ::DB], ksum[:, 0:1], None, ALU.mult).then_inc(kstep, 1)
                for n in range(4):
                    dve.wait_ge(op_ready, 4 * b + n + 1)
                    zz = z[:, 2 * n:2 * n + 2, :]
                    nc.vector.tensor_scalar(zz, op[n % 2][:, :, C:W], EPS_Z, None, ALU.add).then_inc(zstep, 1)
                    dve.wait_ge(zstep, 8 * b + 2 * n + 1)
                    nc.vector.reciprocal(zz, zz).then_inc(zstep, 1)
                    dve.wait_ge(zstep, 8 * b + 2 * n + 2)
                    for k in range(2):
                        last = nc.vector.tensor_tensor(
                            o[:, 2 * n + k, :].rearrange("p (h d) -> p h d", h=HB),
                            op[n % 2][:, k, 0:C].rearrange("p (h d) -> p h d", h=HB),
                            z[:, 2 * n + k, :].unsqueeze(2).to_broadcast([P, HB, DB]), ALU.mult)
                    last.then_inc(o_ready, 1)
                dve.wait_ge(biased, b + 1)
                for h in range(2):
                    dve.wait_ge(pj_ready, 8 * b + 7 + h)
                    xs = X[:, ds(b * BT + h * GT, GT), :]
                    nc.vector.tensor_tensor(xs, pj[h][:, :].rearrange("p (t c) -> p t c", t=GT), xs, ALU.add)\
                        .then_inc(pj_dve, 1)


def kernel(**inputs):
    import numpy as np
    import concourse.bacc as bacc
    from concourse.bass_utils import run_bass_kernel_spmd as run

    g = {k.replace("L0_", ""): np.asarray(v) for k, v in inputs.items()}
    nc = bacc.Bacc("TRN2", target_bir_lowering=False, num_devices=1)
    arrays = {}

    def give(name, a):
        a = np.ascontiguousarray(a, dtype=np.float32)
        arrays[name + "_in"] = a
        return nc.dram_tensor(name + "_in", a.shape, F32, kind="ExternalInput").ap()

    r64 = np.arange(P) % HD
    NEG = -1.0e30
    causal = np.concatenate([np.where(np.arange(P)[None, :] > r64[:, None], NEG, 0.0),
                             np.where(np.arange(HD)[None, :] > r64[:, None], NEG, 0.0)], axis=1)
    causal_sel = np.stack([np.arange(P)[None, :] == r64[:, None], np.arange(P)[None, :] == HD + r64[:, None]], axis=1)
    wqk = np.stack([g["attn_a_w_q"].reshape(C, PAIRS, P).transpose(1, 0, 2),
                    g["attn_a_w_k"].reshape(C, PAIRS, P).transpose(1, 0, 2)], axis=2)
    half, tok = np.arange(P) // HD, np.arange(P)
    offs = (half[:, None] * ZR + np.zeros((1, HE))).astype(np.float32)
    wqkvB = g["attn_b_w_qkv"]
    w1 = g["ffn_w1"].reshape(2, HE, C, F).transpose(1, 2, 0, 3).reshape(HE, C, 2 * F)
    w2 = g["ffn_w2"].reshape(2, HE, F, C).transpose(1, 0, 2, 3).reshape(HE, 2 * F, C)
    args = [
        give("x", g["attn_a_x"].reshape(T, C)),
        give("ident", np.eye(P)), give("causal", causal), give("causal_sel", causal_sel),
        give("wqk", wqk), give("wv", g["attn_a_w_v"].reshape(C, PAIRS, P).transpose(1, 0, 2)),
        give("wu", g["attn_a_w_u"].reshape(PAIRS, P, C)), give("bu", np.broadcast_to(g["attn_a_b_u"], (P, C))),
        give("wqB", wqkvB[:C].T), give("wkvB", wqkvB[C:].T), give("wpB", g["attn_b_w_proj"].T),
        give("bpB", np.broadcast_to(g["attn_b_b_proj"], (P, C))),
        give("headmask", np.kron(np.eye(HB), np.ones((DB, DB)))),
        give("rw", g["ffn_router_weight"].T), give("eb", np.broadcast_to(g["ffn_expert_bias"], (P, E))),
        give("w1", w1), give("w2", w2),
        give("sw1", g["ffn_sw1"].T), give("sw2", g["ffn_sw2"].T),
        give("keyrow", np.broadcast_to(T - np.arange(T), (HD, T))),
        give("offs", np.concatenate([offs, tok[:, None]], axis=1)),
    ]
    out = nc.dram_tensor("out", (T, C), F32, kind="ExternalOutput").ap()
    table = nc.dram_tensor("table", (T, TW), F32).ap()
    zbuf = [nc.dram_tensor(f"zbuf{n}", (2 * ZR, C), F32).ap() for n in range(2)]
    build(nc, *args, out, table, zbuf, STOP)
    r = run(nc, [arrays], core_ids=[0])
    return r.results[0]["out"].reshape(B, N, C)


STOP = None
```

```python
import concourse.bass as bass
from concourse import mybir
from contextlib import ExitStack

F32 = mybir.dt.float32
F32R = mybir.dt.float32r
BF16 = mybir.dt.bfloat16
I32 = mybir.dt.int32
ALU = mybir.AluOpType
ACT = mybir.ActivationFunctionType
AX = mybir.AxisListType
ds = bass.ds

P = 128
B, N, C = 4, 1024, 128
T = B * N
NT = T // P
BT = N // P
GT = 4
NG = NT // GT
GC = GT * P
EPS_LN = 1e-5

HEADS, HD = 16, 64
PAIRS = HEADS // 2
NP = B * PAIRS
SCALE_QK = 1.0 / HD

HB, DB = 16, 8
EPS_Z = 1.1920928955078125e-07

E, K, F = 64, 6, 64
CAP = 2 * ((256 * K + E - 1) // E)
HE = E // 2
SF = 256
ZR = T + P
TW = C + E
ZPARTS = 8
EMPTY = -3.0e38


class Steps:

    def __init__(self, eng, sem):
        self.eng, self.sem, self.n = eng, sem, 0

    def mark(self, ins):
        ins.then_inc(self.sem, 1)
        self.n += 1
        return self.n

    def wait(self, n=None):
        self.eng.wait_ge(self.sem, self.n if n is None else n)


def blocks_of(i):
    return [(k, min(k + GT, i + 1)) for k in range(0, i + 1, GT)]


def evacs(i):
    return sum(len(blocks_of(k)) for k in range(i))


EV_PAIR = evacs(BT)


def build(nc, x, ident_in, causal_in, causal_sel_in, wqk_in, wv_in, wu_in, bu_in,
          wqB_in, wkvB_in, wpB_in, bpB_in, headmask_in, rw_in, eb_in, w1_in, w2_in, sw1_in, sw2_in,
          keyrow_in, offs_in, out, table, zbuf, stop):
    ctx = ExitStack()
    with ctx:
        def sb(name, shape, dt=F32):
            return ctx.enter_context(nc.sbuf_tensor(name, shape, dt))

        def sem(name):
            return ctx.enter_context(nc.semaphore(name))

        X = sb("X", [P, NT, C])
        XT = sb("XT", [P, T])
        ident = sb("ident", [P, P])
        mean_var = sb("mean_var", [P, NT, 2])
        rstd = sb("rstd", [P, NT])
        shift = sb("shift", [P, NT])

        in_loaded = sem("in_loaded")

        with nc.Block() as block:
            @block.sync
            def _(sp):
                sp.dma_start(X[:, :, :], x.rearrange("(t p) c -> p t c", p=P)).then_inc(in_loaded, 16)
                sp.dma_start(ident[:, :], ident_in).then_inc(in_loaded, 16)
                sp.wait_ge(in_loaded, 32)

        layernorm(nc, X, mean_var, rstd, shift, "a")
        transpose_x(nc, X, XT, rstd, shift, ident, "a")
        attention_a(nc, X, XT, ident, causal_in, causal_sel_in, wqk_in, wv_in, wu_in, bu_in, zbuf)
        if stop == "a":
            return store(nc, X, out, sem)
        experts(nc, X, XT, mean_var, rstd, shift, ident, rw_in, eb_in, w1_in, w2_in, sw1_in, sw2_in,
                keyrow_in, offs_in, table, zbuf, 0)
        if stop == "f":
            return store(nc, X, out, sem)
        attention_b(nc, X, mean_var, rstd, shift, ident, wqB_in, wkvB_in, wpB_in, bpB_in, headmask_in)
        if stop == "b":
            return store(nc, X, out, sem)
        experts(nc, X, XT, mean_var, rstd, shift, ident, rw_in, eb_in, w1_in, w2_in, sw1_in, sw2_in,
                keyrow_in, offs_in, table, zbuf, 1)
        store(nc, X, out, sem)


def store(nc, X, out, sem):
    out_done = sem("out_done")
    with nc.Block() as block:
        @block.sync
        def _(sp):
            sp.dma_start(out.rearrange("(t p) c -> p t c", p=P), X[:, :, :]).then_inc(out_done, 16)
            sp.wait_ge(out_done, 16)


def layernorm(nc, X, mean_var, rstd, shift, tag):
    ctx = ExitStack()
    with ctx:
        stats = ctx.enter_context(nc.sbuf_tensor(f"stats_{tag}", [P, 2, BT, 6], F32))
        stat_step = ctx.enter_context(nc.semaphore(f"stat_step_{tag}"))
        fin_step = ctx.enter_context(nc.semaphore(f"fin_step_{tag}"))
        std_done = ctx.enter_context(nc.semaphore(f"std_done_{tag}"))
        block = ctx.enter_context(nc.Block())

        @block.vector
        def _(dve):
            n = 0
            for g in range(B):
                for k in range(BT):
                    nc.vector.bn_stats(stats[:, g % 2, k, :], X[:, g * BT + k, :]).then_inc(stat_step, 1)
                n += BT
                dve.wait_ge(stat_step, n)
                for k in range(BT):
                    nc.vector.bn_aggr(mean_var[:, g * BT + k, :], stats[:, g % 2, k, :]).then_inc(stat_step, 1)
                n += BT
            dve.wait_ge(stat_step, n)
            nc.vector.tensor_scalar(rstd[:, :], mean_var[:, :, 1], EPS_LN, None, ALU.add).then_inc(fin_step, 1)
            dve.wait_ge(std_done, 1)
            nc.vector.reciprocal(rstd[:, :], rstd[:, :]).then_inc(fin_step, 1)
            dve.wait_ge(fin_step, 2)
            nc.vector.scalar_tensor_tensor(out=shift[:, :], in0=mean_var[:, :, 0], scalar=-1.0, in1=rstd[:, :],
                                           op0=ALU.mult, op1=ALU.mult).then_inc(fin_step, 1)

        @block.scalar
        def _(act):
            act.wait_ge(fin_step, 1)
            nc.scalar.activation(rstd[:, :], rstd[:, :], ACT.Sqrt).then_inc(std_done, 1)


def transpose_x(nc, X, XT, rstd, shift, ident, tag):
    ctx = ExitStack()
    with ctx:
        xn = ctx.enter_context(nc.sbuf_tensor(f"xn_{tag}", [P, 2, GT, C], F32))
        tps = [ctx.enter_context(nc.psum_tensor(f"tps_{tag}{u}", [P, GC], F32)) for u in range(2)]
        normed = ctx.enter_context(nc.semaphore(f"normed_{tag}"))
        turned = ctx.enter_context(nc.semaphore(f"turned_{tag}"))
        copied = ctx.enter_context(nc.semaphore(f"copied_{tag}"))
        block = ctx.enter_context(nc.Block())

        @block.vector
        def _(dve):
            with dve.Fori(0, NG // 2) as j:
                for u in range(2):
                    if u == 0:
                        dve.wait_ge(turned, 2 * j + 1)
                    for k in range(GT):
                        t = (2 * j + u) * GT + k
                        nc.vector.tensor_scalar(xn[:, u, k, :], X[:, t, :], rstd[:, ds(t, 1)], shift[:, ds(t, 1)],
                                                ALU.mult, ALU.add).then_inc(normed, 1)

        @block.tensor
        def _(pe):
            pe.sem_inc(turned, 1)
            with pe.Fori(0, NG // 2) as j:
                for u in range(2):
                    pe.wait_ge(normed, (2 * j + u + 1) * GT)
                    pe.wait_ge(copied, 2 * j + 1)
                    for k in range(GT):
                        last = nc.tensor.transpose(tps[u][:, k * P:(k + 1) * P], xn[:, u, k, :], ident[:, :])
                    last.then_inc(turned, 1)

        @block.scalar
        def _(act):
            act.sem_inc(copied, 1)
            with act.Fori(0, NG // 2) as j:
                for u in range(2):
                    act.wait_ge(turned, 2 * j + u + 2)
                    nc.scalar.activation(XT[:, ds((2 * j + u) * GC, GC)], tps[u][:, :], ACT.Copy).then_inc(copied, 1)


def attention_a(nc, X, XT, ident, causal_in, causal_sel_in, wqk_in, wv_in, wu_in, bu_in, zbuf):
    ctx = ExitStack()
    with ctx:
        def sb(name, shape, dt=F32):
            return ctx.enter_context(nc.sbuf_tensor(name, shape, dt))

        def pb(name, shape, dt=F32):
            return ctx.enter_context(nc.psum_tensor(name, shape, dt))

        def sem(name):
            return ctx.enter_context(nc.semaphore(name))

        causal_f = sb("causal_f", [P, P + HD])
        causal_sel_f = sb("causal_sel_f", [P, 2, P])
        causal = sb("causal", [P, P + HD], BF16)
        causal_sel = sb("causal_sel", [P, 2, P], BF16)
        wv = sb("wv", [P, PAIRS, P])
        wu = sb("wu", [P, 2, P])
        bu = sb("bu", [P, C])
        wqk = sb("wqk", [P, 2, 2, P])
        xb = sb("xb", [P, 2, N])
        QT = sb("QT", [P, N])
        KT = sb("KT", [P, N])
        Q2 = sb("Q2", [P, 2, 2, N], F32R)
        KH = sb("KH", [P, 2, 2, N], F32R)
        KL = sb("KL", [P, 2, 2, N], F32R)
        V = sb("V", [P, 2, BT, P])
        probs = sb("probs", [P, 2, 2, N])
        PT = sb("PT", [P, 2, 2, N])
        OT = sb("OT", [P, N])
        YT = sb("YT", [P, T])
        zero_tile = sb("zero_tile", [P, 2 * ZR * C // P // ZPARTS])
        negmax = sb("negmax", [P, 2, 2])
        rowsum = sb("rowsum", [P, 2, BT, 2])
        rinv = sb("rinv", [P, BT, 2])
        rinv_wide = sb("rinv_wide", [P, BT, 2, HD])
        exp_warm = sb("exp_warm", [P, 1])

        S = [pb(f"S{h}", [P, N]) for h in range(2)]
        TP = [pb(f"TP{u}", [P, GC]) for u in range(2)]
        O = pb("O", [P, GC])
        G = pb("G", [P, GC])

        cst_loaded = sem("cst_loaded")
        cst_cast = sem("cst_cast")
        zeroed = sem("zeroed")
        pt_zeroed = sem("pt_zeroed")
        z_cleared = sem("z_cleared")
        bias_added = sem("bias_added")
        pair_loaded = [sem(f"pair_loaded{u}") for u in range(2)]
        scores_ready = sem("scores_ready")
        max_ready = sem("max_ready")
        exp_ready = sem("exp_ready")
        rinv_ready = sem("rinv_ready")
        run_turned = sem("run_turned")
        pt_dve = sem("pt_dve")
        pt_act = sem("pt_act")
        summed = sem("summed")
        o_copied = sem("o_copied")
        widened = sem("widened")
        rinv_turned = sem("rinv_turned")
        ot_scaled = sem("ot_scaled")
        wu_loaded = [sem(f"wu_loaded{u}") for u in range(2)]
        yt_turned = sem("yt_turned")
        x_added = sem("x_added")
        proj_ready = sem("proj_ready")
        g_act = sem("g_act")
        g_dve = sem("g_dve")
        part_act = sem("part_act")
        part_dve = sem("part_dve")
        q_split = sem("q_split")
        k_split = sem("k_split")
        y_added = sem("y_added")

        FILLS = [("q", 0, "act"), ("q", 1, "act"), ("k", 0, "act"), ("k", 1, "dve"),
                 ("y", 0, "dve"), ("y", 1, "dve"), ("v", 0, "act"), ("v", 1, "act")]
        FIRST = [f for f in FILLS if f[0] != "y"]
        A_PAIR = sum(f[2] == "act" for f in FILLS)
        D_PAIR = sum(f[2] == "dve" for f in FILLS)
        A_FIRST = sum(f[2] == "act" for f in FIRST)
        D_FIRST = sum(f[2] == "dve" for f in FIRST)

        HI, LO = slice(0, HD), slice(HD, P)
        OWN, OTHER = (HI, LO), (LO, HI)

        def round_part(eng_copy, n, par, h):
            if n == 0:
                return eng_copy(Q2[OWN[h], par, h, :], QT[OWN[h], :])
            return eng_copy(KH[(OWN if n == 1 else OTHER)[h], par, h, :], KT[OWN[h], :])

        def g_before(fills, n, eng):
            return sum(f[2] == eng for f in fills[:n])

        def copied(fills, kind, who):
            return g_before(fills, max(n + 1 for n in range(len(fills)) if fills[n][0] == kind), who)

        PART_ACT = [2, 4, 6]
        PART_DVE = [3, 4, 5]

        def ev_count(i):
            last = len(blocks_of(BT - 1))
            if i == -2:
                return 0
            return last + evacs(i + 1)

        ONE = 1
        EXP0 = 2
        block = ctx.enter_context(nc.Block())

        @block.sync
        def _(sp):
            sp.dma_start(causal_f[:, :], causal_in).then_inc(cst_loaded, 16)
            sp.dma_start(causal_sel_f[:, :, :], causal_sel_in).then_inc(cst_loaded, 16)
            sp.dma_start(bu[:, :], bu_in).then_inc(cst_loaded, 16)
            sp.dma_start(wv[:, :, :], wv_in.rearrange("n p c -> p n c")).then_inc(cst_loaded, 16)
            sp.dma_start(wu[:, 1, :], wu_in[0]).then_inc(wu_loaded[1], 16)
            for u in range(2):
                sp.dma_start(wqk[:, u, :, :], wqk_in[u]).then_inc(pair_loaded[u], 16)
                sp.dma_start(xb[:, u, :], XT[:, 0:N]).then_inc(pair_loaded[u], 16)
            sp.wait_ge(zeroed, 5)
            for zb in zbuf:
                rows = zb.rearrange("(p r) c -> p (r c)", p=P)
                w = rows.shape[1] // ZPARTS
                for n in range(ZPARTS):
                    sp.dma_start(rows[:, n * w:(n + 1) * w], zero_tile[:, :]).then_inc(z_cleared, 16)
            with sp.Fori(0, NP // 2) as j:
                for u in range(2):
                    nxt = 2 * ((j + 1) % 4) + u
                    batch = ((j + 1) // 4) % 4
                    sp.wait_ge(proj_ready, len(FIRST) + (2 * j + u) * BT)
                    sp.dma_start(wqk[:, u, :, :], wqk_in[ds(nxt, 1)].rearrange("a p q c -> (a p) q c"))\
                        .then_inc(pair_loaded[u], 16)
                    sp.dma_start(xb[:, u, :], XT[:, ds(batch * N, N)]).then_inc(pair_loaded[u], 16)
                    sp.dma_start(wu[:, u, :], wu_in[ds(2 * (j % 4) + u, 1)].rearrange("a p c -> (a p) c"))\
                        .then_inc(wu_loaded[u], 16)
            sp.wait_ge(z_cleared, 16 * 2 * ZPARTS)
            sp.wait_ge(cst_loaded, 64)
            sp.wait_ge(pair_loaded[0], 32 * (NP // 2 + 1))
            sp.wait_ge(pair_loaded[1], 32 * (NP // 2 + 1))
            sp.wait_ge(wu_loaded[0], 16 * (NP // 2))
            sp.wait_ge(wu_loaded[1], 16 * (NP // 2 + 1))

        def pair_fill(kind, half, par, n):
            cols = slice(half * GC, (half + 1) * GC)
            if kind in "qk":
                last = nc.tensor.matmul(G[:, :], wqk[:, par, "qk".index(kind), :], xb[:, par, cols],
                                        start=True, stop=True)
            elif kind == "y":
                last = nc.tensor.matmul(G[:, :], wu[:, par, :], OT[:, cols], start=True, stop=True)
            else:
                for k in range(GT):
                    t = half * GT + k
                    last = nc.tensor.matmul(G[:, k * P:(k + 1) * P], xb[:, par, t * P:(t + 1) * P], wv[:, n, :],
                                            start=True, stop=True)
            last.then_inc(proj_ready, 1)

        @block.tensor
        def _(pe):
            pe.sem_inc(run_turned, ONE)
            pe.sem_inc(summed, ONE)
            pe.wait_ge(pair_loaded[0], 32)
            pe.wait_ge(cst_loaded, 64)
            for n, (kind, half, _) in enumerate(FIRST):
                pe.wait_ge(g_act, g_before(FIRST, n, "act"))
                pe.wait_ge(g_dve, g_before(FIRST, n, "dve"))
                pair_fill(kind, half, 0, 0)
            pe.wait_ge(cst_cast, 2)
            pe.wait_ge(zeroed, 4)
            pe.wait_ge(pt_zeroed, 2)
            nc.tensor.matmul(O[:, :], OT[:, 0:P], OT[:, 0:GC], start=True, stop=True)
            def scores(j, u, i, h):
                s = 2 * BT * j + BT * u + i
                if i == 0 and h == 0:
                    pe.wait_ge(g_act, A_FIRST + (2 * j + u) * A_PAIR)
                    pe.wait_ge(g_dve, D_FIRST + (2 * j + u) * D_PAIR)
                    pe.wait_ge(part_act, (2 * j + u + 1) * 3)
                    pe.wait_ge(part_dve, (2 * j + u + 1) * 3)
                    pe.wait_ge(q_split, (2 * j + u + 1) * 2)
                    pe.wait_ge(k_split, (2 * j + u + 1) * 4)
                if i == GT and h == 0:
                    pe.wait_ge(ot_scaled, 2 * (2 * j + u) + 2)
                pe.wait_ge(exp_ready, EXP0 + 2 * s - 1 + h)
                r = slice(h * HD, (h + 1) * HD)
                for a, b in blocks_of(i):
                    for part in (KH, KL):
                        nc.tensor.matmul(S[h][:, a * P:b * P], Q2[:, u, h, i * P:(i + 1) * P],
                                         part[:, u, h, a * P:b * P], start=part is KH,
                                         stop=part is KL and b != i + 1)
                nc.tensor.matmul(S[h][:, i * P:(i + 1) * P], causal_sel[r, 0, :], causal[r, 0:P],
                                 start=False, stop=False)
                nc.tensor.matmul(S[h][:, i * P + HD:(i + 1) * P], causal_sel[r, 1, :], causal[r, P:],
                                 start=False, stop=True).then_inc(scores_ready, 1)

            def turn(j, u, i, h):
                pi = (i - 1) % BT
                m = len(blocks_of(pi))
                s = 2 * BT * j + BT * u + i
                before = (2 * j + u) * EV_PAIR + ev_count(i - 2)
                pe.wait_ge(exp_ready, EXP0 + 2 * s - 1 + h)
                for r, (a, b) in enumerate(blocks_of(pi)):
                    n = h * m + r
                    done = [(hh, rr) for hh in range(2) for rr in range(m)][:max(n - 1, 0)]
                    pe.wait_ge(pt_dve, ONE + before + sum(hh == 0 for hh, _ in done))
                    pe.wait_ge(pt_act, ONE + before + sum(hh == 1 for hh, _ in done))
                    for k in range(a, b):
                        last = nc.tensor.transpose(TP[n % 2][:, (k - a) * P:(k - a + 1) * P],
                                                   probs[:, h, pi % 2, k * P:(k + 1) * P], ident[:, :])
                    last.then_inc(run_turned, 1)

            def sum_values(j, u, i):
                pi, pu = (i - 2) % BT, (u if i >= 2 else 1 - u)
                pe.wait_ge(pt_dve, ONE + (2 * j + u) * EV_PAIR + ev_count(i - 2))
                pe.wait_ge(pt_act, ONE + (2 * j + u) * EV_PAIR + ev_count(i - 2))
                if pi % GT == 0:
                    pe.wait_ge(o_copied, 2 * (2 * j + u) + 1 + pi // GT)
                for k in range(pi + 1):
                    for h in range(2):
                        last = nc.tensor.matmul(O[OWN[h], (pi % GT) * P:(pi % GT + 1) * P],
                                                V[:, pu, k, h * HD:(h + 1) * HD], PT[:, h, pi % 2, k * P:(k + 1) * P],
                                                start=(k == 0), stop=(k == pi))
                last.then_inc(summed, 1)

            def turn_rinv(pair, half):
                pe.wait_ge(widened, pair + 1)
                for k in range(GT):
                    last = nc.tensor.transpose(S[half][:, (GT + k) * P:(GT + k + 1) * P],
                                               rinv_wide[:, half * GT + k, :, :].rearrange("p h d -> p (h d)"), ident[:, :])
                last.then_inc(rinv_turned, 1)

            with pe.Fori(0, NP // 2) as j:
                for u in range(2):
                    for i in range(BT):
                        scores(j, u, i, 0)
                        kind, half, _ = FILLS[i]
                        if i == 0:
                            pe.wait_ge(pair_loaded[1 - u], 32 * (j + 1) if u == 0 else 32 * (j + 2))
                        pe.wait_ge(g_act, A_FIRST + (2 * j + u) * A_PAIR + g_before(FILLS, i, "act"))
                        pe.wait_ge(g_dve, D_FIRST + (2 * j + u) * D_PAIR + g_before(FILLS, i, "dve"))
                        if kind == "y":
                            pe.wait_ge(ot_scaled, 2 * (2 * j + u) + 1 + half)
                            pe.wait_ge(wu_loaded[1 - u], 16 * (j + 1))
                        n = (2 * (j % 4) + 1 if u == 0 else 2 * ((j + 1) % 4)) if kind == "v" else 0
                        pair_fill(kind, half, 1 - u, n)
                        if i == 2:
                            turn_rinv(2 * j + u, 0)
                        turn(j, u, i, 0)
                        scores(j, u, i, 1)
                        if i == 2:
                            turn_rinv(2 * j + u, 1)
                        turn(j, u, i, 1)
                        sum_values(j, u, i)
            J = NP // 2
            for h in range(2):
                turn(J, 0, 0, h)
            for i in (0, 1):
                sum_values(J, 0, i)
            for half in range(2):
                turn_rinv(NP, half)
            pe.wait_ge(wu_loaded[1], 16 * (J + 1))
            for half in range(2):
                pe.wait_ge(ot_scaled, 2 * NP + 1 + half)
                pe.wait_ge(g_act, A_FIRST + NP * A_PAIR)
                pe.wait_ge(g_dve, D_FIRST + NP * D_PAIR + half)
                pair_fill("y", half, 1, PAIRS - 1)
            for g in range(NG):
                if g >= 4:
                    pe.wait_ge(x_added, g - 3)
                pe.wait_ge(g_dve, D_FIRST + NP * D_PAIR + max(0, g - NG + 3))
                for k in range(GT):
                    bank = S[g % 2][:, (g // 2 % 2) * GC:(g // 2 % 2 + 1) * GC]
                    last = nc.tensor.transpose(bank[:, k * P:(k + 1) * P],
                                               YT[:, (g * GT + k) * P:(g * GT + k + 1) * P], ident[:, :])
                last.then_inc(yt_turned, 1)

        def empty_act(kind, half, par):
            dst = {"q": QT, "k": KT}.get(kind)
            if kind in "qk":
                nc.scalar.activation(dst[:, half * GC:(half + 1) * GC], G[:, :], ACT.Copy,
                                     scale=SCALE_QK if kind == "q" else 1.0).then_inc(g_act, 1)
            else:
                nc.scalar.activation(V[:, par, half * GT:(half + 1) * GT, :],
                                     G[:, :].rearrange("p (t c) -> p t c", t=GT), ACT.Copy).then_inc(g_act, 1)

        @block.scalar
        def _(act):
            act.sem_inc(exp_ready, EXP0)
            act.sem_inc(pt_act, ONE)
            for n, (kind, half, who) in enumerate(FIRST):
                if who == "act":
                    act.wait_ge(proj_ready, n + 1)
                    if n == 0:
                        act.wait_ge(zeroed, 4)
                        act.wait_ge(pt_zeroed, 2)
                    empty_act(kind, half, 0)

            def part(n, par, a_done, d_done):
                act.wait_ge(g_act, a_done)
                if n:
                    act.wait_ge(g_dve, d_done)
                round_part(lambda dst, src: nc.scalar.activation(dst, src, ACT.Copy), n, par, 0)\
                    .then_inc(part_act, 1)

            for n in range(3):
                part(n, 0, copied(FIRST, "q" if n == 0 else "k", "act"), copied(FIRST, "k", "dve"))
            nc.scalar.activation(exp_warm[:, :], ident[:, 0:1], ACT.Exp)

            def copy_runs(j, u, i):
                pi = (i - 1) % BT
                m = len(blocks_of(pi))
                before = 2 * ((2 * j + u) * EV_PAIR + ev_count(i - 2))
                for r, (a, b) in enumerate(blocks_of(pi)):
                    act.wait_ge(run_turned, ONE + before + m + r + 1)
                    if r == 0:
                        act.wait_ge(summed, ONE + 2 * BT * j + BT * u + i)
                    nc.scalar.activation(PT[:, 1, pi % 2, a * P:b * P], TP[(m + r) % 2][:, 0:(b - a) * P],
                                         ACT.Copy).then_inc(pt_act, 1)

            def copy_output(j, u, i):
                pi = (i - 2) % BT
                act.wait_ge(summed, ONE + 2 * BT * j + BT * u + i + 1)
                if i == 5:
                    act.wait_ge(proj_ready, len(FIRST) + (2 * j + u) * BT + 6)
                nc.scalar.activation(OT[:, (pi // GT) * GC:(pi // GT + 1) * GC], O[:, :], ACT.Copy)\
                    .then_inc(o_copied, 1)

            with act.Fori(0, NP // 2) as j:
                for u in range(2):
                    for i in range(BT):
                        s = 2 * BT * j + BT * u + i
                        kind, half, who = FILLS[i]
                        if i == 2 or i == 6:
                            copy_output(j, u, i - 1)
                        for h in range(2):
                            act.wait_ge(max_ready, 2 * s + h + 1)
                            act.wait_ge(run_turned, ONE + 2 * ((2 * j + u) * EV_PAIR + ev_count(i - 2)))
                            w = (i + 1) * P
                            nc.scalar.activation(probs[:, h, i % 2, 0:w], S[h][:, 0:w], ACT.Exp,
                                                 bias=negmax[:, i % 2, h:h + 1],
                                                 accum_out=rowsum[:, u, i, h:h + 1]).then_inc(exp_ready, 1)
                            if h == 0 and who == "act":
                                act.wait_ge(proj_ready, len(FIRST) + (2 * j + u) * BT + i + 1)
                                if kind == "q":
                                    act.wait_ge(q_split, (2 * j + u + 1) * 2)
                                if kind == "k":
                                    act.wait_ge(k_split, (2 * j + u + 1) * 4)
                                    act.wait_ge(part_dve, (2 * j + u + 1) * 3)
                                empty_act(kind, half, 1 - u)
                        if i in PART_ACT:
                            n = PART_ACT.index(i)
                            part(n, 1 - u, A_FIRST + (2 * j + u) * A_PAIR + copied(FILLS, "q" if n == 0 else "k", "act"),
                                 D_FIRST + (2 * j + u) * D_PAIR + copied(FILLS, "k", "dve"))
                        copy_runs(j, u, i)
            J = NP // 2
            copy_runs(J, 0, 0)
            copy_output(J, 0, 1)

        @block.vector
        def _(dve):
            dve.sem_inc(pt_dve, ONE)
            nc.vector.memset(PT[:, :, 0, :], 0.0).then_inc(pt_zeroed, 1)
            nc.vector.memset(rowsum[:, 1, :, :], 1.0).then_inc(pt_zeroed, 1)
            dve.wait_ge(cst_loaded, 64)
            nc.vector.tensor_copy(causal[:, :], causal_f[:, :]).then_inc(cst_cast, 1)
            nc.vector.tensor_copy(causal_sel[:, :, :], causal_sel_f[:, :, :]).then_inc(cst_cast, 1)

            def empty_dve(kind, half, par, j, u):
                if kind == "y":
                    b = ((j + 15) // 4) % 4 if u == 0 else j // 4
                    ys = YT[:, ds(b * N + half * GC, GC)]
                    nc.vector.tensor_tensor(ys, G[:, :], ys, ALU.add).then_inc(g_dve, 1)
                elif kind == "k":
                    nc.vector.tensor_copy(KT[:, half * GC:(half + 1) * GC], G[:, :]).then_inc(g_dve, 1)
                else:
                    nc.vector.tensor_copy(V[:, par, half * GT:(half + 1) * GT, :],
                                          G[:, :].rearrange("p (t c) -> p t c", t=GT)).then_inc(g_dve, 1)

            for n, (kind, half, who) in enumerate(FIRST):
                if who == "dve":
                    dve.wait_ge(proj_ready, n + 1)
                    if n < 4:
                        dve.wait_ge(zeroed, 4)
                        dve.wait_ge(pt_zeroed, 2)
                    empty_dve(kind, half, 0, 0, 0)
            def part(n, par, a_done, d_done):
                dve.wait_ge(g_act, a_done)
                if n:
                    dve.wait_ge(g_dve, d_done)
                round_part(nc.vector.tensor_copy, n, par, 1).then_inc(part_dve, 1)

            for n in range(3):
                part(n, 0, copied(FIRST, "q" if n == 0 else "k", "act"), copied(FIRST, "k", "dve"))
            dve.wait_ge(bias_added, 1)

            def copy_runs(j, u, i):
                pi = (i - 1) % BT
                before = 2 * ((2 * j + u) * EV_PAIR + ev_count(i - 2))
                for r, (a, b) in enumerate(blocks_of(pi)):
                    dve.wait_ge(run_turned, ONE + before + r + 1)
                    if r == 0:
                        dve.wait_ge(summed, ONE + 2 * BT * j + BT * u + i)
                    nc.vector.tensor_copy(PT[:, 0, pi % 2, a * P:b * P], TP[r % 2][:, 0:(b - a) * P])\
                        .then_inc(pt_dve, 1)

            def scale_output(pair, half):
                dve.wait_ge(rinv_turned, 2 * pair + half + 1)
                dve.wait_ge(o_copied, 2 * pair + 1)
                cols = slice(half * GC, (half + 1) * GC)
                nc.vector.tensor_tensor(OT[:, cols], S[half][:, GC:], OT[:, cols], ALU.mult).then_inc(ot_scaled, 1)

            def invert_sums(pair, par, exps):
                dve.wait_ge(exp_ready, exps)
                nc.vector.reciprocal(rinv[:, :, :], rowsum[:, par, :, :]).then_inc(rinv_ready, 1)

            with dve.Fori(0, NP // 2) as j:
                for u in range(2):
                    for i in range(BT):
                        s = 2 * BT * j + BT * u + i
                        kind, half, who = FILLS[i]
                        for h in range(2):
                            dve.wait_ge(scores_ready, 2 * s + h + 1)
                            if h == 0:
                                dve.wait_ge(exp_ready, EXP0 + 2 * s - 1)
                            nc.vector.tensor_reduce(out=negmax[:, i % 2, h:h + 1], in_=S[h][:, 0:(i + 1) * P],
                                                    op=ALU.max, axis=AX.X, negate=True).then_inc(max_ready, 1)
                            if h == 0:
                                copy_runs(j, u, i)
                            if h == 0 and who == "dve":
                                dve.wait_ge(proj_ready, len(FIRST) + (2 * j + u) * BT + i + 1)
                                if kind == "k":
                                    dve.wait_ge(k_split, (2 * j + u + 1) * 4)
                                    dve.wait_ge(part_act, (2 * j + u + 1) * 3)
                                if kind == "y":
                                    dve.wait_ge(g_dve, D_FIRST + (2 * j + u) * D_PAIR + g_before(FILLS, i, "dve"))
                                empty_dve(kind, half, 1 - u, j, u)
                        if i == 0:
                            invert_sums(2 * j + u, 1 - u, EXP0 + 2 * s)
                        if i == 2:
                            scale_output(2 * j + u, 0)
                            scale_output(2 * j + u, 1)
                        if i in PART_DVE:
                            n = PART_DVE.index(i)
                            part(n, 1 - u, A_FIRST + (2 * j + u) * A_PAIR + copied(FILLS, "q" if n == 0 else "k", "act"),
                                 D_FIRST + (2 * j + u) * D_PAIR + copied(FILLS, "k", "dve"))
            J = NP // 2
            copy_runs(J, 0, 0)
            invert_sums(NP, 1, EXP0 + 2 * BT * NP)
            for half in range(2):
                scale_output(NP, half)
            for half in range(2):
                dve.wait_ge(proj_ready, len(FIRST) + NP * BT + half + 1)
                dve.wait_ge(g_dve, D_FIRST + NP * D_PAIR + half)
                ys = YT[:, (B - 1) * N + half * GC:(B - 1) * N + (half + 1) * GC]
                nc.vector.tensor_tensor(ys, G[:, :], ys, ALU.add).then_inc(g_dve, 1)
            for g in range(NG):
                dve.wait_ge(yt_turned, g + 1)
                bank = S[g % 2][:, (g // 2 % 2) * GC:(g // 2 % 2 + 1) * GC]
                xs = X[:, g * GT:(g + 1) * GT, :]
                nc.vector.tensor_tensor(xs, bank.rearrange("p (t c) -> p t c", t=GT), xs, ALU.add).then_inc(x_added, 1)

        @block.gpsimd
        def _(pool):
            nc.gpsimd.memset(probs[:, :, 1, :], 0.0).then_inc(zeroed, 1)
            nc.gpsimd.memset(V[:, 1, :, :], 0.0).then_inc(zeroed, 1)
            nc.gpsimd.memset(OT[:, :], 0.0).then_inc(zeroed, 1)
            nc.gpsimd.memset(YT[:, :], 0.0).then_inc(zeroed, 1)
            nc.gpsimd.memset(zero_tile[:, :], 0.0).then_inc(zeroed, 1)
            pool.wait_ge(cst_loaded, 64)
            nc.gpsimd.tensor_tensor(X[:, :, :], X[:, :, :], bu[:, :].unsqueeze(1).to_broadcast([P, NT, C]), ALU.add)\
                .then_inc(bias_added, 1)

            def split(par, p):
                for h in range(2):
                    pool.wait_ge(part_act if h == 0 else part_dve, 3 * p + 1)
                    pool.nop(nofuse=True)
                    nc.gpsimd.tensor_tensor(Q2[OTHER[h], par, h, :], QT[OWN[h], :], Q2[OWN[h], par, h, :].bitcast(F32),
                                            ALU.subtract).then_inc(q_split, 1)
                    pool.wait_ge(q_split, 2 * p + h + 1)
                for h in range(2):
                    pool.wait_ge(part_act if h == 0 else part_dve, 3 * p + 2)
                    for n, rows in enumerate((OWN[h], OTHER[h])):
                        pool.nop(nofuse=True)
                        nc.gpsimd.tensor_tensor(KL[rows, par, h, :], KT[OWN[h], :], KH[OWN[h], par, h, :].bitcast(F32),
                                                ALU.subtract).then_inc(k_split, 1)
                        pool.wait_ge(k_split, 4 * p + 2 * h + n + 1)

            def widen(pair):
                pool.wait_ge(rinv_ready, pair + 1)
                pool.nop(nofuse=True)
                nc.gpsimd.tensor_copy(rinv_wide[:, :, :, :], rinv[:, :, :].unsqueeze(3).to_broadcast([P, BT, 2, HD]))\
                    .then_inc(widened, 1)
                pool.wait_ge(widened, pair + 1)

            pool.wait_ge(bias_added, 1)
            split(0, 0)
            with pool.Fori(0, NP // 2) as j:
                for u in range(2):
                    widen(2 * j + u)
                    split(1 - u, 2 * j + u + 1)
            widen(NP)


def experts(nc, X, XT, mean_var, rstd, shift, ident, rw_in, eb_in, w1_in, w2_in, sw1_in, sw2_in,
            keyrow_in, offs_in, table, zbuf, layer):
    tag = f"f{layer}"
    layernorm(nc, X, mean_var, rstd, shift, tag)
    ctx = ExitStack()
    with ctx:
        shared_out = ctx.enter_context(nc.sbuf_tensor(f"shared_out_{tag}", [P, NT, C], F32))
        gather_idx = ctx.enter_context(nc.sbuf_tensor(f"gather_idx_{tag}", [P, HE], I32))
        scatter_idx = ctx.enter_context(nc.sbuf_tensor(f"scatter_idx_{tag}", [P, HE], I32))
        router(nc, X, XT, rstd, shift, ident, rw_in, eb_in, keyrow_in, offs_in, table,
               gather_idx, scatter_idx, tag)
        routed(nc, XT, ident, w1_in, w2_in, sw1_in, sw2_in, table, zbuf[layer], gather_idx, scatter_idx,
               shared_out, tag)
        combine(nc, X, zbuf[layer], shared_out, tag)


def router(nc, X, XT, rstd, shift, ident, rw_in, eb_in, keyrow_in, offs_in, table,
           gather_idx, scatter_idx, tag):
    ctx = ExitStack()
    with ctx:
        def sb(name, shape, dt=F32):
            return ctx.enter_context(nc.sbuf_tensor(f"{name}_{tag}", shape, dt))

        def pb(name, shape, dt=F32):
            return ctx.enter_context(nc.psum_tensor(f"{name}_{tag}", shape, dt))

        def sem(name):
            return ctx.enter_context(nc.semaphore(f"{name}_{tag}"))

        rw = sb("rw", [P, E])
        eb = sb("eb", [P, E])
        keyrow = sb("keyrow", [P, T // 2])
        offs = sb("offs", [P, HE + 1])
        ident_bf = sb("ident_bf", [P, P], BF16)
        xn = sb("xn", [P, 2, GT, C])
        xg = sb("xg", [P, GC])
        scores = sb("scores", [P, GT, E])
        biased = sb("biased", [P, GT, E])
        top8 = sb("top8", [P, GT, 8])
        marked = sb("marked", [P, GT, E])
        mask = sb("mask", [P, GT, E], BF16)
        chosen = sb("chosen", [P, GT, E])
        total = sb("total", [P, GT])
        weights = sb("weights", [P, GT, E])
        keys = sb("keys", [P, T // 2])
        first = sb("first", [P, CAP])
        both = sb("both", [E, 2 * CAP])
        merged = sb("merged", [E, CAP])
        spread = sb("spread", [HE, P])
        slot_key = sb("slot_key", [P, HE])
        slot_tok = sb("slot_tok", [P, HE])
        spare = sb("spare", [P, HE])
        spare2 = sb("spare2", [P, HE])
        table_warm = sb("table_warm", [P, 1])

        tp = pb("tp", [P, GC])
        lg = pb("lg", [P, GC])
        mt = pb("mt", [P, GC], BF16)
        st = pb("st", [P, GC])

        loaded = sem("loaded")
        cast = sem("cast")
        normed = sem("normed")
        turned = sem("turned")
        xt_copied = sem("xt_copied")
        logits = sem("logits")
        scored = sem("scored")
        step = sem("step")
        mask_ready = sem("mask_ready")
        mask_turned = sem("mask_turned")
        keys_ready = sem("keys_ready")
        written = [sem(f"written{u}") for u in range(2)]
        fstep = sem("fstep")
        spread_ready = sem("spread_ready")
        spread_turned = sem("spread_turned")
        block = ctx.enter_context(nc.Block())
        tab = table.rearrange("(t p) w -> p t w", p=P)

        @block.sync
        def _(sp):
            sp.dma_start(rw[:, :], rw_in).then_inc(loaded, 16)
            sp.dma_start(eb[:, :], eb_in).then_inc(loaded, 16)
            for h in range(2):
                sp.dma_start(keyrow[h * E:(h + 1) * E, :], keyrow_in[:, h * T // 2:(h + 1) * T // 2]).then_inc(loaded, 16)
            sp.dma_start(offs[:, :], offs_in).then_inc(loaded, 16)
            for u in range(2):
                sp.sem_inc(written[u], 1)
            with sp.Fori(0, NG // 2) as j:
                for u in range(2):
                    g = 2 * j + u
                    sp.wait_ge(normed, (g + 1) * GT)
                    sp.dma_start(tab[:, ds(g * GT, GT), 0:C], xn[:, u, :, :]).then_inc(written[u], 16)
                    sp.wait_ge(mask_ready, 2 * g + 3)
                    sp.dma_start(tab[:, ds(g * GT, GT), C:], weights[:, :, :]).then_inc(written[u], 16)
            for u in range(2):
                sp.wait_ge(written[u], 32 * (NG // 2) + 1)

        @block.tensor
        def _(pe):
            pe.sem_inc(turned, 1)
            pe.sem_inc(mask_turned, 1)
            pe.wait_ge(loaded, 80)
            pe.wait_ge(cast, 1)
            for half in range(2):
                with pe.Fori(half * NG // 4, (half + 1) * NG // 4) as j:
                    for u in range(2):
                        g = 2 * j + u
                        pe.wait_ge(normed, (g + 1) * GT)
                        for k in range(GT):
                            last = nc.tensor.transpose(tp[:, k * P:(k + 1) * P], xn[:, u, k, :], ident[:, :])
                        last.then_inc(turned, 1)
                        pe.wait_ge(xt_copied, 2 * (g + 1))
                        for k in range(GT):
                            last = nc.tensor.matmul(lg[:, k * E:(k + 1) * E], xg[:, k * P:(k + 1) * P], rw[:, :],
                                                    start=True, stop=True)
                        last.then_inc(logits, 1)
                        pe.wait_ge(mask_ready, 2 * g + 2)
                        pe.nop(nofuse=True)
                        for k in range(GT):
                            last = nc.tensor.transpose(mt[half * E:(half + 1) * E, k * P:(k + 1) * P],
                                                       mask[:, k, :], ident_bf[:, :])
                        last.then_inc(mask_turned, 1)
            pe.wait_ge(spread_ready, 1)
            nc.tensor.transpose(st[:, 0:HE], spread[:, :], ident[0:HE, 0:HE]).then_inc(spread_turned, 1)

        @block.scalar
        def _(act):
            nc.scalar.activation(table_warm[:, :], ident[:, 0:1], ACT.Sigmoid)
            with act.Fori(0, NG) as g:
                act.wait_ge(turned, g + 2)
                nc.scalar.activation(xg[:, :], tp[:, :], ACT.Copy).then_inc(xt_copied, 1)
                nc.scalar.activation(XT[:, ds(g * GC, GC)], tp[:, :], ACT.Copy).then_inc(xt_copied, 1)
                act.wait_ge(logits, g + 1)
                act.wait_ge(mask_ready, 2 * g + 1)
                nc.scalar.activation(scores[:, :, :], lg[:, 0:GT * E].rearrange("p (k e) -> p k e", k=GT),
                                     ACT.Sigmoid).then_inc(scored, 1)

        @block.vector
        def _(dve):
            dve.sem_inc(mask_ready, 1)
            nc.vector.tensor_copy(ident_bf[:, :], ident[:, :]).then_inc(cast, 1)
            dve.wait_ge(loaded, 80)
            per = 2 * GT + 6

            def normalise(g, u, j):
                for k in range(GT):
                    t = g * GT + k
                    nc.vector.tensor_scalar(xn[:, u, k, :], X[:, t, :], rstd[:, ds(t, 1)], shift[:, ds(t, 1)],
                                            ALU.mult, ALU.add).then_inc(normed, 1)

            normalise(0, 0, 0)
            for half in range(2):
                with dve.Fori(half * NG // 4, (half + 1) * NG // 4) as j:
                    for u in range(2):
                        g = 2 * j + u
                        if u == 0:
                            dve.wait_ge(turned, g + 1)
                            dve.wait_ge(written[1], 32 * j + 1)
                            normalise(g + 1, 1, j)
                        else:
                            dve.wait_ge(turned, g + 1)
                            dve.wait_ge(written[0], 32 * j + 33)
                            normalise((g + 1) % NG, 0, j)
                        dve.wait_ge(scored, g + 1)
                        nc.vector.tensor_tensor(biased[:, :, :], scores[:, :, :],
                                                eb[:, :].unsqueeze(1).to_broadcast([P, GT, E]), ALU.add).then_inc(step, 1)
                        dve.wait_ge(step, g * per + 1)
                        dve.nop(nofuse=True)
                        for k in range(GT):
                            nc.vector.max(top8[:, k, :], biased[:, k, :]).then_inc(step, 1)
                        dve.wait_ge(step, g * per + 1 + GT)
                        nc.vector.memset(top8[:, :, K:], EMPTY).then_inc(step, 1)
                        dve.wait_ge(step, g * per + 2 + GT)
                        dve.nop(nofuse=True)
                        for k in range(GT):
                            nc.vector.match_replace(marked[:, k, :], top8[:, k, :], biased[:, k, :], 2 * EMPTY / 3).then_inc(step, 1)
                        dve.wait_ge(step, g * per + 2 + 2 * GT)
                        dve.wait_ge(mask_turned, g + 1)
                        nc.vector.tensor_tensor(mask[:, :, :], marked[:, :, :], biased[:, :, :], ALU.not_equal)\
                            .then_inc(mask_ready, 1)
                        dve.wait_ge(mask_ready, 2 * g + 2)
                        nc.vector.tensor_tensor(chosen[:, :, :], mask[:, :, :], scores[:, :, :], ALU.mult).then_inc(step, 1)
                        dve.wait_ge(step, g * per + 3 + 2 * GT)
                        nc.vector.tensor_reduce(out=total[:, :], in_=chosen[:, :, :], op=ALU.add, axis=AX.X).then_inc(step, 1)
                        dve.wait_ge(step, g * per + 4 + 2 * GT)
                        nc.vector.tensor_scalar(total[:, :], total[:, :], 1e-20, None, ALU.add).then_inc(step, 1)
                        dve.wait_ge(step, g * per + 5 + 2 * GT)
                        nc.vector.reciprocal(total[:, :], total[:, :]).then_inc(step, 1)
                        dve.wait_ge(step, g * per + 6 + 2 * GT)
                        nc.vector.tensor_tensor(weights[:, :, :], chosen[:, :, :],
                                                total[:, :].unsqueeze(2).to_broadcast([P, GT, E]), ALU.mult)\
                            .then_inc(mask_ready, 1)
                        dve.wait_ge(mask_turned, g + 2)
                        r = slice(half * E, (half + 1) * E)
                        cols = ds((g - half * NG // 2) * GC, GC)
                        nc.vector.tensor_tensor(keys[r, cols], mt[r, :], keyrow[r, cols], ALU.mult).then_inc(keys_ready, 1)
            dve.wait_ge(keys_ready, NG)
            n = 0

            def link(ins):
                nonlocal n
                ins.then_inc(fstep, 1)
                n += 1
                dve.wait_ge(fstep, n)

            for r in range(CAP // 8):
                link(nc.vector.max(first[:, r * 8:(r + 1) * 8], keys[:, :]))
                link(nc.vector.match_replace(keys[:, :], first[:, r * 8:(r + 1) * 8], keys[:, :], -1.0))
            link(nc.vector.tensor_copy(both[:, 0:CAP], first[0:E, :]))
            link(nc.vector.tensor_copy(both[:, CAP:], first[E:, :]))
            for r in range(CAP // 8):
                link(nc.vector.max(merged[:, r * 8:(r + 1) * 8], both[:, :]))
                link(nc.vector.match_replace(both[:, :], merged[:, r * 8:(r + 1) * 8], both[:, :], -1.0))
            link(nc.vector.memset(spread[:, :], 0.0))
            link(nc.vector.tensor_copy(spread[:, 0:CAP], merged[0:HE, :]))
            nc.vector.tensor_copy(spread[:, HD:HD + CAP], merged[HE:, :]).then_inc(spread_ready, 1)
            dve.wait_ge(spread_turned, 1)
            link(nc.vector.tensor_copy(slot_key[:, :], st[:, 0:HE]))
            link(nc.vector.tensor_scalar(slot_tok[:, :], slot_key[:, :], -1.0, float(T), ALU.mult, ALU.add))
            link(nc.vector.tensor_scalar(gather_idx[:, :], slot_tok[:, :], float(T - 1), None, ALU.min))
            link(nc.vector.tensor_scalar(spare[:, :], slot_key[:, :], 0.0, offs[:, HE:], ALU.is_equal, ALU.mult))
            link(nc.vector.tensor_tensor(spare2[:, :], spare[:, :], offs[:, 0:HE], ALU.add))
            link(nc.vector.tensor_tensor(scatter_idx[:, :], spare2[:, :], slot_tok[:, :], ALU.add))


def routed(nc, XT, ident, w1_in, w2_in, sw1_in, sw2_in, table, zb, gather_idx, scatter_idx, shared_out, tag):
    ctx = ExitStack()
    with ctx:
        def sb(name, shape, dt=F32):
            return ctx.enter_context(nc.sbuf_tensor(f"{name}_{tag}", shape, dt))

        def pb(name, shape, dt=F32):
            return ctx.enter_context(nc.psum_tensor(f"{name}_{tag}", shape, dt))

        def sem(name):
            return ctx.enter_context(nc.semaphore(f"{name}_{tag}"))

        R = 4
        w1 = sb("w1", [P, R, P])
        w2 = sb("w2", [P, R, P])
        sw1 = sb("sw1", [P, SF])
        sw2 = sb("sw2", [P, 2, C])
        gi = [sb(f"gi{u}", [P, 1], I32) for u in range(R)]
        si = [sb(f"si{u}", [P, 1], I32) for u in range(R)]
        rows = [sb(f"rows{u}", [P, TW]) for u in range(R)]
        xs = sb("xs", [P, 2, P])
        hid = sb("hid", [P, 2, HD])
        ys = [sb(f"ys{u}", [P, C]) for u in range(2)]
        hidden = sb("hidden", [P, 2, 2 * P])
        table_warm = sb("table_warm2", [P, 1])
        tg = [pb(f"tg{u}", [P, P]) for u in range(2)]
        hq = [pb(f"hq{u}", [P, HD]) for u in range(2)]
        yq = [pb(f"yq{u}", [P, C]) for u in range(2)]
        hp = pb("hp", [P, 2, 2 * P])
        sp_out = pb("sp_out", [P, 2, C])

        w_loaded = [sem(f"w_loaded{u}") for u in range(R)]
        sw_loaded = sem("sw_loaded")
        idx_ready = sem("idx_ready")
        gathered = [sem(f"gathered{u}") for u in range(R)]
        scattered = sem("scattered")
        rows_turned = sem("rows_turned")
        xs_copied = sem("xs_copied")
        h_ready = sem("hid_ready")
        gelu_ready = sem("hgelu_ready")
        y_ready = sem("y_ready")
        y_scaled = sem("y_scaled")
        sh_ready = sem("sh_ready")
        sh_gelu = sem("sh_gelu")
        s_ready = sem("s_ready")
        s_copied = sem("s_copied")
        block = ctx.enter_context(nc.Block())
        J = HE // R
        AHEAD = R - 1

        @block.sync
        def _(sp):
            sp.dma_start(sw1[:, :], sw1_in).then_inc(sw_loaded, 16)
            sp.dma_start(sw2[:, :, :], sw2_in.rearrange("(k p) c -> p k c", p=P)).then_inc(sw_loaded, 16)
            with sp.Fori(0, J) as j:
                for u in range(R):
                    m = R * j + u
                    if u == 0:
                        sp.wait_ge(y_ready, m + 1)
                    sp.dma_start(w1[:, u, :], w1_in[ds(m, 1)].rearrange("a p c -> (a p) c")).then_inc(w_loaded[u], 16)
                    sp.dma_start(w2[:, u, :], w2_in[ds(m, 1)].rearrange("a p c -> (a p) c")).then_inc(w_loaded[u], 16)
            sp.wait_ge(sw_loaded, 32)

        @block.gpsimd
        def _(pool):
            def gather(m, u, done):
                nc.gpsimd.tensor_copy(gi[u][:, :], gather_idx[:, ds(m, 1)]).then_inc(idx_ready, 1)
                pool.wait_ge(idx_ready, done)
                pool.nop(nofuse=True)
                nc.gpsimd.indirect_dma_start(out=rows[u][:, :], out_offset=None, in_=table,
                                             in_offset=bass.IndirectOffsetOnAxis(ap=gi[u][:, 0:1], axis=0))\
                    .then_inc(gathered[u], 16)

            for m in range(AHEAD):
                gather(m, m, m + 1)
            with pool.Fori(0, J) as j:
                for u in range(R):
                    m = R * j + u
                    nc.gpsimd.tensor_copy(si[u][:, :], scatter_idx[:, ds(m, 1)]).then_inc(idx_ready, 1)
                    pool.wait_ge(y_scaled, 2 * m + 1)
                    gather((m + AHEAD) % HE, (u + AHEAD) % R, 2 * m + AHEAD + 2)
                    if u:
                        pool.wait_ge(scattered, 16 * m)
                    pool.wait_ge(y_scaled, 2 * m + 3)
                    pool.nop(nofuse=True)
                    nc.gpsimd.indirect_dma_start(out=zb, out_offset=bass.IndirectOffsetOnAxis(ap=si[u][:, 0:1], axis=0),
                                                 in_=ys[u % 2][:, :], in_offset=None, compute_op=ALU.add)\
                        .then_inc(scattered, 16)
                pool.wait_ge(scattered, 16 * R * (j + 1))
            pool.wait_ge(scattered, 16 * HE)
            for u in range(AHEAD):
                pool.wait_ge(gathered[u], 16 * (J + 1))

        @block.tensor
        def _(pe):
            def turn(u, at, n):
                pe.wait_ge(gathered[u], n)
                nc.tensor.transpose(tg[at][:, :], rows[u][:, 0:C], ident[:, :]).then_inc(rows_turned, 1)

            pe.sem_inc(y_ready, 1)
            turn(0, 0, 16)
            pe.wait_ge(sw_loaded, 32)
            with pe.Fori(0, J) as j:
                for u in range(R):
                    m = R * j + u
                    b = u % 2
                    turn((u + 1) % R, 1 - b, 16 * (j + 1) if u + 1 < R else 16 * (j + 2))
                    pe.wait_ge(xs_copied, m + 1)
                    pe.wait_ge(w_loaded[u], 32 * (j + 1))
                    for h in range(2):
                        last = nc.tensor.matmul(hq[b][h * HD:(h + 1) * HD, :], w1[:, u, h * HD:(h + 1) * HD],
                                                xs[:, b, h * HD:(h + 1) * HD], start=True, stop=True)
                    last.then_inc(h_ready, 1)
                    if b == 0:
                        for c in range(2):
                            last = nc.tensor.matmul(hp[:, c, :], sw1[:, c * P:(c + 1) * P],
                                                    XT[:, ds(m * P, 2 * P)], start=True, stop=True)
                        last.then_inc(sh_ready, 1)
                    else:
                        n = (R // 2) * j + u // 2
                        pe.wait_ge(sh_gelu, n + 1)
                        pe.wait_ge(s_copied, n + 1)
                        for k in range(2):
                            for c in range(2):
                                last = nc.tensor.matmul(sp_out[:, k, :], hidden[:, c, k * P:(k + 1) * P],
                                                        sw2[:, c, :], start=(c == 0), stop=(c == 1))
                        last.then_inc(s_ready, 1)
                    pe.wait_ge(gelu_ready, m + 1)
                    pe.nop(nofuse=True)
                    for h in range(2):
                        r = slice(h * HD, (h + 1) * HD)
                        last = nc.tensor.matmul(yq[b][r, :], hid[r, b, :], w2[r, u, :], start=True, stop=True)
                    last.then_inc(y_ready, 1)

        @block.scalar
        def _(act):
            act.sem_inc(s_copied, 1)
            nc.scalar.activation(table_warm[:, :], ident[:, 0:1], ACT.Gelu_apprx_tanh)
            with act.Fori(0, J) as j:
                for u in range(R):
                    m = R * j + u
                    b = u % 2
                    act.wait_ge(h_ready, m + 1)
                    nc.scalar.activation(hid[:, b, :], hq[b][:, :], ACT.Gelu_apprx_tanh).then_inc(gelu_ready, 1)
                    n = (R // 2) * j + u // 2
                    if b == 0:
                        act.wait_ge(sh_ready, n + 1)
                        nc.scalar.activation(hidden[:, :, :], hp[:, :, :], ACT.Gelu_apprx_tanh).then_inc(sh_gelu, 1)
                    else:
                        act.wait_ge(s_ready, n + 1)
                        nc.scalar.activation(shared_out[:, ds(2 * n, 2), :], sp_out[:, :, :], ACT.Copy)\
                            .then_inc(s_copied, 1)

        @block.vector
        def _(dve):
            dve.sem_inc(y_scaled, 1)

            def copy_xs(m, b):
                dve.wait_ge(rows_turned, m + 1)
                nc.vector.tensor_copy(xs[:, b, :], tg[b][:, :]).then_inc(xs_copied, 1)

            copy_xs(0, 0)
            with dve.Fori(0, J) as j:
                for u in range(R):
                    m = R * j + u
                    b = u % 2
                    copy_xs(m + 1, 1 - b)
                    dve.wait_ge(y_ready, m + 2)
                    dve.wait_ge(idx_ready, 2 * m + AHEAD + 1)
                    for h in range(2):
                        r = slice(h * HD, (h + 1) * HD)
                        nc.vector.tensor_scalar(ys[b][r, :], yq[b][r, :], rows[u][r, ds(C + h * HE + m, 1)], None,
                                                ALU.mult).then_inc(y_scaled, 1)


def combine(nc, X, zb, shared_out, tag):
    ctx = ExitStack()
    with ctx:
        z = [ctx.enter_context(nc.sbuf_tensor(f"z{h}_{tag}", [P, NT, C], F32)) for h in range(2)]
        z_loaded = [ctx.enter_context(nc.semaphore(f"z_loaded{c}_{tag}")) for c in range(B)]
        added = ctx.enter_context(nc.semaphore(f"added_{tag}"))
        block = ctx.enter_context(nc.Block())

        @block.sync
        def _(sp):
            for c in range(B):
                for h in range(2):
                    src = zb[h * ZR:h * ZR + T, :].rearrange("(t p) c -> p t c", p=P)
                    ts = slice(c * BT, (c + 1) * BT)
                    sp.dma_start(z[h][:, ts, :], src[:, ts, :]).then_inc(z_loaded[c], 16)

        @block.vector
        def _(dve):
            nc.vector.tensor_tensor(X[:, :, :], X[:, :, :], shared_out[:, :, :], ALU.add).then_inc(added, 1)
            n = 1
            for c in range(B):
                ts = slice(c * BT, (c + 1) * BT)
                dve.wait_ge(z_loaded[c], 32)
                for h in range(2):
                    dve.wait_ge(added, n)
                    nc.vector.tensor_tensor(X[:, ts, :], X[:, ts, :], z[h][:, ts, :], ALU.add).then_inc(added, 1)
                    n += 1


def attention_b(nc, X, mean_var, rstd, shift, ident, wq_in, wkv_in, wp_in, bp_in, headmask_in):
    layernorm(nc, X, mean_var, rstd, shift, "b")
    ctx = ExitStack()
    with ctx:
        def sb(name, shape, dt=F32):
            return ctx.enter_context(nc.sbuf_tensor(f"{name}_b", shape, dt))

        def pb(name, shape, dt=F32):
            return ctx.enter_context(nc.psum_tensor(f"{name}_b", shape, dt))

        def sem(name):
            return ctx.enter_context(nc.semaphore(f"{name}_b"))

        wq = sb("wq", [P, C])
        wkv = sb("wkv", [P, 2 * C])
        wp = sb("wp", [P, C])
        bp = sb("bp", [P, C])
        headmask = sb("headmask", [P, C])
        xn = sb("xn", [P, BT, C])
        xb = sb("xb", [P, N])
        kk = sb("kk", [P, BT, C])
        vv = sb("vv", [P, BT, C + 1])
        qT = sb("qT", [P, N])
        W = C + HB
        kv = sb("kv", [P, W])
        ksum = sb("ksum", [P, 1])
        z = sb("z", [P, BT, HB])
        o = sb("o", [P, BT, C])
        oT = sb("oT", [P, N])
        tp = [pb(f"tp{u}", [P, GC]) for u in range(2)]
        pj = [pb(f"pj{u}", [P, GC]) for u in range(2)]
        kvp = pb("kvp", [P, GC])
        op = [pb(f"op{u}", [P, 2, 2 * C]) for u in range(2)]

        loaded = sem("loaded")
        ones_set = sem("ones_set")
        normed = sem("normed")
        turned = sem("turned")
        t_copied = sem("t_copied")
        pj_ready = sem("pj_ready")
        pj_act = sem("pj_act")
        pj_dve = sem("pj_dve")
        kv_ready = sem("kv_ready")
        kstep = sem("kstep")
        op_ready = sem("op_ready")
        o_ready = sem("o_ready")
        zstep = sem("zstep")
        biased = sem("biased")
        block = ctx.enter_context(nc.Block())

        @block.sync
        def _(sp):
            for dst, src in ((wq, wq_in), (wkv, wkv_in), (wp, wp_in), (bp, bp_in), (headmask, headmask_in)):
                sp.dma_start(dst[:, :], src).then_inc(loaded, 16)

        @block.gpsimd
        def _(pool):
            nc.gpsimd.memset(vv[:, :, C:], 1.0).then_inc(ones_set, 1)
            pool.wait_ge(loaded, 80)
            with pool.Fori(0, B) as b:
                pool.wait_ge(normed, (b + 1) * BT)
                xs = X[:, ds(b * BT, BT), :]
                nc.gpsimd.tensor_tensor(xs, xs, bp[:, :].unsqueeze(1).to_broadcast([P, BT, C]), ALU.add)\
                    .then_inc(biased, 1)

        @block.tensor
        def _(pe):
            pe.wait_ge(loaded, 80)
            pe.wait_ge(ones_set, 1)
            with pe.Fori(0, B) as b:
                for h in range(2):
                    pe.wait_ge(normed, b * BT + (h + 1) * GT)
                    for k in range(GT):
                        last = nc.tensor.transpose(tp[h][:, k * P:(k + 1) * P], xn[:, h * GT + k, :], ident[:, :])
                    last.then_inc(turned, 1)
                pe.wait_ge(t_copied, 4 * b + 2)
                for n in range(4):
                    if n >= 2:
                        pe.wait_ge(pj_act, 6 * b + n - 1)
                        pe.wait_ge(pj_dve, 6 * b + n)
                    elif n == 0:
                        pe.wait_ge(pj_dve, 6 * b + 1)
                    for k in range(2):
                        t = 2 * n + k
                        last = nc.tensor.matmul(pj[n % 2][:, k * 2 * C:(k + 1) * 2 * C], xb[:, t * P:(t + 1) * P],
                                                wkv[:, :], start=True, stop=True)
                    last.then_inc(pj_ready, 1)
                for n in range(2):
                    pe.wait_ge(pj_act, 6 * b + n + 3)
                    pe.wait_ge(pj_dve, 6 * b + n + 4)
                    nc.tensor.matmul(pj[n][:, :], wq[:, :], xb[:, n * GC:(n + 1) * GC], start=True, stop=True)\
                        .then_inc(pj_ready, 1)
                for t in range(BT):
                    last = nc.tensor.matmul(kvp[:, 0:C + 1], kk[:, t, :], vv[:, t, :], start=(t == 0), stop=(t == BT - 1))
                last.then_inc(kv_ready, 1)
                pe.wait_ge(pj_act, 6 * b + 6)
                pe.wait_ge(kstep, 3 * b + 3)
                for n in range(4):
                    if n >= 2:
                        pe.wait_ge(o_ready, 4 * b + n - 1)
                    for k in range(2):
                        t = 2 * n + k
                        last = nc.tensor.matmul(op[n % 2][:, k, 0:W], qT[:, t * P:(t + 1) * P], kv[:, :],
                                                start=True, stop=True)
                    last.then_inc(op_ready, 1)
                for h in range(2):
                    pe.wait_ge(o_ready, 4 * b + 2 * h + 2)
                    for k in range(GT):
                        last = nc.tensor.transpose(tp[h][:, k * P:(k + 1) * P], o[:, h * GT + k, :], ident[:, :])
                    last.then_inc(turned, 1)
                for h in range(2):
                    pe.wait_ge(t_copied, 4 * b + 3 + h)
                    for k in range(GT):
                        t = h * GT + k
                        last = nc.tensor.matmul(pj[h][:, k * P:(k + 1) * P], oT[:, t * P:(t + 1) * P], wp[:, :],
                                                start=True, stop=True)
                    last.then_inc(pj_ready, 1)

        @block.scalar
        def _(act):
            with act.Fori(0, B) as b:
                for h in range(2):
                    act.wait_ge(turned, 4 * b + h + 1)
                    nc.scalar.activation(xb[:, h * GC:(h + 1) * GC], tp[h][:, :], ACT.Copy).then_inc(t_copied, 1)
                for n in range(4):
                    act.wait_ge(pj_dve, 6 * b + n + 2)
                    nc.scalar.activation(kk[:, 2 * n:2 * n + 2, :],
                                         pj[n % 2][:, :].rearrange("p (k s c) -> p k s c", k=2, s=2)[:, :, 0, :],
                                         ACT.Relu).then_inc(pj_act, 1)
                for n in range(2):
                    act.wait_ge(pj_ready, 8 * b + 5 + n)
                    nc.scalar.activation(qT[:, n * GC:(n + 1) * GC], pj[n][:, :], ACT.Relu).then_inc(pj_act, 1)
                for h in range(2):
                    act.wait_ge(turned, 4 * b + 3 + h)
                    nc.scalar.activation(oT[:, h * GC:(h + 1) * GC], tp[h][:, :], ACT.Copy).then_inc(t_copied, 1)

        @block.vector
        def _(dve):
            dve.sem_inc(pj_dve, 1)
            dve.wait_ge(loaded, 80)
            dve.wait_ge(ones_set, 1)
            with dve.Fori(0, B) as b:
                for t in range(BT):
                    tt = b * BT + t
                    nc.vector.tensor_scalar(xn[:, t, :], X[:, tt, :], rstd[:, ds(tt, 1)], shift[:, ds(tt, 1)],
                                            ALU.mult, ALU.add).then_inc(normed, 1)
                for n in range(4):
                    dve.wait_ge(pj_ready, 8 * b + n + 1)
                    nc.vector.tensor_copy(vv[:, 2 * n:2 * n + 2, 0:C],
                                          pj[n % 2][:, :].rearrange("p (k s c) -> p k s c", k=2, s=2)[:, :, 1, :])\
                        .then_inc(pj_dve, 1)
                dve.wait_ge(kv_ready, b + 1)
                nc.vector.tensor_tensor(kv[:, 0:C], kvp[:, 0:C], headmask[:, :], ALU.mult).then_inc(kstep, 1)
                nc.vector.tensor_copy(ksum[:, :], kvp[:, C:C + 1]).then_inc(kstep, 1)
                dve.wait_ge(kstep, 3 * b + 2)
                nc.vector.tensor_scalar(kv[:, C:], headmask[:, ::DB], ksum[:, 0:1], None, ALU.mult).then_inc(kstep, 1)
                for n in range(4):
                    dve.wait_ge(op_ready, 4 * b + n + 1)
                    zz = z[:, 2 * n:2 * n + 2, :]
                    nc.vector.tensor_scalar(zz, op[n % 2][:, :, C:W], EPS_Z, None, ALU.add).then_inc(zstep, 1)
                    dve.wait_ge(zstep, 8 * b + 2 * n + 1)
                    nc.vector.reciprocal(zz, zz).then_inc(zstep, 1)
                    dve.wait_ge(zstep, 8 * b + 2 * n + 2)
                    for k in range(2):
                        last = nc.vector.tensor_tensor(
                            o[:, 2 * n + k, :].rearrange("p (h d) -> p h d", h=HB),
                            op[n % 2][:, k, 0:C].rearrange("p (h d) -> p h d", h=HB),
                            z[:, 2 * n + k, :].unsqueeze(2).to_broadcast([P, HB, DB]), ALU.mult)
                    last.then_inc(o_ready, 1)
                dve.wait_ge(biased, b + 1)
                for h in range(2):
                    dve.wait_ge(pj_ready, 8 * b + 7 + h)
                    xs = X[:, ds(b * BT + h * GT, GT), :]
                    nc.vector.tensor_tensor(xs, pj[h][:, :].rearrange("p (t c) -> p t c", t=GT), xs, ALU.add)\
                        .then_inc(pj_dve, 1)


def kernel(**inputs):
    import numpy as np
    import concourse.bacc as bacc
    from concourse.bass_utils import run_bass_kernel_spmd as run

    g = {k.replace("L0_", ""): np.asarray(v) for k, v in inputs.items()}
    nc = bacc.Bacc("TRN2", target_bir_lowering=False, num_devices=1)
    arrays = {}

    def give(name, a):
        a = np.ascontiguousarray(a, dtype=np.float32)
        arrays[name + "_in"] = a
        return nc.dram_tensor(name + "_in", a.shape, F32, kind="ExternalInput").ap()

    r64 = np.arange(P) % HD
    NEG = -1.0e30
    causal = np.concatenate([np.where(np.arange(P)[None, :] > r64[:, None], NEG, 0.0),
                             np.where(np.arange(HD)[None, :] > r64[:, None], NEG, 0.0)], axis=1)
    causal_sel = np.stack([np.arange(P)[None, :] == r64[:, None], np.arange(P)[None, :] == HD + r64[:, None]], axis=1)
    wqk = np.stack([g["attn_a_w_q"].reshape(C, PAIRS, P).transpose(1, 0, 2),
                    g["attn_a_w_k"].reshape(C, PAIRS, P).transpose(1, 0, 2)], axis=2)
    half, tok = np.arange(P) // HD, np.arange(P)
    offs = (half[:, None] * ZR + np.zeros((1, HE))).astype(np.float32)
    wqkvB = g["attn_b_w_qkv"]
    w1 = g["ffn_w1"].reshape(2, HE, C, F).transpose(1, 2, 0, 3).reshape(HE, C, 2 * F)
    w2 = g["ffn_w2"].reshape(2, HE, F, C).transpose(1, 0, 2, 3).reshape(HE, 2 * F, C)
    args = [
        give("x", g["attn_a_x"].reshape(T, C)),
        give("ident", np.eye(P)), give("causal", causal), give("causal_sel", causal_sel),
        give("wqk", wqk), give("wv", g["attn_a_w_v"].reshape(C, PAIRS, P).transpose(1, 0, 2)),
        give("wu", g["attn_a_w_u"].reshape(PAIRS, P, C)), give("bu", np.broadcast_to(g["attn_a_b_u"], (P, C))),
        give("wqB", wqkvB[:C].T), give("wkvB", wqkvB[C:].T), give("wpB", g["attn_b_w_proj"].T),
        give("bpB", np.broadcast_to(g["attn_b_b_proj"], (P, C))),
        give("headmask", np.kron(np.eye(HB), np.ones((DB, DB)))),
        give("rw", g["ffn_router_weight"].T), give("eb", np.broadcast_to(g["ffn_expert_bias"], (P, E))),
        give("w1", w1), give("w2", w2),
        give("sw1", g["ffn_sw1"].T), give("sw2", g["ffn_sw2"].T),
        give("keyrow", np.broadcast_to(T - np.arange(T), (HD, T))),
        give("offs", np.concatenate([offs, tok[:, None]], axis=1)),
    ]
    out = nc.dram_tensor("out", (T, C), F32, kind="ExternalOutput").ap()
    table = nc.dram_tensor("table", (T, TW), F32).ap()
    zbuf = [nc.dram_tensor(f"zbuf{n}", (2 * ZR, C), F32).ap() for n in range(2)]
    build(nc, *args, out, table, zbuf, STOP)
    r = run(nc, [arrays], core_ids=[0])
    return r.results[0]["out"].reshape(B, N, C)


STOP = None
```

```python
import concourse.bass as bass
from concourse import mybir
from contextlib import ExitStack

F32 = mybir.dt.float32
F32R = mybir.dt.float32r
BF16 = mybir.dt.bfloat16
I32 = mybir.dt.int32
ALU = mybir.AluOpType
ACT = mybir.ActivationFunctionType
AX = mybir.AxisListType
ds = bass.ds

P = 128
B, N, C = 4, 1024, 128
T = B * N
NT = T // P
BT = N // P
GT = 4
NG = NT // GT
GC = GT * P
EPS_LN = 1e-5

HEADS, HD = 16, 64
PAIRS = HEADS // 2
NP = B * PAIRS
SCALE_QK = 1.0 / HD

HB, DB = 16, 8
EPS_Z = 1.1920928955078125e-07

E, K, F = 64, 6, 64
CAP = 2 * ((256 * K + E - 1) // E)
HE = E // 2
SF = 256
ZR = T + P
TW = C + E
ZPARTS = 8
EMPTY = -3.0e38


def blocks_of(i):
    return [(k, min(k + GT, i + 1)) for k in range(0, i + 1, GT)]


def evacs(i):
    return sum(len(blocks_of(k)) for k in range(i))


EV_PAIR = evacs(BT)


def build(nc, x, ident_in, causal_in, wqk_in, wv_in, wu_in, bu_in,
          wqB_in, wkvB_in, wpB_in, bpB_in, headmask_in, rw_in, eb_in, w1_in, w2_in, sw1_in, sw2_in,
          keyrow_in, offs_in, out, table, zbuf):
    ctx = ExitStack()
    with ctx:
        def sb(name, shape, dt=F32):
            return ctx.enter_context(nc.sbuf_tensor(name, shape, dt))

        X = sb("X", [P, NT, C])
        XT = sb("XT", [P, T])
        ident = sb("ident", [P, P])
        mean_var = sb("mean_var", [P, NT, 2])
        rstd = sb("rstd", [P, NT])
        shift = sb("shift", [P, NT])

        attention_a(nc, x, X, XT, mean_var, rstd, shift, ident, ident_in, causal_in, wqk_in, wv_in, wu_in, bu_in, zbuf)
        experts(nc, X, XT, mean_var, rstd, shift, ident, rw_in, eb_in, w1_in, w2_in, sw1_in, sw2_in,
                keyrow_in, offs_in, table, zbuf, 0, out)
        attention_b(nc, X, rstd, shift, ident, wqB_in, wkvB_in, wpB_in, bpB_in, headmask_in)
        experts(nc, X, XT, mean_var, rstd, shift, ident, rw_in, eb_in, w1_in, w2_in, sw1_in, sw2_in,
                keyrow_in, offs_in, table, zbuf, 1, out)


def layernorm(nc, X, mean_var, rstd, shift, tag, prepare=None, meanwhile=None):
    ctx = ExitStack()
    with ctx:
        stats = ctx.enter_context(nc.sbuf_tensor(f"stats_{tag}", [P, 2, BT, 6], F32))
        stat_step = ctx.enter_context(nc.semaphore(f"stat_step_{tag}"))
        fin_step = ctx.enter_context(nc.semaphore(f"fin_step_{tag}"))
        std_done = ctx.enter_context(nc.semaphore(f"std_done_{tag}"))
        block = ctx.enter_context(nc.Block())
        if meanwhile:
            meanwhile(block)

        @block.vector
        def _(dve):
            n = 0
            for g in range(B):
                if prepare:
                    prepare(dve, g)
                for k in range(BT):
                    nc.vector.bn_stats(stats[:, g % 2, k, :], X[:, g * BT + k, :]).then_inc(stat_step, 1)
                n += BT
                dve.wait_ge(stat_step, n)
                for k in range(BT):
                    nc.vector.bn_aggr(mean_var[:, g * BT + k, :], stats[:, g % 2, k, :]).then_inc(stat_step, 1)
                n += BT
            dve.wait_ge(stat_step, n)
            nc.vector.tensor_scalar(rstd[:, :], mean_var[:, :, 1], EPS_LN, None, ALU.add).then_inc(fin_step, 1)
            dve.wait_ge(std_done, 1)
            nc.vector.reciprocal(rstd[:, :], rstd[:, :]).then_inc(fin_step, 1)
            dve.wait_ge(fin_step, 2)
            nc.vector.scalar_tensor_tensor(out=shift[:, :], in0=mean_var[:, :, 0], scalar=-1.0, in1=rstd[:, :],
                                           op0=ALU.mult, op1=ALU.mult).then_inc(fin_step, 1)

        @block.scalar
        def _(act):
            act.wait_ge(fin_step, 1)
            nc.scalar.activation(rstd[:, :], rstd[:, :], ACT.Sqrt).then_inc(std_done, 1)


def transpose_x(nc, X, XT, xb, rstd, shift, ident, ident_loaded, banks):
    ctx = ExitStack()
    with ctx:
        R = len(banks)
        xn = ctx.enter_context(nc.sbuf_tensor("xn_a", [P, R, GT, C], F32))
        normed = ctx.enter_context(nc.semaphore("normed_a"))
        turned = ctx.enter_context(nc.semaphore("turned_a"))
        copied = ctx.enter_context(nc.semaphore("copied_a"))
        doubled = ctx.enter_context(nc.semaphore("doubled_a"))
        block = ctx.enter_context(nc.Block())

        @block.vector
        def _(dve):
            for g in range(NG):
                if g >= R:
                    dve.wait_ge(turned, g - R + 1)
                for k in range(GT):
                    t = g * GT + k
                    nc.vector.tensor_scalar(xn[:, g % R, k, :], X[:, t, :], rstd[:, t:t + 1], shift[:, t:t + 1],
                                            ALU.mult, ALU.add).then_inc(normed, 1)

        @block.tensor
        def _(pe):
            pe.wait_ge(ident_loaded, 16)
            for g in range(NG):
                pe.wait_ge(normed, (g + 1) * GT)
                if g >= R:
                    pe.wait_ge(copied, g - R + 1)
                for k in range(GT):
                    last = nc.tensor.transpose(banks[g % R][:, k * P:(k + 1) * P], xn[:, g % R, k, :], ident[:, :])
                last.then_inc(turned, 1)

        @block.scalar
        def _(act):
            for g in range(NG):
                act.wait_ge(turned, g + 1)
                nc.scalar.activation(XT[:, g * GC:(g + 1) * GC], banks[g % R][:, :], ACT.Copy).then_inc(copied, 1)
                if g < N // GC:
                    act.wait_ge(copied, g + 1)
                    nc.scalar.activation(xb[:, 0, g * GC:(g + 1) * GC], XT[:, g * GC:(g + 1) * GC], ACT.Copy)\
                        .then_inc(doubled, 1)

        @block.gpsimd
        def _(pool):
            pool.wait_ge(copied, N // GC)
            pool.nop(nofuse=True)
            nc.gpsimd.tensor_copy(xb[:, 1, :], XT[:, 0:N])


def attention_a(nc, x, X, XT, mean_var, rstd, shift, ident, ident_in, causal_in, wqk_in, wv_in, wu_in, bu_in, zbuf):
    ctx = ExitStack()
    with ctx:
        def sb(name, shape, dt=F32):
            return ctx.enter_context(nc.sbuf_tensor(name, shape, dt))

        def pb(name, shape, dt=F32):
            return ctx.enter_context(nc.psum_tensor(name, shape, dt))

        def sem(name):
            return ctx.enter_context(nc.semaphore(name))

        causal_f = sb("causal_f", [P, P])
        causal = sb("causal", [P, P], BF16)
        ident_bf = sb("ident_bf", [P, P], BF16)
        wv = sb("wv", [P, PAIRS, P])
        wu = sb("wu", [P, 2, P])
        bu = sb("bu", [P, 1])
        wqk = sb("wqk", [P, 2, 2, P])
        xb = sb("xb", [P, 2, N])
        QT = sb("QT", [P, N])
        KT = sb("KT", [P, N])
        Q2 = sb("Q2", [P, 2, 2, N], F32R)
        KH = sb("KH", [P, 2, 2, N], F32R)
        KL = sb("KL", [P, 2, 2, N], F32R)
        V = sb("V", [P, 2, BT, P])
        probs = sb("probs", [P, 2, 2, N])
        PT = sb("PT", [P, 2, 2, N])
        OT = sb("OT", [P, N])
        YT = sb("YT", [P, T])
        zero_tile = sb("zero_tile", [P, 2 * ZR * C // P // ZPARTS])
        negmax = sb("negmax", [P, 2, 2])
        rowsum = sb("rowsum", [P, 2, BT, 2])
        rinv = sb("rinv", [P, BT, 2])
        rinv_wide = sb("rinv_wide", [P, BT, 2, HD])
        exp_warm = sb("exp_warm", [P, 1])

        S = [pb(f"S{h}", [P, N]) for h in range(2)]
        TP = [pb(f"TP{u}", [P, GC]) for u in range(2)]
        O = pb("O", [P, GC])
        G = pb("G", [P, GC])

        x_loaded = [sem(f"x_loaded{b}") for b in range(B)]
        bu_loaded = sem("bu_loaded")
        ident_loaded = sem("ident_loaded")
        cst_loaded = sem("cst_loaded")
        cst_cast = sem("cst_cast")
        z_cleared = sem("z_cleared")
        bias_set = sem("bias_set")
        pair_loaded = [sem(f"pair_loaded{u}") for u in range(2)]
        scores_ready = sem("scores_ready")
        max_ready = sem("max_ready")
        exp_ready = sem("exp_ready")
        rinv_ready = sem("rinv_ready")
        run_turned = sem("run_turned")
        pt_dve = sem("pt_dve")
        pt_act = sem("pt_act")
        summed = sem("summed")
        o_copied = sem("o_copied")
        widened = sem("widened")
        rinv_turned = sem("rinv_turned")
        ot_scaled = sem("ot_scaled")
        wu_loaded = [sem(f"wu_loaded{u}") for u in range(2)]
        yt_turned = sem("yt_turned")
        x_added = sem("x_added")
        proj_ready = sem("proj_ready")
        g_act = sem("g_act")
        g_dve = sem("g_dve")
        part_act = sem("part_act")
        part_dve = sem("part_dve")
        q_split = sem("q_split")
        k_split = sem("k_split")

        FILLS = [("q", 0, "act"), ("q", 1, "act"), ("k", 0, "dve"), ("k", 1, "act"),
                 ("y", 0, "dve"), ("y", 1, "dve"), ("v", 0, "act"), ("v", 1, "act")]
        FIRST = [f for f in FILLS if f[0] != "y"]
        A_PAIR = sum(f[2] == "act" for f in FILLS)
        D_PAIR = sum(f[2] == "dve" for f in FILLS)
        A_FIRST = sum(f[2] == "act" for f in FIRST)
        D_FIRST = sum(f[2] == "dve" for f in FIRST)

        HI, LO = slice(0, HD), slice(HD, P)
        OWN, OTHER = (HI, LO), (LO, HI)

        def round_part(eng_copy, n, par, h):
            if n == 0:
                return eng_copy(Q2[OWN[h], par, h, :], QT[OWN[h], :])
            return eng_copy(KH[(OWN if n == 1 else OTHER)[h], par, h, :], KT[OWN[h], :])

        def g_before(fills, n, eng):
            return sum(f[2] == eng for f in fills[:n])

        def copied(fills, kind, who):
            return g_before(fills, max(n + 1 for n in range(len(fills)) if fills[n][0] == kind), who)

        PART_ACT = [2, 4, 6]
        PART_DVE = [3, 4, 5]

        def ev_count(i):
            last = len(blocks_of(BT - 1))
            if i == -2:
                return 0
            return last + evacs(i + 1)

        ONE = 1
        EXP0 = 2

        def load_all(block):
            @block.sync
            def _(sp):
                for b in range(B):
                    ts = slice(b * BT, (b + 1) * BT)
                    sp.dma_start(X[:, ts, :], x.rearrange("(t p) c -> p t c", p=P)[:, ts, :]).then_inc(x_loaded[b], 16)
                sp.dma_start(bu[:, :], bu_in).then_inc(bu_loaded, 16)
                sp.dma_start(ident[:, :], ident_in).then_inc(ident_loaded, 16)
                sp.dma_start(causal_f[:, :], causal_in).then_inc(cst_loaded, 16)
                sp.dma_start(wv[:, :, :], wv_in.rearrange("n p c -> p n c")).then_inc(cst_loaded, 16)
                sp.dma_start(wu[:, 1, :], wu_in[0]).then_inc(wu_loaded[1], 16)
                for u in range(2):
                    for q in range(2):
                        sp.dma_start(wqk[:, u, q, :], wqk_in[u][:, q, :]).then_inc(pair_loaded[u], 16)

            @block.gpsimd
            def _(pool):
                nc.gpsimd.memset(probs[:, :, 1, :], 0.0)
                nc.gpsimd.memset(V[:, 1, :, :], 0.0)
                nc.gpsimd.memset(OT[:, :], 0.0)
                nc.gpsimd.memset(zero_tile[:, :], 0.0)
                nc.gpsimd.memset(PT[:, :, 0, :], 0.0)
                nc.gpsimd.memset(rowsum[:, 1, :, :], 1.0)

        def await_x(dve, b):
            dve.wait_ge(x_loaded[b], 16)

        layernorm(nc, X, mean_var, rstd, shift, "a", await_x, load_all)
        transpose_x(nc, X, XT, xb, rstd, shift, ident, ident_loaded,
                    [S[h][:, k * GC:(k + 1) * GC] for h in range(2) for k in range(2)])
        block = ctx.enter_context(nc.Block())

        @block.sync
        def _(sp):
            for zb in zbuf:
                rows = zb.rearrange("(p r) c -> p (r c)", p=P)
                w = rows.shape[1] // ZPARTS
                for n in range(ZPARTS):
                    sp.dma_start(rows[:, n * w:(n + 1) * w], zero_tile[:, :]).then_inc(z_cleared, 16)
            with sp.Fori(0, NP // 2) as j:
                for u in range(2):
                    nxt = 2 * ((j + 1) % 4) + u
                    batch = ((j + 1) // 4) % 4
                    sp.wait_ge(proj_ready, len(FIRST) + (2 * j + u) * BT)
                    sp.dma_start(wqk[:, u, :, :], wqk_in[ds(nxt, 1)].rearrange("a p q c -> (a p) q c"))\
                        .then_inc(pair_loaded[u], 16)
                    sp.dma_start(xb[:, u, :], XT[:, ds(batch * N, N)]).then_inc(pair_loaded[u], 16)
                    sp.dma_start(wu[:, u, :], wu_in[ds(2 * (j % 4) + u, 1)].rearrange("a p c -> (a p) c"))\
                        .then_inc(wu_loaded[u], 16)
            sp.wait_ge(z_cleared, 16 * 2 * ZPARTS)
            sp.wait_ge(cst_loaded, 32)
            sp.wait_ge(pair_loaded[0], 32 * (NP // 2 + 1))
            sp.wait_ge(pair_loaded[1], 32 * (NP // 2 + 1))
            sp.wait_ge(wu_loaded[0], 16 * (NP // 2))
            sp.wait_ge(wu_loaded[1], 16 * (NP // 2 + 1))

        def pair_fill(kind, half, par, n):
            cols = slice(half * GC, (half + 1) * GC)
            if kind in "qk":
                last = nc.tensor.matmul(G[:, :], wqk[:, par, "qk".index(kind), :], xb[:, par, cols],
                                        start=True, stop=True)
            elif kind == "y":
                last = nc.tensor.matmul(G[:, :], wu[:, par, :], OT[:, cols], start=True, stop=True)
            else:
                for k in range(GT):
                    t = half * GT + k
                    last = nc.tensor.matmul(G[:, k * P:(k + 1) * P], xb[:, par, t * P:(t + 1) * P], wv[:, n, :],
                                            start=True, stop=True)
            last.then_inc(proj_ready, 1)

        @block.tensor
        def _(pe):
            pe.sem_inc(run_turned, ONE)
            pe.sem_inc(summed, ONE)
            pe.wait_ge(pair_loaded[0], 32)
            pe.wait_ge(cst_loaded, 32)
            for n, (kind, half, _) in enumerate(FIRST):
                pe.wait_ge(g_act, g_before(FIRST, n, "act"))
                pe.wait_ge(g_dve, g_before(FIRST, n, "dve"))
                pair_fill(kind, half, 0, 0)
            pe.wait_ge(cst_cast, 2)
            nc.tensor.matmul(O[:, :], OT[:, 0:P], OT[:, 0:GC], start=True, stop=True)
            def scores(j, u, i, h):
                s = 2 * BT * j + BT * u + i
                if i == 0:
                    pe.wait_ge(part_dve if h else part_act, (2 * j + u + 1) * 3)
                    pe.wait_ge(q_split, (2 * j + u) * 2 + h + 1)
                    pe.wait_ge(k_split, (2 * j + u) * 4 + 2 * h + 2)
                if i == GT and h == 0:
                    pe.wait_ge(ot_scaled, 2 * (2 * j + u) + 2)
                pe.wait_ge(exp_ready, EXP0 + 2 * s - 1 + h)
                for a, b in blocks_of(i):
                    for part in (KH, KL):
                        nc.tensor.matmul(S[h][:, a * P:b * P], Q2[:, u, h, i * P:(i + 1) * P],
                                         part[:, u, h, a * P:b * P], start=part is KH,
                                         stop=part is KL and b != i + 1)
                nc.tensor.matmul(S[h][:, i * P:(i + 1) * P], ident_bf[:, :], causal[:, :],
                                 start=False, stop=True).then_inc(scores_ready, 1)

            def turn(j, u, i, h):
                pi = (i - 1) % BT
                m = len(blocks_of(pi))
                s = 2 * BT * j + BT * u + i
                before = (2 * j + u) * EV_PAIR + ev_count(i - 2)
                pe.wait_ge(exp_ready, EXP0 + 2 * s - 1 + h)
                for r, (a, b) in enumerate(blocks_of(pi)):
                    n = h * m + r
                    done = [(hh, rr) for hh in range(2) for rr in range(m)][:max(n - 1, 0)]
                    pe.wait_ge(pt_dve, ONE + before + sum(hh == 0 for hh, _ in done))
                    pe.wait_ge(pt_act, ONE + before + sum(hh == 1 for hh, _ in done))
                    for k in range(a, b):
                        last = nc.tensor.transpose(TP[n % 2][:, (k - a) * P:(k - a + 1) * P],
                                                   probs[:, h, pi % 2, k * P:(k + 1) * P], ident[:, :])
                    last.then_inc(run_turned, 1)

            def sum_values(j, u, i):
                pi, pu = (i - 2) % BT, (u if i >= 2 else 1 - u)
                pe.wait_ge(pt_dve, ONE + (2 * j + u) * EV_PAIR + ev_count(i - 2))
                pe.wait_ge(pt_act, ONE + (2 * j + u) * EV_PAIR + ev_count(i - 2))
                if pi % GT == 0:
                    pe.wait_ge(o_copied, 2 * (2 * j + u) + 1 + pi // GT)
                for k in range(pi + 1):
                    for h in range(2):
                        last = nc.tensor.matmul(O[OWN[h], (pi % GT) * P:(pi % GT + 1) * P],
                                                V[:, pu, k, h * HD:(h + 1) * HD], PT[:, h, pi % 2, k * P:(k + 1) * P],
                                                start=(k == 0), stop=(k == pi))
                last.then_inc(summed, 1)

            def turn_rinv(pair, half):
                pe.wait_ge(widened, pair + 1)
                for k in range(GT):
                    last = nc.tensor.transpose(S[half][:, (GT + k) * P:(GT + k + 1) * P],
                                               rinv_wide[:, half * GT + k, :, :].rearrange("p h d -> p (h d)"), ident[:, :])
                last.then_inc(rinv_turned, 1)

            with pe.Fori(0, NP // 2) as j:
                for u in range(2):
                    for i in range(BT):
                        scores(j, u, i, 0)
                        kind, half, _ = FILLS[i]
                        if i == 0:
                            pe.wait_ge(pair_loaded[1 - u], 32 * (j + 1) if u == 0 else 32 * (j + 2))
                        pe.wait_ge(g_act, A_FIRST + (2 * j + u) * A_PAIR + g_before(FILLS, i, "act"))
                        pe.wait_ge(g_dve, D_FIRST + (2 * j + u) * D_PAIR + g_before(FILLS, i, "dve"))
                        if kind == "y":
                            pe.wait_ge(ot_scaled, 2 * (2 * j + u) + 1 + half)
                            pe.wait_ge(wu_loaded[1 - u], 16 * (j + 1))
                        n = (2 * (j % 4) + 1 if u == 0 else 2 * ((j + 1) % 4)) if kind == "v" else 0
                        pair_fill(kind, half, 1 - u, n)
                        if i == 2:
                            turn_rinv(2 * j + u, 0)
                        turn(j, u, i, 0)
                        scores(j, u, i, 1)
                        if i == 2:
                            turn_rinv(2 * j + u, 1)
                        sum_values(j, u, i)
                        turn(j, u, i, 1)
            J = NP // 2
            for h in range(2):
                turn(J, 0, 0, h)
            for i in (0, 1):
                sum_values(J, 0, i)
            for half in range(2):
                turn_rinv(NP, half)
            pe.wait_ge(wu_loaded[1], 16 * (J + 1))
            for half in range(2):
                pe.wait_ge(ot_scaled, 2 * NP + 1 + half)
                pe.wait_ge(g_act, A_FIRST + NP * A_PAIR)
                pe.wait_ge(g_dve, D_FIRST + NP * D_PAIR + half)
                pair_fill("y", half, 1, PAIRS - 1)
            for g in range(NG):
                if g >= 4:
                    pe.wait_ge(x_added, g - 3)
                pe.wait_ge(g_dve, D_FIRST + NP * D_PAIR + max(0, g - NG + 3))
                for k in range(GT):
                    bank = S[g % 2][:, (g // 2 % 2) * GC:(g // 2 % 2 + 1) * GC]
                    last = nc.tensor.transpose(bank[:, k * P:(k + 1) * P],
                                               YT[:, (g * GT + k) * P:(g * GT + k + 1) * P], ident[:, :])
                last.then_inc(yt_turned, 1)

        def empty_act(kind, half, par):
            dst = {"q": QT, "k": KT}.get(kind)
            if kind in "qk":
                nc.scalar.activation(dst[:, half * GC:(half + 1) * GC], G[:, :], ACT.Copy,
                                     scale=SCALE_QK if kind == "q" else 1.0).then_inc(g_act, 1)
            else:
                nc.scalar.activation(V[:, par, half * GT:(half + 1) * GT, :],
                                     G[:, :].rearrange("p (t c) -> p t c", t=GT), ACT.Copy).then_inc(g_act, 1)

        @block.scalar
        def _(act):
            act.sem_inc(exp_ready, EXP0)
            act.sem_inc(pt_act, ONE)
            for n, (kind, half, who) in enumerate(FIRST):
                if who == "act":
                    act.wait_ge(proj_ready, n + 1)
                    empty_act(kind, half, 0)

            def part(n, par, a_done, d_done):
                act.wait_ge(g_act, a_done)
                if n:
                    act.wait_ge(g_dve, d_done)
                round_part(lambda dst, src: nc.scalar.activation(dst, src, ACT.Copy), n, par, 0)\
                    .then_inc(part_act, 1)

            for n in range(3):
                part(n, 0, copied(FIRST, "q" if n == 0 else "k", "act"), copied(FIRST, "k", "dve"))
            nc.scalar.activation(exp_warm[:, :], ident[:, 0:1], ACT.Exp)

            def copy_runs(j, u, i):
                pi = (i - 1) % BT
                m = len(blocks_of(pi))
                before = 2 * ((2 * j + u) * EV_PAIR + ev_count(i - 2))
                for r, (a, b) in enumerate(blocks_of(pi)):
                    act.wait_ge(run_turned, ONE + before + m + r + 1)
                    if r == 0:
                        act.wait_ge(summed, ONE + 2 * BT * j + BT * u + i)
                    nc.scalar.activation(PT[:, 1, pi % 2, a * P:b * P], TP[(m + r) % 2][:, 0:(b - a) * P],
                                         ACT.Copy).then_inc(pt_act, 1)

            def copy_output(j, u, i):
                pi = (i - 2) % BT
                act.wait_ge(summed, ONE + 2 * BT * j + BT * u + i + 1)
                if i == 5:
                    act.wait_ge(proj_ready, len(FIRST) + (2 * j + u) * BT + 6)
                nc.scalar.activation(OT[:, (pi // GT) * GC:(pi // GT + 1) * GC], O[:, :], ACT.Copy)\
                    .then_inc(o_copied, 1)

            with act.Fori(0, NP // 2) as j:
                for u in range(2):
                    for i in range(BT):
                        s = 2 * BT * j + BT * u + i
                        kind, half, who = FILLS[i]
                        if i == 2 or i == 6:
                            copy_output(j, u, i - 1)
                        for h in range(2):
                            act.wait_ge(max_ready, 2 * s + h + 1)
                            act.wait_ge(run_turned, ONE + 2 * ((2 * j + u) * EV_PAIR + ev_count(i - 2)))
                            w = (i + 1) * P
                            nc.scalar.activation(probs[:, h, i % 2, 0:w], S[h][:, 0:w], ACT.Exp,
                                                 bias=negmax[:, i % 2, h:h + 1],
                                                 accum_out=rowsum[:, u, i, h:h + 1]).then_inc(exp_ready, 1)
                            if h == 0 and who == "act":
                                act.wait_ge(proj_ready, len(FIRST) + (2 * j + u) * BT + i + 1)
                                if kind == "q":
                                    act.wait_ge(q_split, (2 * j + u + 1) * 2)
                                if kind == "k":
                                    act.wait_ge(k_split, (2 * j + u + 1) * 4)
                                    act.wait_ge(part_dve, (2 * j + u + 1) * 3)
                                empty_act(kind, half, 1 - u)
                        copy_runs(j, u, i)
                        if i in PART_ACT:
                            n = PART_ACT.index(i)
                            part(n, 1 - u, A_FIRST + (2 * j + u) * A_PAIR + copied(FILLS, "q" if n == 0 else "k", "act"),
                                 D_FIRST + (2 * j + u) * D_PAIR + copied(FILLS, "k", "dve"))
            J = NP // 2
            copy_runs(J, 0, 0)
            copy_output(J, 0, 1)

        @block.vector
        def _(dve):
            dve.sem_inc(pt_dve, ONE)
            dve.wait_ge(cst_loaded, 32)
            nc.vector.tensor_copy(causal[:, :], causal_f[:, :]).then_inc(cst_cast, 1)
            nc.vector.tensor_copy(ident_bf[:, :], ident[:, :]).then_inc(cst_cast, 1)

            def empty_dve(kind, half, par, j, u):
                if kind == "y":
                    b = ((j + 15) // 4) % 4 if u == 0 else j // 4
                    ys = YT[:, ds(b * N + half * GC, GC)]
                    nc.vector.tensor_tensor(ys, G[:, :], ys, ALU.add).then_inc(g_dve, 1)
                elif kind == "k":
                    nc.vector.tensor_copy(KT[:, half * GC:(half + 1) * GC], G[:, :]).then_inc(g_dve, 1)
                else:
                    nc.vector.tensor_copy(V[:, par, half * GT:(half + 1) * GT, :],
                                          G[:, :].rearrange("p (t c) -> p t c", t=GT)).then_inc(g_dve, 1)

            for n, (kind, half, who) in enumerate(FIRST):
                if who == "dve":
                    dve.wait_ge(proj_ready, n + 1)
                    empty_dve(kind, half, 0, 0, 0)
            def part(n, par, a_done, d_done):
                dve.wait_ge(g_act, a_done)
                if n:
                    dve.wait_ge(g_dve, d_done)
                round_part(nc.vector.tensor_copy, n, par, 1).then_inc(part_dve, 1)

            for n in range(3):
                part(n, 0, copied(FIRST, "q" if n == 0 else "k", "act"), copied(FIRST, "k", "dve"))
            dve.wait_ge(bu_loaded, 16)
            nc.vector.tensor_copy(YT[:, :], bu[:, 0:1].to_broadcast([P, T])).then_inc(bias_set, 1)
            dve.wait_ge(bias_set, 1)

            def copy_runs(j, u, i):
                pi = (i - 1) % BT
                before = 2 * ((2 * j + u) * EV_PAIR + ev_count(i - 2))
                for r, (a, b) in enumerate(blocks_of(pi)):
                    dve.wait_ge(run_turned, ONE + before + r + 1)
                    if r == 0:
                        dve.wait_ge(summed, ONE + 2 * BT * j + BT * u + i)
                    nc.vector.tensor_copy(PT[:, 0, pi % 2, a * P:b * P], TP[r % 2][:, 0:(b - a) * P])\
                        .then_inc(pt_dve, 1)

            def scale_output(pair, half):
                dve.wait_ge(rinv_turned, 2 * pair + half + 1)
                dve.wait_ge(o_copied, 2 * pair + 1)
                cols = slice(half * GC, (half + 1) * GC)
                nc.vector.tensor_tensor(OT[:, cols], S[half][:, GC:], OT[:, cols], ALU.mult).then_inc(ot_scaled, 1)

            def invert_sums(par, exps):
                dve.wait_ge(exp_ready, exps)
                nc.vector.reciprocal(rinv[:, :, :], rowsum[:, par, :, :]).then_inc(rinv_ready, 1)

            with dve.Fori(0, NP // 2) as j:
                for u in range(2):
                    for i in range(BT):
                        s = 2 * BT * j + BT * u + i
                        kind, half, who = FILLS[i]
                        for h in range(2):
                            dve.wait_ge(scores_ready, 2 * s + h + 1)
                            if h == 0:
                                dve.wait_ge(exp_ready, EXP0 + 2 * s - 1)
                            nc.vector.tensor_reduce(out=negmax[:, i % 2, h:h + 1], in_=S[h][:, 0:(i + 1) * P],
                                                    op=ALU.max, axis=AX.X, negate=True).then_inc(max_ready, 1)
                            if h == 0:
                                copy_runs(j, u, i)
                            if h == 0 and who == "dve":
                                dve.wait_ge(proj_ready, len(FIRST) + (2 * j + u) * BT + i + 1)
                                if kind == "k":
                                    dve.wait_ge(k_split, (2 * j + u + 1) * 4)
                                    dve.wait_ge(part_act, (2 * j + u + 1) * 3)
                                if kind == "y":
                                    dve.wait_ge(g_dve, D_FIRST + (2 * j + u) * D_PAIR + g_before(FILLS, i, "dve"))
                                empty_dve(kind, half, 1 - u, j, u)
                        if i == 0:
                            invert_sums(1 - u, EXP0 + 2 * s)
                        if i == 2:
                            scale_output(2 * j + u, 0)
                            scale_output(2 * j + u, 1)
                        if i in PART_DVE:
                            n = PART_DVE.index(i)
                            part(n, 1 - u, A_FIRST + (2 * j + u) * A_PAIR + copied(FILLS, "q" if n == 0 else "k", "act"),
                                 D_FIRST + (2 * j + u) * D_PAIR + copied(FILLS, "k", "dve"))
            J = NP // 2
            copy_runs(J, 0, 0)
            invert_sums(1, EXP0 + 2 * BT * NP)
            for half in range(2):
                scale_output(NP, half)
            for half in range(2):
                dve.wait_ge(proj_ready, len(FIRST) + NP * BT + half + 1)
                dve.wait_ge(g_dve, D_FIRST + NP * D_PAIR + half)
                ys = YT[:, (B - 1) * N + half * GC:(B - 1) * N + (half + 1) * GC]
                nc.vector.tensor_tensor(ys, G[:, :], ys, ALU.add).then_inc(g_dve, 1)
            for g in range(NG):
                dve.wait_ge(yt_turned, g + 1)
                bank = S[g % 2][:, (g // 2 % 2) * GC:(g // 2 % 2 + 1) * GC]
                xs = X[:, g * GT:(g + 1) * GT, :]
                nc.vector.tensor_tensor(xs, bank.rearrange("p (t c) -> p t c", t=GT), xs, ALU.add).then_inc(x_added, 1)

        @block.gpsimd
        def _(pool):
            def split(par, p):
                for h in range(2):
                    pool.wait_ge(part_act if h == 0 else part_dve, 3 * p + 1)
                    pool.nop(nofuse=True)
                    nc.gpsimd.tensor_tensor(Q2[OTHER[h], par, h, :], QT[OWN[h], :], Q2[OWN[h], par, h, :].bitcast(F32),
                                            ALU.subtract).then_inc(q_split, 1)
                    pool.wait_ge(q_split, 2 * p + h + 1)
                for h in range(2):
                    pool.wait_ge(part_act if h == 0 else part_dve, 3 * p + 2)
                    for n, rows in enumerate((OWN[h], OTHER[h])):
                        pool.nop(nofuse=True)
                        nc.gpsimd.tensor_tensor(KL[rows, par, h, :], KT[OWN[h], :], KH[OWN[h], par, h, :].bitcast(F32),
                                                ALU.subtract).then_inc(k_split, 1)
                        pool.wait_ge(k_split, 4 * p + 2 * h + n + 1)

            def widen(pair):
                pool.wait_ge(rinv_ready, pair + 1)
                pool.nop(nofuse=True)
                nc.gpsimd.tensor_copy(rinv_wide[:, :, :, :], rinv[:, :, :].unsqueeze(3).to_broadcast([P, BT, 2, HD]))\
                    .then_inc(widened, 1)
                pool.wait_ge(widened, pair + 1)

            split(0, 0)
            with pool.Fori(0, NP // 2) as j:
                for u in range(2):
                    widen(2 * j + u)
                    split(1 - u, 2 * j + u + 1)
            widen(NP)


def experts(nc, X, XT, mean_var, rstd, shift, ident, rw_in, eb_in, w1_in, w2_in, sw1_in, sw2_in,
            keyrow_in, offs_in, table, zbuf, layer, out):
    tag = f"f{layer}"
    layernorm(nc, X, mean_var, rstd, shift, tag)
    ctx = ExitStack()
    with ctx:
        shared_out = ctx.enter_context(nc.sbuf_tensor(f"shared_out_{tag}", [P, NT, C], F32))
        gather_idx = ctx.enter_context(nc.sbuf_tensor(f"gather_idx_{tag}", [P, HE], I32))
        scatter_idx = ctx.enter_context(nc.sbuf_tensor(f"scatter_idx_{tag}", [P, HE], I32))
        router(nc, X, XT, rstd, shift, ident, rw_in, eb_in, sw1_in, sw2_in, keyrow_in, offs_in, table,
               gather_idx, scatter_idx, shared_out, tag)
        routed(nc, ident, w1_in, w2_in, table, zbuf[layer], gather_idx, scatter_idx, tag)
        combine(nc, X, zbuf[layer], shared_out, mean_var, rstd, shift, out if layer else None, tag)


def router(nc, X, XT, rstd, shift, ident, rw_in, eb_in, sw1_in, sw2_in, keyrow_in, offs_in, table,
           gather_idx, scatter_idx, shared_out, tag):
    ctx = ExitStack()
    with ctx:
        def sb(name, shape, dt=F32):
            return ctx.enter_context(nc.sbuf_tensor(f"{name}_{tag}", shape, dt))

        def pb(name, shape, dt=F32):
            return ctx.enter_context(nc.psum_tensor(f"{name}_{tag}", shape, dt))

        def sem(name):
            return ctx.enter_context(nc.semaphore(f"{name}_{tag}"))

        rw = sb("rw", [P, E])
        eb = sb("eb", [P, E])
        keyrow = sb("keyrow", [P, T // 2])
        offs = sb("offs", [P, HE + 1])
        sw1 = sb("sw1", [P, SF])
        sw2 = sb("sw2", [P, 2, C])
        ident_bf = sb("ident_bf", [P, P], BF16)
        xn = sb("xn", [P, 2, BT, C])
        scores = sb("scores", [P, 2, BT, E])
        biased = sb("biased", [P, BT, E])
        top8 = sb("top8", [P, BT, 8])
        marked = sb("marked", [P, BT, E])
        mask = sb("mask", [P, BT, E], BF16)
        chosen = sb("chosen", [P, BT, E])
        total = sb("total", [P, BT])
        weights = sb("weights", [P, 2, BT, E])
        keys = sb("keys", [P, T // 2])
        first = sb("first", [P, CAP])
        both = sb("both", [E, 2 * CAP])
        merged = sb("merged", [E, CAP])
        spread = sb("spread", [HE, P])
        slot_key = sb("slot_key", [P, HE])
        slot_tok = sb("slot_tok", [P, HE])
        spare = sb("spare", [P, HE])
        spare2 = sb("spare2", [P, HE])
        table_warm = sb("table_warm", [P, 2])
        hidden = sb("hidden", [P, 2, 2, GC])

        tp = [pb(f"tp{u}", [P, N]) for u in range(2)]
        lg = pb("lg", [P, GC])
        mt = pb("mt", [P, N], BF16)
        st = pb("st", [P, GC])
        so = [lg, pb("so", [P, GC])]

        loaded = sem("loaded")
        rest_loaded = sem("rest_loaded")
        normed = sem("normed")
        turned = sem("turned")
        xt_copied = sem("xt_copied")
        logits = sem("logits")
        scored = sem("scored")
        step = sem("step")
        mask_ready = sem("mask_ready")
        weights_ready = sem("weights_ready")
        mask_turned = sem("mask_turned")
        keys_ready = sem("keys_ready")
        xn_stored = [sem(f"xn_stored{u}") for u in range(2)]
        w_stored = [sem(f"w_stored{u}") for u in range(2)]
        fstep = sem("fstep")
        sh_ready = sem("sh_ready")
        sh_gelu = sem("sh_gelu")
        s_ready = sem("s_ready")
        s_copied = sem("s_copied")
        PER = 2 * BT + 6
        STEPS_LATE = 3
        block = ctx.enter_context(nc.Block())
        tab = table.rearrange("(t p) w -> p t w", p=P)

        @block.sync
        def _(sp):
            sp.dma_start(rw[:, :], rw_in).then_inc(loaded, 16)
            sp.dma_start(eb[:, :], eb_in).then_inc(loaded, 16)
            for h in range(2):
                sp.dma_start(keyrow[h * E:(h + 1) * E, :], keyrow_in[:, h * T // 2:(h + 1) * T // 2]).then_inc(rest_loaded, 16)
            sp.dma_start(offs[:, :], offs_in).then_inc(rest_loaded, 16)
            sp.dma_start(sw1[:, :], sw1_in).then_inc(rest_loaded, 16)
            sp.dma_start(sw2[:, :, :], sw2_in.rearrange("(k p) c -> p k c", p=P)).then_inc(rest_loaded, 16)
            for g in range(B):
                sp.wait_ge(normed, (g + 1) * BT)
                sp.dma_start(tab[:, g * BT:(g + 1) * BT, 0:C], xn[:, g % 2, :, :]).then_inc(xn_stored[g % 2], 16)
                sp.wait_ge(weights_ready, g + 1)
                sp.dma_start(tab[:, g * BT:(g + 1) * BT, C:], weights[:, g % 2, :, :]).then_inc(w_stored[g % 2], 16)
            for u in range(2):
                sp.wait_ge(xn_stored[u], 16 * B // 2)
                sp.wait_ge(w_stored[u], 16 * B // 2)

        @block.tensor
        def _(pe):
            pe.wait_ge(loaded, 32)
            pe.wait_ge(fstep, 1)

            def turn(g):
                pe.wait_ge(normed, (g + 1) * BT)
                if g >= 2:
                    pe.wait_ge(xt_copied, g - 1)
                for k in range(BT):
                    last = nc.tensor.transpose(tp[g % 2][:, k * P:(k + 1) * P], xn[:, g % 2, k, :], ident[:, :])
                last.then_inc(turned, 1)

            def score(g):
                pe.wait_ge(xt_copied, g + 1)
                if g:
                    pe.wait_ge(scored, g)
                for k in range(BT):
                    t = g * BT + k
                    last = nc.tensor.matmul(lg[:, k * E:(k + 1) * E], XT[:, t * P:(t + 1) * P], rw[:, :],
                                            start=True, stop=True)
                last.then_inc(logits, 1)

            turn(0)
            score(0)
            for g in range(B):
                if g + 1 < B:
                    turn(g + 1)
                    score(g + 1)
                pe.wait_ge(mask_ready, g + 1)
                if g:
                    pe.wait_ge(keys_ready, g)
                pe.nop(nofuse=True)
                r = slice(g // 2 * E, (g // 2 + 1) * E)
                for k in range(BT):
                    last = nc.tensor.transpose(mt[r, k * P:(k + 1) * P], mask[:, k, :], ident_bf[:, :])
                last.then_inc(mask_turned, 1)

            def first_product(q, u):
                for c in range(2):
                    last = nc.tensor.matmul(tp[u][:, c * GC:(c + 1) * GC], sw1[:, c * P:(c + 1) * P],
                                            XT[:, ds(q * GC, GC)], start=True, stop=True)
                last.then_inc(sh_ready, 1)

            pe.wait_ge(xt_copied, B)
            pe.wait_ge(scored, B)
            pe.wait_ge(rest_loaded, 80)
            first_product(0, 0)
            with pe.Fori(0, NG // 2) as j:
                for u in range(2):
                    q = 2 * j + u
                    pe.wait_ge(sh_gelu, q + 1)
                    first_product((q + 1) % NG, 1 - u)
                    pe.wait_ge(sh_gelu, q + 2)
                    pe.wait_ge(s_copied, q + 1)
                    for k in range(GT):
                        for c in range(2):
                            last = nc.tensor.matmul(so[u][:, k * P:(k + 1) * P], hidden[:, u, c, k * P:(k + 1) * P],
                                                    sw2[:, c, :], start=(c == 0), stop=(c == 1))
                    last.then_inc(s_ready, 1)
            pe.wait_ge(keys_ready, B + 1)
            nc.tensor.transpose(st[:, 0:HE], spread[:, :], ident[0:HE, 0:HE]).then_inc(mask_turned, 1)

        @block.scalar
        def _(act):
            act.sem_inc(sh_gelu, 1)
            act.sem_inc(s_copied, 2)

            def copy_x(g):
                act.wait_ge(turned, g + 1)
                nc.scalar.activation(XT[:, g * N:(g + 1) * N], tp[g % 2][:, :], ACT.Copy).then_inc(xt_copied, 1)

            nc.scalar.activation(table_warm[:, 0:1], ident[:, 0:1], ACT.Sigmoid)
            copy_x(0)
            for g in range(B):
                act.wait_ge(logits, g + 1)
                if g >= 2:
                    act.wait_ge(step, (g - 1) * PER - STEPS_LATE)
                nc.scalar.activation(scores[:, g % 2, :, :], lg[:, :].rearrange("p (k e) -> p k e", k=BT),
                                     ACT.Sigmoid).then_inc(scored, 1)
                if g + 1 < B:
                    copy_x(g + 1)

            def gelu(q, u):
                act.wait_ge(sh_ready, q + 1)
                nc.scalar.activation(hidden[:, u, :, :], tp[u][:, :].rearrange("p (c t) -> p c t", c=2),
                                     ACT.Gelu_apprx_tanh).then_inc(sh_gelu, 1)

            nc.scalar.activation(table_warm[:, 1:2], ident[:, 0:1], ACT.Gelu_apprx_tanh)
            gelu(0, 0)
            with act.Fori(0, NG // 2) as j:
                for u in range(2):
                    q = 2 * j + u
                    gelu(q + 1, 1 - u)
                    act.wait_ge(s_ready, q + 1)
                    nc.scalar.activation(shared_out[:, ds(q * GT, GT), :],
                                         so[u][:, :].rearrange("p (t c) -> p t c", t=GT), ACT.Copy).then_inc(s_copied, 1)

        @block.gpsimd
        def _(pool):
            def normalise(g):
                if g >= 2:
                    pool.wait_ge(turned, g - 1)
                    pool.wait_ge(xn_stored[g % 2], 16)
                for k in range(BT):
                    t = g * BT + k
                    nc.gpsimd.tensor_scalar(xn[:, g % 2, k, :], X[:, t, :], rstd[:, t:t + 1], shift[:, t:t + 1],
                                            ALU.mult, ALU.add).then_inc(normed, 1)

            normalise(0)
            normalise(1)
            for g in range(B):
                if g + 2 < B:
                    normalise(g + 2)
                pool.wait_ge(step, (g + 1) * PER)
                if g >= 2:
                    pool.wait_ge(w_stored[g % 2], 16)
                nc.gpsimd.tensor_tensor(weights[:, g % 2, :, :], chosen[:, :, :],
                                        total[:, :].unsqueeze(2).to_broadcast([P, BT, E]), ALU.mult)\
                    .then_inc(weights_ready, 1)

        @block.vector
        def _(dve):
            nc.vector.tensor_copy(ident_bf[:, :], ident[:, :]).then_inc(fstep, 1)

            dve.wait_ge(loaded, 32)
            for g in range(B):
                n = g * PER
                dve.wait_ge(scored, g + 1)
                nc.vector.tensor_tensor(biased[:, :, :], scores[:, g % 2, :, :],
                                        eb[:, :].unsqueeze(1).to_broadcast([P, BT, E]), ALU.add).then_inc(step, 1)
                dve.wait_ge(step, n + 1)
                for k in range(BT):
                    nc.vector.max(top8[:, k, :], biased[:, k, :]).then_inc(step, 1)
                dve.wait_ge(step, n + 1 + BT)
                nc.vector.memset(top8[:, :, K:], EMPTY).then_inc(step, 1)
                dve.wait_ge(step, n + 2 + BT)
                for k in range(BT):
                    nc.vector.match_replace(marked[:, k, :], top8[:, k, :], biased[:, k, :], 2 * EMPTY / 3).then_inc(step, 1)
                dve.wait_ge(step, n + 2 + 2 * BT)
                if g:
                    dve.wait_ge(mask_turned, g)
                nc.vector.tensor_tensor(mask[:, :, :], marked[:, :, :], biased[:, :, :], ALU.not_equal)\
                    .then_inc(mask_ready, 1)
                dve.wait_ge(mask_ready, g + 1)
                if g:
                    dve.wait_ge(weights_ready, g)
                nc.vector.tensor_tensor(chosen[:, :, :], mask[:, :, :], scores[:, g % 2, :, :], ALU.mult).then_inc(step, 1)
                dve.wait_ge(step, n + 3 + 2 * BT)
                nc.vector.tensor_reduce(out=total[:, :], in_=chosen[:, :, :], op=ALU.add, axis=AX.X).then_inc(step, 1)
                dve.wait_ge(step, n + 4 + 2 * BT)
                nc.vector.tensor_scalar(total[:, :], total[:, :], 1e-20, None, ALU.add).then_inc(step, 1)
                dve.wait_ge(step, n + 5 + 2 * BT)
                nc.vector.reciprocal(total[:, :], total[:, :]).then_inc(step, 1)
                dve.wait_ge(mask_turned, g + 1)
                if g == 0:
                    dve.wait_ge(rest_loaded, 80)
                r = slice(g // 2 * E, (g // 2 + 1) * E)
                cols = slice(g % 2 * N, (g % 2 + 1) * N)
                nc.vector.tensor_tensor(keys[r, cols], mt[r, :], keyrow[r, cols], ALU.mult).then_inc(keys_ready, 1)
            dve.wait_ge(keys_ready, B)
            n = 1

            def link(ins):
                nonlocal n
                ins.then_inc(fstep, 1)
                n += 1
                dve.wait_ge(fstep, n)

            for r in range(CAP // 8):
                link(nc.vector.max(first[:, r * 8:(r + 1) * 8], keys[:, :]))
                link(nc.vector.match_replace(keys[:, :], first[:, r * 8:(r + 1) * 8], keys[:, :], -1.0))
            link(nc.vector.tensor_copy(both[:, 0:CAP], first[0:E, :]))
            link(nc.vector.tensor_copy(both[:, CAP:], first[E:, :]))
            for r in range(CAP // 8):
                link(nc.vector.max(merged[:, r * 8:(r + 1) * 8], both[:, :]))
                link(nc.vector.match_replace(both[:, :], merged[:, r * 8:(r + 1) * 8], both[:, :], -1.0))
            link(nc.vector.memset(spread[:, :], 0.0))
            link(nc.vector.tensor_copy(spread[:, 0:CAP], merged[0:HE, :]))
            nc.vector.tensor_copy(spread[:, HD:HD + CAP], merged[HE:, :]).then_inc(keys_ready, 1)
            dve.wait_ge(mask_turned, B + 1)
            link(nc.vector.tensor_copy(slot_key[:, :], st[:, 0:HE]))
            link(nc.vector.tensor_scalar(slot_tok[:, :], slot_key[:, :], -1.0, float(T), ALU.mult, ALU.add))
            link(nc.vector.tensor_scalar(gather_idx[:, :], slot_tok[:, :], float(T - 1), None, ALU.min))
            link(nc.vector.tensor_scalar(spare[:, :], slot_key[:, :], 0.0, offs[:, HE:], ALU.is_equal, ALU.mult))
            link(nc.vector.tensor_tensor(spare2[:, :], spare[:, :], offs[:, 0:HE], ALU.add))
            link(nc.vector.tensor_tensor(scatter_idx[:, :], spare2[:, :], slot_tok[:, :], ALU.add))


def routed(nc, ident, w1_in, w2_in, table, zb, gather_idx, scatter_idx, tag):
    ctx = ExitStack()
    with ctx:
        def sb(name, shape, dt=F32):
            return ctx.enter_context(nc.sbuf_tensor(f"{name}_{tag}", shape, dt))

        def pb(name, shape, dt=F32):
            return ctx.enter_context(nc.psum_tensor(f"{name}_{tag}", shape, dt))

        def sem(name):
            return ctx.enter_context(nc.semaphore(f"{name}_{tag}"))

        R = 4
        w1 = sb("w1", [P, R, P])
        w2 = sb("w2", [P, R, P])
        gi = [sb(f"gi{u}", [P, 1], I32) for u in range(R)]
        si = [sb(f"si{u}", [P, 1], I32) for u in range(R)]
        rows = [sb(f"rows{u}", [P, TW]) for u in range(R)]
        xs = sb("xs", [P, 2, P])
        hid = sb("hid", [P, 2, HD])
        ys = [sb(f"ys{u}", [P, C]) for u in range(2)]
        table_warm = sb("table_warm2", [P, 1])
        tg = [pb(f"tg{u}", [P, P]) for u in range(2)]
        hq = [pb(f"hq{u}", [P, HD]) for u in range(2)]
        yq = [pb(f"yq{u}", [P, C]) for u in range(2)]

        w_loaded = [sem(f"w_loaded{u}") for u in range(R)]
        idx_ready = sem("idx_ready")
        gathered = [sem(f"gathered{u}") for u in range(R)]
        scattered = sem("scattered")
        rows_turned = sem("rows_turned")
        xs_copied = sem("xs_copied")
        h_ready = sem("hid_ready")
        gelu_ready = sem("hgelu_ready")
        y_ready = sem("y_ready")
        y_scaled = sem("y_scaled")
        block = ctx.enter_context(nc.Block())
        J = HE // R
        AHEAD = R - 1

        @block.sync
        def _(sp):
            with sp.Fori(0, J) as j:
                for u in range(R):
                    m = R * j + u
                    if u == 0:
                        sp.wait_ge(y_ready, m + 1)
                    sp.dma_start(w1[:, u, :], w1_in[ds(m, 1)].rearrange("a p c -> (a p) c")).then_inc(w_loaded[u], 16)
                    sp.dma_start(w2[:, u, :], w2_in[ds(m, 1)].rearrange("a p c -> (a p) c")).then_inc(w_loaded[u], 16)

        @block.gpsimd
        def _(pool):
            def gather(m, u, done):
                nc.gpsimd.tensor_copy(gi[u][:, :], gather_idx[:, ds(m, 1)]).then_inc(idx_ready, 1)
                pool.wait_ge(idx_ready, done)
                pool.nop(nofuse=True)
                nc.gpsimd.indirect_dma_start(out=rows[u][:, :], out_offset=None, in_=table,
                                             in_offset=bass.IndirectOffsetOnAxis(ap=gi[u][:, 0:1], axis=0))\
                    .then_inc(gathered[u], 16)

            for m in range(AHEAD):
                gather(m, m, m + 1)
            with pool.Fori(0, J) as j:
                for u in range(R):
                    m = R * j + u
                    nc.gpsimd.tensor_copy(si[u][:, :], scatter_idx[:, ds(m, 1)]).then_inc(idx_ready, 1)
                    pool.wait_ge(y_scaled, 2 * m + 1)
                    gather((m + AHEAD) % HE, (u + AHEAD) % R, 2 * m + AHEAD + 2)
                    if u:
                        pool.wait_ge(scattered, 16 * m)
                    pool.wait_ge(y_scaled, 2 * m + 3)
                    pool.nop(nofuse=True)
                    nc.gpsimd.indirect_dma_start(out=zb, out_offset=bass.IndirectOffsetOnAxis(ap=si[u][:, 0:1], axis=0),
                                                 in_=ys[u % 2][:, :], in_offset=None, compute_op=ALU.add)\
                        .then_inc(scattered, 16)
                pool.wait_ge(scattered, 16 * R * (j + 1))
            pool.wait_ge(scattered, 16 * HE)
            for u in range(AHEAD):
                pool.wait_ge(gathered[u], 16 * (J + 1))

        @block.tensor
        def _(pe):
            def turn(u, at, n):
                pe.wait_ge(gathered[u], n)
                nc.tensor.transpose(tg[at][:, :], rows[u][:, 0:C], ident[:, :]).then_inc(rows_turned, 1)

            pe.sem_inc(y_ready, 1)
            turn(0, 0, 16)
            with pe.Fori(0, J) as j:
                for u in range(R):
                    m = R * j + u
                    b = u % 2
                    turn((u + 1) % R, 1 - b, 16 * (j + 1) if u + 1 < R else 16 * (j + 2))
                    pe.wait_ge(xs_copied, m + 1)
                    pe.wait_ge(w_loaded[u], 32 * (j + 1))
                    for h in range(2):
                        last = nc.tensor.matmul(hq[b][h * HD:(h + 1) * HD, :], w1[:, u, h * HD:(h + 1) * HD],
                                                xs[:, b, h * HD:(h + 1) * HD], start=True, stop=True)
                    last.then_inc(h_ready, 1)
                    pe.wait_ge(gelu_ready, m + 1)
                    pe.nop(nofuse=True)
                    for h in range(2):
                        r = slice(h * HD, (h + 1) * HD)
                        last = nc.tensor.matmul(yq[b][r, :], hid[r, b, :], w2[r, u, :], start=True, stop=True)
                    last.then_inc(y_ready, 1)

        @block.scalar
        def _(act):
            nc.scalar.activation(table_warm[:, :], ident[:, 0:1], ACT.Gelu_apprx_tanh)
            with act.Fori(0, J) as j:
                for u in range(R):
                    m = R * j + u
                    b = u % 2
                    act.wait_ge(h_ready, m + 1)
                    nc.scalar.activation(hid[:, b, :], hq[b][:, :], ACT.Gelu_apprx_tanh).then_inc(gelu_ready, 1)

        @block.vector
        def _(dve):
            dve.sem_inc(y_scaled, 1)

            def copy_xs(m, b):
                dve.wait_ge(rows_turned, m + 1)
                nc.vector.tensor_copy(xs[:, b, :], tg[b][:, :]).then_inc(xs_copied, 1)

            copy_xs(0, 0)
            with dve.Fori(0, J) as j:
                for u in range(R):
                    m = R * j + u
                    b = u % 2
                    copy_xs(m + 1, 1 - b)
                    dve.wait_ge(y_ready, m + 2)
                    dve.wait_ge(idx_ready, 2 * m + AHEAD + 1)
                    for h in range(2):
                        r = slice(h * HD, (h + 1) * HD)
                        nc.vector.tensor_scalar(ys[b][r, :], yq[b][r, :], rows[u][r, ds(C + h * HE + m, 1)], None,
                                                ALU.mult).then_inc(y_scaled, 1)


def combine(nc, X, zb, shared_out, mean_var, rstd, shift, out, tag):
    ctx = ExitStack()
    with ctx:
        z = [ctx.enter_context(nc.sbuf_tensor(f"z{h}_{tag}", [P, NT, C], F32)) for h in range(2)]
        z_loaded = [ctx.enter_context(nc.semaphore(f"z_loaded{c}_{tag}")) for c in range(B)]
        joined = ctx.enter_context(nc.semaphore(f"joined_{tag}"))
        added = ctx.enter_context(nc.semaphore(f"added_{tag}"))
        out_done = ctx.enter_context(nc.semaphore("out_done")) if out is not None else None

        def batch(c):
            return slice(c * BT, (c + 1) * BT)

        def load_and_join(block):
            @block.sync
            def _(sp):
                for c in range(B):
                    for h in range(2):
                        src = zb[h * ZR:h * ZR + T, :].rearrange("(t p) c -> p t c", p=P)
                        sp.dma_start(z[h][:, batch(c), :], src[:, batch(c), :]).then_inc(z_loaded[c], 16)
                if out is not None:
                    for c in range(B):
                        sp.wait_ge(added, 2 * c + 2)
                        sp.dma_start(out.rearrange("(t p) c -> p t c", p=P)[:, batch(c), :], X[:, batch(c), :])\
                            .then_inc(out_done, 16)
                    sp.wait_ge(out_done, 16 * B)

            @block.gpsimd
            def _(pool):
                for c in range(B):
                    pool.wait_ge(z_loaded[c], 32)
                    nc.gpsimd.tensor_tensor(z[1][:, batch(c), :], z[1][:, batch(c), :], shared_out[:, batch(c), :],
                                            ALU.add).then_inc(joined, 1)

        def add(dve, c):
            xs = X[:, batch(c), :]
            dve.wait_ge(z_loaded[c], 32)
            nc.vector.tensor_tensor(xs, xs, z[0][:, batch(c), :], ALU.add).then_inc(added, 1)
            dve.wait_ge(joined, c + 1)
            dve.wait_ge(added, 2 * c + 1)
            nc.vector.tensor_tensor(xs, xs, z[1][:, batch(c), :], ALU.add).then_inc(added, 1)
            if out is None:
                dve.wait_ge(added, 2 * c + 2)

        if out is None:
            layernorm(nc, X, mean_var, rstd, shift, "b", add, load_and_join)
        else:
            with nc.Block() as block:
                load_and_join(block)

                @block.vector
                def _(dve):
                    for c in range(B):
                        add(dve, c)


def attention_b(nc, X, rstd, shift, ident, wq_in, wkv_in, wp_in, bp_in, headmask_in):
    ctx = ExitStack()
    with ctx:
        def sb(name, shape, dt=F32):
            return ctx.enter_context(nc.sbuf_tensor(f"{name}_b", shape, dt))

        def pb(name, shape, dt=F32):
            return ctx.enter_context(nc.psum_tensor(f"{name}_b", shape, dt))

        def sem(name):
            return ctx.enter_context(nc.semaphore(f"{name}_b"))

        W = C + HB
        wq = sb("wq", [P, C])
        wkv = sb("wkv", [P, 2 * C])
        wp = sb("wp", [P, C])
        bp = sb("bp", [P, C])
        headmask = sb("headmask", [P, C])
        xn = sb("xn", [P, 2, BT, C])
        xb = sb("xb", [P, 2, N])
        kk = sb("kk", [P, 2, BT, C])
        vv = sb("vv", [P, 2, BT, C + 1])
        qT = sb("qT", [P, 2, N])
        kv = sb("kv", [P, W])
        ksum = sb("ksum", [P, 1])
        z = sb("z", [P, BT, HB])
        o = sb("o", [P, BT, C])
        oT = sb("oT", [P, N])
        tp = pb("tp", [P, GC])
        pj = [pb(f"pj{u}", [P, GC]) for u in range(2)]
        kvp = pb("kvp", [P, GC])
        op = [pb(f"op{u}", [P, 2, 2 * C]) for u in range(2)]
        to = pb("to", [P, GC])
        yo = pb("yo", [P, GC])

        loaded = sem("loaded")
        ones_set = sem("ones_set")
        normed = sem("normed")
        turned = sem("turned")
        xb_copied = sem("xb_copied")
        pj_ready = sem("pj_ready")
        v_copied = sem("v_copied")
        pj_read = sem("pj_read")
        kv_ready = sem("kv_ready")
        kstep = sem("kstep")
        op_ready = sem("op_ready")
        zstep = sem("zstep")
        o_ready = sem("o_ready")
        o_turned = sem("o_turned")
        o_copied = sem("o_copied")
        y_ready = sem("y_ready")
        y_added = sem("y_added")
        biased = sem("biased")
        block = ctx.enter_context(nc.Block())

        @block.sync
        def _(sp):
            for dst, src in ((wq, wq_in), (wkv, wkv_in), (wp, wp_in), (bp, bp_in), (headmask, headmask_in)):
                sp.dma_start(dst[:, :], src).then_inc(loaded, 16)

        @block.gpsimd
        def _(pool):
            for u in range(2):
                nc.gpsimd.memset(vv[:, u, :, C:], 1.0).then_inc(ones_set, 1)
            pool.wait_ge(loaded, 80)
            for b in range(B):
                pool.wait_ge(normed, (b + 1) * BT)
                xs = X[:, b * BT:(b + 1) * BT, :]
                nc.gpsimd.tensor_tensor(xs, xs, bp[:, :].unsqueeze(1).to_broadcast([P, BT, C]), ALU.add)\
                    .then_inc(biased, 1)

        @block.tensor
        def _(pe):
            def project(b):
                u = b % 2
                for h in range(2):
                    pe.wait_ge(normed, b * BT + (h + 1) * GT)
                    if 2 * b + h:
                        pe.wait_ge(xb_copied, 2 * b + h)
                    for k in range(GT):
                        last = nc.tensor.transpose(tp[:, k * P:(k + 1) * P], xn[:, u, h * GT + k, :], ident[:, :])
                    last.then_inc(turned, 1)
                for n in range(6):
                    m = 6 * b + n
                    if n in (0, 2):
                        pe.wait_ge(xb_copied, 2 * b + n // 2 + 1)
                    if m >= 2:
                        pe.wait_ge(pj_read, m - 1)
                    if n < 4:
                        for k in range(2):
                            t = 2 * n + k
                            last = nc.tensor.matmul(pj[n % 2][:, k * 2 * C:(k + 1) * 2 * C],
                                                    xb[:, u, t * P:(t + 1) * P], wkv[:, :], start=True, stop=True)
                    else:
                        last = nc.tensor.matmul(pj[n % 2][:, :], wq[:, :], xb[:, u, (n - 4) * GC:(n - 3) * GC],
                                                start=True, stop=True)
                    last.then_inc(pj_ready, 1)

            def sum_kv(b):
                pe.wait_ge(pj_read, 6 * b + 4)
                if b:
                    pe.wait_ge(kstep, 3 * b)
                for t in range(BT):
                    last = nc.tensor.matmul(kvp[:, 0:C + 1], kk[:, b % 2, t, :], vv[:, b % 2, t, :],
                                            start=(t == 0), stop=(t == BT - 1))
                last.then_inc(kv_ready, 1)

            pe.wait_ge(loaded, 80)
            project(0)
            pe.wait_ge(ones_set, 2)
            sum_kv(0)
            for b in range(B):
                if b + 1 < B:
                    project(b + 1)
                pe.wait_ge(pj_read, 6 * b + 6)
                pe.wait_ge(kstep, 3 * b + 3)
                for n in range(4):
                    if 4 * b + n >= 2:
                        pe.wait_ge(o_ready, 4 * b + n - 1)
                    for k in range(2):
                        t = 2 * n + k
                        last = nc.tensor.matmul(op[n % 2][:, k, 0:W], qT[:, b % 2, t * P:(t + 1) * P], kv[:, :],
                                                start=True, stop=True)
                    last.then_inc(op_ready, 1)
                if b + 1 < B:
                    sum_kv(b + 1)
                for h in range(2):
                    pe.wait_ge(o_ready, 4 * b + 2 * h + 2)
                    if 2 * b + h:
                        pe.wait_ge(o_copied, 2 * b + h)
                    for k in range(GT):
                        last = nc.tensor.transpose(to[:, k * P:(k + 1) * P], o[:, h * GT + k, :], ident[:, :])
                    last.then_inc(o_turned, 1)
                for h in range(2):
                    pe.wait_ge(o_copied, 2 * b + h + 1)
                    if 2 * b + h:
                        pe.wait_ge(y_added, 2 * b + h)
                    for k in range(GT):
                        t = h * GT + k
                        last = nc.tensor.matmul(yo[:, k * P:(k + 1) * P], oT[:, t * P:(t + 1) * P], wp[:, :],
                                                start=True, stop=True)
                    last.then_inc(y_ready, 1)

        @block.scalar
        def _(act):
            def copy_projections(b):
                u = b % 2
                for h in range(2):
                    act.wait_ge(turned, 2 * b + h + 1)
                    nc.scalar.activation(xb[:, u, h * GC:(h + 1) * GC], tp[:, :], ACT.Copy).then_inc(xb_copied, 1)
                for n in range(4):
                    act.wait_ge(v_copied, 4 * b + n + 1)
                    nc.scalar.activation(kk[:, u, 2 * n:2 * n + 2, :],
                                         pj[n % 2][:, :].rearrange("p (k s c) -> p k s c", k=2, s=2)[:, :, 0, :],
                                         ACT.Relu).then_inc(pj_read, 1)
                for n in range(2):
                    act.wait_ge(pj_ready, 6 * b + 5 + n)
                    nc.scalar.activation(qT[:, u, n * GC:(n + 1) * GC], pj[n][:, :], ACT.Relu).then_inc(pj_read, 1)

            copy_projections(0)
            for b in range(B):
                if b + 1 < B:
                    copy_projections(b + 1)
                for h in range(2):
                    act.wait_ge(o_turned, 2 * b + h + 1)
                    nc.scalar.activation(oT[:, h * GC:(h + 1) * GC], to[:, :], ACT.Copy).then_inc(o_copied, 1)

        @block.vector
        def _(dve):
            def normalise(b):
                if b >= 2:
                    dve.wait_ge(turned, 2 * (b - 1))
                for k in range(BT):
                    t = b * BT + k
                    nc.vector.tensor_scalar(xn[:, b % 2, k, :], X[:, t, :], rstd[:, t:t + 1], shift[:, t:t + 1],
                                            ALU.mult, ALU.add).then_inc(normed, 1)

            def copy_v(b):
                for n in range(4):
                    dve.wait_ge(pj_ready, 6 * b + n + 1)
                    nc.vector.tensor_copy(vv[:, b % 2, 2 * n:2 * n + 2, 0:C],
                                          pj[n % 2][:, :].rearrange("p (k s c) -> p k s c", k=2, s=2)[:, :, 1, :])\
                        .then_inc(v_copied, 1)

            def mask_kv(b):
                dve.wait_ge(kv_ready, b + 1)
                if b:
                    dve.wait_ge(op_ready, 4 * b)
                nc.vector.tensor_tensor(kv[:, 0:C], kvp[:, 0:C], headmask[:, :], ALU.mult).then_inc(kstep, 1)
                nc.vector.tensor_copy(ksum[:, :], kvp[:, C:C + 1]).then_inc(kstep, 1)
                dve.wait_ge(kstep, 3 * b + 2)
                nc.vector.tensor_scalar(kv[:, C:], headmask[:, ::DB], ksum[:, 0:1], None, ALU.mult).then_inc(kstep, 1)

            normalise(0)
            dve.wait_ge(loaded, 80)
            dve.wait_ge(ones_set, 2)
            normalise(1)
            copy_v(0)
            mask_kv(0)
            for b in range(B):
                if b + 2 < B:
                    normalise(b + 2)
                if b + 1 < B:
                    copy_v(b + 1)
                for n in range(4):
                    dve.wait_ge(op_ready, 4 * b + n + 1)
                    zz = z[:, 2 * n:2 * n + 2, :]
                    nc.vector.tensor_scalar(zz, op[n % 2][:, :, C:W], EPS_Z, None, ALU.add).then_inc(zstep, 1)
                    dve.wait_ge(zstep, 8 * b + 2 * n + 1)
                    nc.vector.reciprocal(zz, zz).then_inc(zstep, 1)
                    dve.wait_ge(zstep, 8 * b + 2 * n + 2)
                    if b and n == 0:
                        dve.wait_ge(o_turned, 2 * b)
                    for k in range(2):
                        last = nc.vector.tensor_tensor(
                            o[:, 2 * n + k, :].rearrange("p (h d) -> p h d", h=HB),
                            op[n % 2][:, k, 0:C].rearrange("p (h d) -> p h d", h=HB),
                            z[:, 2 * n + k, :].unsqueeze(2).to_broadcast([P, HB, DB]), ALU.mult)
                    last.then_inc(o_ready, 1)
                if b + 1 < B:
                    mask_kv(b + 1)
                dve.wait_ge(biased, b + 1)
                for h in range(2):
                    dve.wait_ge(y_ready, 2 * b + h + 1)
                    xs = X[:, b * BT + h * GT:b * BT + (h + 1) * GT, :]
                    nc.vector.tensor_tensor(xs, yo[:, :].rearrange("p (t c) -> p t c", t=GT), xs, ALU.add)\
                        .then_inc(y_added, 1)


def kernel(**inputs):
    import numpy as np
    import concourse.bacc as bacc
    from concourse.bass_utils import run_bass_kernel_spmd as run

    g = {k.replace("L0_", ""): np.asarray(v) for k, v in inputs.items()}
    nc = bacc.Bacc("TRN2", target_bir_lowering=False, num_devices=1)
    arrays = {}

    def give(name, a):
        a = np.ascontiguousarray(a, dtype=np.float32)
        arrays[name + "_in"] = a
        return nc.dram_tensor(name + "_in", a.shape, F32, kind="ExternalInput").ap()

    causal = np.triu(np.full((P, P), -1.0e30), 1)
    wqk = np.stack([g["attn_a_w_q"].reshape(C, PAIRS, P).transpose(1, 0, 2),
                    g["attn_a_w_k"].reshape(C, PAIRS, P).transpose(1, 0, 2)], axis=2)
    half, tok = np.arange(P) // HD, np.arange(P)
    offs = (half[:, None] * ZR + np.zeros((1, HE))).astype(np.float32)
    wqkvB = g["attn_b_w_qkv"]
    w1 = g["ffn_w1"].reshape(2, HE, C, F).transpose(1, 2, 0, 3).reshape(HE, C, 2 * F)
    w2 = g["ffn_w2"].reshape(2, HE, F, C).transpose(1, 0, 2, 3).reshape(HE, 2 * F, C)
    args = [
        give("x", g["attn_a_x"].reshape(T, C)),
        give("ident", np.eye(P)), give("causal", causal),
        give("wqk", wqk), give("wv", g["attn_a_w_v"].reshape(C, PAIRS, P).transpose(1, 0, 2)),
        give("wu", g["attn_a_w_u"].reshape(PAIRS, P, C)), give("bu", g["attn_a_b_u"][:, None]),
        give("wqB", wqkvB[:C].T), give("wkvB", wqkvB[C:].T), give("wpB", g["attn_b_w_proj"].T),
        give("bpB", np.broadcast_to(g["attn_b_b_proj"], (P, C))),
        give("headmask", np.kron(np.eye(HB), np.ones((DB, DB)))),
        give("rw", g["ffn_router_weight"].T), give("eb", np.broadcast_to(g["ffn_expert_bias"], (P, E))),
        give("w1", w1), give("w2", w2),
        give("sw1", g["ffn_sw1"].T), give("sw2", g["ffn_sw2"].T),
        give("keyrow", np.broadcast_to(T - np.arange(T), (HD, T))),
        give("offs", np.concatenate([offs, tok[:, None]], axis=1)),
    ]
    out = nc.dram_tensor("out", (T, C), F32, kind="ExternalOutput").ap()
    table = nc.dram_tensor("table", (T, TW), F32).ap()
    zbuf = [nc.dram_tensor(f"zbuf{n}", (2 * ZR, C), F32).ap() for n in range(2)]
    build(nc, *args, out, table, zbuf)
    r = run(nc, [arrays], core_ids=[0])
    return r.results[0]["out"].reshape(B, N, C)
```
